# Optimizing a Trainium2 kernel written in Bass

```python
import numpy as np
import jax
import jax.numpy as jnp

def _softmax(x, axis=-1):
    return jax.nn.softmax(x, axis=axis)

def _gelu(x):
    return jax.nn.gelu(x, approximate=True)

def _silu(x):
    return jax.nn.silu(x)

def _sigmoid(x):
    return jax.nn.sigmoid(x)

def _layernorm(x, axis=-1, eps=1e-05):
    m = jnp.mean(x, axis=axis, keepdims=True)
    v = jnp.var(x, axis=axis, keepdims=True)
    return (x - m) / jnp.sqrt(v + eps)

def _scatter_add(tgt, idx, src, axis=0):
    return tgt.at[idx].add(src)

def _segment_sum(src, seg, n):
    return jax.ops.segment_sum(src, seg, n)
kernel_name = 'mk_seq_postln_d2_jaxref_r8_f73302'

def setup_inputs(seed: int=0):
    np.random.seed(seed)
    _w = jnp.asarray

    def _L0_attn_setup():
        import jax, jax.numpy as jnp
        import numpy as np
        NUM_HEADS = 16

        def rotate_half(x):
            h = x.shape[-1] // 2
            return jnp.concatenate([-x[..., h:], x[..., :h]], axis=-1)
        key = jax.random.key(seed)
        ks = jax.random.split(key, 9)
        d = 128
        s = 0.02
        return {'x': jax.random.normal(ks[0], (4, 256, d), dtype=jnp.float32), 'wq': jax.random.normal(ks[1], (d, d), dtype=jnp.float32) * s, 'bq': jax.random.normal(ks[2], (d,), dtype=jnp.float32) * s, 'wk': jax.random.normal(ks[3], (d, d), dtype=jnp.float32) * s, 'bk': jax.random.normal(ks[4], (d,), dtype=jnp.float32) * s, 'wv': jax.random.normal(ks[5], (d, d), dtype=jnp.float32) * s, 'bv': jax.random.normal(ks[6], (d,), dtype=jnp.float32) * s, 'wo': jax.random.normal(ks[7], (d, d), dtype=jnp.float32) * s, 'bo': jax.random.normal(ks[8], (d,), dtype=jnp.float32) * s}
    _L0_attn_in = _L0_attn_setup()

    def _L0_ffn_setup():
        import jax, jax.numpy as jnp
        import numpy as np
        HIDDEN = 128
        INTER = 512
        key = jax.random.key(seed)
        k1, k2, k3, k4, k5 = jax.random.split(key, 5)
        hidden_states = jax.random.normal(k1, (4, 256, HIDDEN), dtype=jnp.float32)
        W1 = jax.random.normal(k2, (HIDDEN, INTER), dtype=jnp.float32) * (1.0 / np.sqrt(HIDDEN))
        b1 = jax.random.normal(k3, (INTER,), dtype=jnp.float32) * 0.02
        W2 = jax.random.normal(k4, (INTER, HIDDEN), dtype=jnp.float32) * (1.0 / np.sqrt(INTER))
        b2 = jax.random.normal(k5, (HIDDEN,), dtype=jnp.float32) * 0.02
        return {'hidden_states': hidden_states, 'W1': W1, 'b1': b1, 'W2': W2, 'b2': b2}
    _L0_ffn_in = _L0_ffn_setup()

    def _L1_attn_setup():
        import jax, jax.numpy as jnp
        import numpy as np
        H = 8
        ROPE_DIM = 64
        GAMMA = 0.96875
        GROUPS = 16
        EPS = 1e-05

        def _rope(x, offset=0):
            T = x.shape[-2]
            inv_freq = 1.0 / 10000.0 ** (np.arange(0, ROPE_DIM, 2, dtype=np.float32) / ROPE_DIM)
            t = jnp.arange(T, dtype=jnp.float32) + offset
            freqs = t[:, None] * inv_freq[None, :]
            freqs = jnp.repeat(freqs, 2, axis=-1)
            cos, sin = (jnp.cos(freqs), jnp.sin(freqs))
            xr, xp = (x[..., :ROPE_DIM], x[..., ROPE_DIM:])
            x1, x2 = (xr[..., 0::2], xr[..., 1::2])
            rot = jnp.stack([-x2, x1], axis=-1).reshape(xr.shape)
            return jnp.concatenate([xr * cos + rot * sin, xp], axis=-1)

        def _to_scores(X, W):
            B, T, C = X.shape
            return (X @ W).reshape(B, T, H, C).transpose(0, 2, 1, 3)
        key = jax.random.key(seed)
        ks = jax.random.split(key, 4)
        B, T, C = (1, 256, 128)
        return {'X_Q': jax.random.normal(ks[0], (B, T, C), jnp.float32), 'W_Q': jax.random.normal(ks[1], (C, C * H), jnp.float32) / C, 'W_K': jax.random.normal(ks[2], (C, C * H), jnp.float32) / C, 'W_V': jax.random.normal(ks[3], (C, C * H), jnp.float32) / C, 'gn_weight': jnp.ones((C,), jnp.float32), 'gn_bias': jnp.zeros((C,), jnp.float32)}
    _L1_attn_in = _L1_attn_setup()

    def _L1_ffn_setup():
        import jax, jax.numpy as jnp
        import numpy as np
        B, S, DIM = (4, 512, 128)
        BASE_COUPLING = 0.1
        NUM_CYCLES = 3

        def _gelu(x):
            return jax.nn.gelu(x, approximate=False)

        def _coupling_net(h, w1, b1, w2, b2, w3, b3, w4, b4):
            h = _gelu(h @ w1 + b1)
            h = _gelu(h @ w2 + b2)
            h = _gelu(h @ w3 + b3)
            return jax.nn.sigmoid(h @ w4 + b4)

        def _global_net(h, w1, b1, w2, b2, w3, b3):
            h = _gelu(h @ w1 + b1)
            h = _gelu(h @ w2 + b2)
            return jax.nn.sigmoid(h @ w3 + b3)

        def _twist(x):
            o_r, o_i, p_r, p_i = jnp.split(x, 4, axis=-1)
            return jnp.concatenate([p_r, -p_i, -o_r, o_i], axis=-1)
        key = jax.random.key(seed)
        ks = jax.random.split(key, 9)
        d = DIM

        def w(k, fan_in, fan_out):
            return jax.random.normal(k, (fan_in, fan_out), dtype=jnp.float32) / np.sqrt(fan_in).astype(np.float32)
        inp = {'x': jax.random.normal(ks[0], (B, S, d), dtype=jnp.float32)}
        cn_dims = [(d, d), (d, d // 2), (d // 2, d // 4), (d // 4, 1)]
        for i, (a, b) in enumerate(cn_dims):
            inp[f'cn_w{i + 1}'] = w(ks[1 + i], a, b)
            inp[f'cn_b{i + 1}'] = jnp.zeros((b,), dtype=jnp.float32)
        gc_dims = [(d, d // 2), (d // 2, d // 4), (d // 4, 1)]
        for i, (a, b) in enumerate(gc_dims):
            inp[f'gc_w{i + 1}'] = w(ks[5 + i], a, b)
            inp[f'gc_b{i + 1}'] = jnp.zeros((b,), dtype=jnp.float32)
        inp['adaptive_range'] = jnp.full((1,), 0.2, dtype=jnp.float32)
        return inp
    _L1_ffn_in = _L1_ffn_setup()
    _d = {'L0_attn_x': _L0_attn_in['x'], 'L0_attn_wq': _L0_attn_in['wq'], 'L0_attn_bq': _L0_attn_in['bq'], 'L0_attn_wk': _L0_attn_in['wk'], 'L0_attn_bk': _L0_attn_in['bk'], 'L0_attn_wv': _L0_attn_in['wv'], 'L0_attn_bv': _L0_attn_in['bv'], 'L0_attn_wo': _L0_attn_in['wo'], 'L0_attn_bo': _L0_attn_in['bo'], 'L0_ffn_W1': _L0_ffn_in['W1'], 'L0_ffn_b1': _L0_ffn_in['b1'], 'L0_ffn_W2': _L0_ffn_in['W2'], 'L0_ffn_b2': _L0_ffn_in['b2'], 'L1_attn_W_Q': _L1_attn_in['W_Q'], 'L1_attn_W_K': _L1_attn_in['W_K'], 'L1_attn_W_V': _L1_attn_in['W_V'], 'L1_attn_gn_weight': _L1_attn_in['gn_weight'], 'L1_attn_gn_bias': _L1_attn_in['gn_bias'], 'L1_ffn_cn_w1': _L1_ffn_in['cn_w1'], 'L1_ffn_cn_b1': _L1_ffn_in['cn_b1'], 'L1_ffn_cn_w2': _L1_ffn_in['cn_w2'], 'L1_ffn_cn_b2': _L1_ffn_in['cn_b2'], 'L1_ffn_cn_w3': _L1_ffn_in['cn_w3'], 'L1_ffn_cn_b3': _L1_ffn_in['cn_b3'], 'L1_ffn_cn_w4': _L1_ffn_in['cn_w4'], 'L1_ffn_cn_b4': _L1_ffn_in['cn_b4'], 'L1_ffn_gc_w1': _L1_ffn_in['gc_w1'], 'L1_ffn_gc_b1': _L1_ffn_in['gc_b1'], 'L1_ffn_gc_w2': _L1_ffn_in['gc_w2'], 'L1_ffn_gc_b2': _L1_ffn_in['gc_b2'], 'L1_ffn_gc_w3': _L1_ffn_in['gc_w3'], 'L1_ffn_gc_b3': _L1_ffn_in['gc_b3'], 'L1_ffn_adaptive_range': _L1_ffn_in['adaptive_range']}
    _x0 = _d['L0_attn_x']
    _d['L0_attn_x'] = jax.random.normal(jax.random.fold_in(jax.random.key(seed), 1), (4, 1024, 128), dtype=_x0.dtype)
    del _x0
    return _d

def reference(L0_attn_x, L0_attn_wq, L0_attn_bq, L0_attn_wk, L0_attn_bk, L0_attn_wv, L0_attn_bv, L0_attn_wo, L0_attn_bo, L0_ffn_W1, L0_ffn_b1, L0_ffn_W2, L0_ffn_b2, L1_attn_W_Q, L1_attn_W_K, L1_attn_W_V, L1_attn_gn_weight, L1_attn_gn_bias, L1_ffn_cn_w1, L1_ffn_cn_b1, L1_ffn_cn_w2, L1_ffn_cn_b2, L1_ffn_cn_w3, L1_ffn_cn_b3, L1_ffn_cn_w4, L1_ffn_cn_b4, L1_ffn_gc_w1, L1_ffn_gc_b1, L1_ffn_gc_w2, L1_ffn_gc_b2, L1_ffn_gc_w3, L1_ffn_gc_b3, L1_ffn_adaptive_range):

    def _L0_attn_ref(x, wq, bq, wk, bk, wv, bv, wo, bo):
        import jax, jax.numpy as jnp
        import numpy as np
        NUM_HEADS = 16

        def rotate_half(x):
            h = x.shape[-1] // 2
            return jnp.concatenate([-x[..., h:], x[..., :h]], axis=-1)
        b, s, d = x.shape
        h = NUM_HEADS
        hd = d // h
        q = x @ wq.T + bq
        k = x @ wk.T + bk
        v = x @ wv.T + bv
        q = q.reshape(b, s, h, hd).transpose(0, 2, 1, 3)
        k = k.reshape(b, s, h, hd).transpose(0, 2, 1, 3)
        v = v.reshape(b, s, h, hd).transpose(0, 2, 1, 3)
        theta = 10000.0 ** (-2.0 * jnp.arange(hd // 2, dtype=jnp.float32) / hd)
        freqs = jnp.arange(s, dtype=jnp.float32)[:, None] * theta[None, :]
        cos = jnp.repeat(jnp.cos(freqs), 2, axis=-1)[None, None]
        sin = jnp.repeat(jnp.sin(freqs), 2, axis=-1)[None, None]
        q = q * cos + rotate_half(q) * sin
        k = k * cos + rotate_half(k) * sin
        scores = jnp.einsum('bhqd,bhkd->bhqk', q, k) / jnp.sqrt(jnp.float32(hd))
        attn = jax.nn.softmax(scores, axis=-1)
        out = jnp.einsum('bhqk,bhkd->bhqd', attn, v)
        out = out.transpose(0, 2, 1, 3).reshape(b, s, d)
        return out @ wo.T + bo

    def _L0_ffn_ref(hidden_states, W1, b1, W2, b2):
        import jax, jax.numpy as jnp
        import numpy as np
        HIDDEN = 128
        INTER = 512
        h = jax.nn.relu(jnp.einsum('bsh,hi->bsi', hidden_states, W1) + b1)
        return jnp.einsum('bsi,ih->bsh', h, W2) + b2

    def _L1_attn_ref(X_Q, W_Q, W_K, W_V, gn_weight, gn_bias):
        import jax, jax.numpy as jnp
        import numpy as np
        H = 8
        ROPE_DIM = 64
        GAMMA = 0.96875
        GROUPS = 16
        EPS = 1e-05

        def _rope(x, offset=0):
            T = x.shape[-2]
            inv_freq = 1.0 / 10000.0 ** (np.arange(0, ROPE_DIM, 2, dtype=np.float32) / ROPE_DIM)
            t = jnp.arange(T, dtype=jnp.float32) + offset
            freqs = t[:, None] * inv_freq[None, :]
            freqs = jnp.repeat(freqs, 2, axis=-1)
            cos, sin = (jnp.cos(freqs), jnp.sin(freqs))
            xr, xp = (x[..., :ROPE_DIM], x[..., ROPE_DIM:])
            x1, x2 = (xr[..., 0::2], xr[..., 1::2])
            rot = jnp.stack([-x2, x1], axis=-1).reshape(xr.shape)
            return jnp.concatenate([xr * cos + rot * sin, xp], axis=-1)

        def _to_scores(X, W):
            B, T, C = X.shape
            return (X @ W).reshape(B, T, H, C).transpose(0, 2, 1, 3)
        B, T, C = X_Q.shape
        Q = _rope(_to_scores(X_Q, W_Q))
        K = _rope(_to_scores(X_Q, W_K))
        V = _to_scores(X_Q, W_V)
        Q, K, V = (jax.nn.silu(Q), jax.nn.silu(K), jax.nn.silu(V))
        n = jnp.arange(T)
        diff = n[:, None] - n[None, :]
        D = jnp.where(diff >= 0, GAMMA ** jnp.maximum(diff, 0).astype(jnp.float32), 0.0)
        A = jnp.einsum('bhqc,bhkc->bhqk', Q, K)
        A = A * D
        A = jnp.swapaxes(A, -2, -1)
        out = A @ V
        out = out.sum(axis=1)
        x = out.reshape(B * T, GROUPS, C // GROUPS)
        mu = x.mean(-1, keepdims=True)
        var = x.var(-1, keepdims=True)
        xn = (x - mu) * jax.lax.rsqrt(var + EPS)
        out = xn.reshape(B * T, C) * gn_weight + gn_bias
        return out.reshape(B, T, C)

    def _L1_ffn_ref(x, cn_w1, cn_b1, cn_w2, cn_b2, cn_w3, cn_b3, cn_w4, cn_b4, gc_w1, gc_b1, gc_w2, gc_b2, gc_w3, gc_b3, adaptive_range):
        import jax, jax.numpy as jnp
        import numpy as np
        B, S, DIM = (4, 512, 128)
        BASE_COUPLING = 0.1
        NUM_CYCLES = 3

        def _gelu(x):
            return jax.nn.gelu(x, approximate=False)

        def _coupling_net(h, w1, b1, w2, b2, w3, b3, w4, b4):
            h = _gelu(h @ w1 + b1)
            h = _gelu(h @ w2 + b2)
            h = _gelu(h @ w3 + b3)
            return jax.nn.sigmoid(h @ w4 + b4)

        def _global_net(h, w1, b1, w2, b2, w3, b3):
            h = _gelu(h @ w1 + b1)
            h = _gelu(h @ w2 + b2)
            return jax.nn.sigmoid(h @ w3 + b3)

        def _twist(x):
            o_r, o_i, p_r, p_i = jnp.split(x, 4, axis=-1)
            return jnp.concatenate([p_r, -p_i, -o_r, o_i], axis=-1)
        global_context = x.mean(axis=1, keepdims=True)
        gf = _global_net(global_context, gc_w1, gc_b1, gc_w2, gc_b2, gc_w3, gc_b3)
        out = x
        for _ in range(NUM_CYCLES):
            tf = _coupling_net(out, cn_w1, cn_b1, cn_w2, cn_b2, cn_w3, cn_b3, cn_w4, cn_b4)
            combined = 0.7 * gf + 0.3 * tf
            coupling = BASE_COUPLING + adaptive_range * (combined - 0.5) * 2.0
            out = out + coupling * _twist(out)
        return out
    x = L0_attn_x
    x = _layernorm(x + _L0_attn_ref(x, L0_attn_wq, L0_attn_bq, L0_attn_wk, L0_attn_bk, L0_attn_wv, L0_attn_bv, L0_attn_wo, L0_attn_bo), axis=-1)
    x = _layernorm(x + _L0_ffn_ref(x, L0_ffn_W1, L0_ffn_b1, L0_ffn_W2, L0_ffn_b2), axis=-1)
    x = _layernorm(x + _L1_attn_ref(x, L1_attn_W_Q, L1_attn_W_K, L1_attn_W_V, L1_attn_gn_weight, L1_attn_gn_bias), axis=-1)
    x = _layernorm(x + _L1_ffn_ref(x, L1_ffn_cn_w1, L1_ffn_cn_b1, L1_ffn_cn_w2, L1_ffn_cn_b2, L1_ffn_cn_w3, L1_ffn_cn_b3, L1_ffn_cn_w4, L1_ffn_cn_b4, L1_ffn_gc_w1, L1_ffn_gc_b1, L1_ffn_gc_w2, L1_ffn_gc_b2, L1_ffn_gc_w3, L1_ffn_gc_b3, L1_ffn_adaptive_range), axis=-1)
    return x

_drawn_inputs = setup_inputs


def setup_inputs(seed=0):
    import zlib

    import numpy as np

    out = dict(_drawn_inputs(seed))
    spreads = {'L1_attn_gn_weight': (1.0, 0.2),
     'L1_attn_gn_bias': (0.0, 0.1),
     'L1_ffn_cn_b1': (0.0, 0.8),
     'L1_ffn_cn_b2': (0.0, 0.8),
     'L1_ffn_cn_b3': (0.0, 0.8),
     'L1_ffn_gc_b1': (0.0, 0.8),
     'L1_ffn_gc_b2': (0.0, 0.8)}
    factors = {'L0_attn_wq': 8.0,
     'L0_attn_bq': 8.0,
     'L0_attn_wk': 8.0,
     'L0_attn_bk': 8.0,
     'L0_attn_wv': 8.0,
     'L0_attn_bv': 5.062,
     'L0_attn_wo': 5.435,
     'L0_ffn_b1': 2.846,
     'L1_ffn_cn_w1': 7.02,
     'L1_ffn_cn_w2': 5.935,
     'L1_ffn_cn_w3': 5.802,
     'L1_ffn_cn_w4': 5.805,
     'L1_ffn_gc_w1': 6.956,
     'L1_ffn_gc_w2': 7.669,
     'L1_ffn_gc_w3': 8.0}
    for name, (base, spread) in spreads.items():
        noise = np.random.default_rng([zlib.crc32(name.encode()), seed]).standard_normal(out[name].shape)
        drawn = base * np.exp(spread * noise) if base else spread * noise
        out[name] = jnp.asarray(drawn.astype(out[name].dtype))
    for name, factor in factors.items():
        out[name] = (out[name] * factor).astype(out[name].dtype)
    return out
```

```python
from contextlib import ExitStack

import numpy as np

import concourse.bass as bass
from concourse import mybir

F32 = mybir.dt.float32
BF16 = mybir.dt.bfloat16
ALU = mybir.AluOpType
ACT = mybir.ActivationFunctionType
AX = mybir.AxisListType

BATCH, SEQ, DIM = 4, 1024, 128
TOKENS = BATCH * SEQ
P = 128
N = 512
CPT = N // P
TILES = TOKENS // N
CHUNKS = TOKENS // P
CPB = SEQ // P
EPS = 1e-5
START = 1

HEADS, HD = 16, 8
GH = 4
GROUPS = HEADS // GH
PARTS = 3
TERM_ROWS = PARTS * PARTS * HD
MAX_ROWS = 96
SHIFT_ROWS = MAX_ROWS + PARTS
VW = HD + 1
INTER = 512

RHEADS = 8
ROPE_DIM = 64
GAMMA = 0.96875
GN = 16
GW = DIM // GN
BASE_COUPLING = 0.1
CYCLES = 3


class Count:

    def __init__(self, base=0):
        self.base, self.n = base, 0

    def next(self):
        self.n += 1
        return self.base + self.n


def wait_apart(engine, sem, value, passed):
    engine.wait_ge(sem, value)
    engine.sem_inc(passed, 1)


def project_and_split(nc, io, scr):
    with ExitStack() as ctx:
        def sb(name, shape, dt=F32):
            return ctx.enter_context(nc.sbuf_tensor(name, shape, dt))

        def sem(name):
            return ctx.enter_context(nc.semaphore(name))

        ps = ctx.enter_context(nc.psum_tensor("a_ps", [P, 5, N], F32))
        w = sb("a_w", [P, 5, P])
        bias = sb("a_bias", [P, 4])
        bv = sb("a_bv", [P, N])
        cos, sin = sb("a_cos", [P, SEQ]), sb("a_sin", [P, SEQ])
        xt = sb("a_xt", [P, 2, N])
        cos_part, sin_part = sb("a_cos_part", [P, 2, N]), sb("a_sin_part", [P, 2, N])
        turned, rest = sb("a_turned", [P, 2, N]), sb("a_rest", [P, 2, N])
        parts = sb("a_parts", [P, 2, 2, PARTS, N], BF16)
        vals = sb("a_vals", [P, 2, CPT, HEADS, VW])

        consts_loaded = sem("a_consts_loaded")
        x_loaded = [sem(f"a_x_loaded{k}") for k in range(2)]
        projected = [sem(f"a_projected{z}") for z in range(2)]
        v_projected = sem("a_v_projected")
        v_read = sem("a_v_read")
        ones_set = sem("a_ones_set")
        angled = [sem(f"a_angled{z}") for z in range(2)]
        turned_ready = [sem(f"a_turned_ready{z}") for z in range(2)]
        high_ready = [sem(f"a_high_ready{z}") for z in range(2)]
        rest_ready = [sem(f"a_rest_ready{z}") for z in range(2)]
        mid_ready = [sem(f"a_mid_ready{z}") for z in range(2)]
        low_ready = [sem(f"a_low_ready{z}") for z in range(2)]
        parts_stored = [[sem(f"a_parts_stored{z}{k}") for k in range(2)] for z in range(2)]
        vals_stored = [sem(f"a_vals_stored{k}") for k in range(2)]
        passed = sem("a_passed")
        block = ctx.enter_context(nc.Block())

        @block.sync
        def _(sp):
            for k in range(2):
                sp.dma_start(xt[:, k], io["xT"][:, k * N:(k + 1) * N]).then_inc(x_loaded[k], 16)
            with sp.Fori(0, TILES // 2) as i:
                for k in range(2):
                    for z in range(2):
                        sp.wait_ge(mid_ready[z], i * 2 + k + 1)
                        wait_apart(sp, low_ready[z], i * 2 + k + 1, passed)
                        sp.dma_start(scr["parts"][z].rearrange("s p t -> p s t")[:, :, bass.ds(i * (2 * N) + k * N, N)],
                                     parts[:, z, k]).then_inc(parts_stored[z][k], 16)
                    wait_apart(sp, v_read, START + i * 2 + k + 1, passed)
                    sp.dma_start(scr["vals"].rearrange("(t c p) w -> t p c w", c=CPT, p=P)[i * 2 + k],
                                 vals[:, k].rearrange("p c h w -> p c (h w)")).then_inc(vals_stored[k], 16)
            for k in range(2):
                sp.wait_ge(vals_stored[k], START + 16 * TILES // 2)
                for z in range(2):
                    sp.wait_ge(parts_stored[z][k], START + 16 * TILES // 2)

        @block.gpsimd
        def _(pool):
            for primed in (*angled, v_read, *(s for pair in parts_stored for s in pair), *vals_stored):
                pool.sem_inc(primed, START)
            nc.gpsimd.memset(vals[:], 1.0).then_inc(ones_set, 1)
            with pool.Fori(0, TILES // 2) as i:
                for k in range(2):
                    for z in range(2):
                        pool.wait_ge(angled[z], START + i * 2 + k + 1)
                        nc.gpsimd.tensor_tensor(turned[:, z], cos_part[:, z], sin_part[:, z],
                                                ALU.add).then_inc(turned_ready[z], 1)
                    for z in range(2):
                        pool.wait_ge(mid_ready[z], i * 2 + k + 1)
                        nc.gpsimd.tensor_tensor(parts[:, z, k, 2], rest[:, z], parts[:, z, k, 1],
                                                ALU.subtract).then_inc(low_ready[z], 1)

        @block.scalar
        def _(act):
            for t, name in ((w, "w0"), (bias, "bias0"), (cos, "cos0"), (sin, "sin0"), (bv, "bv")):
                act.dma_start(t[:], io[name]).then_inc(consts_loaded, 16)

            def pair(i, last):
                for k in range(2):
                    for z in range(2):
                        act.wait_ge(turned_ready[z], i * 2 + k + 1)
                        act.wait_ge(parts_stored[z][k], START + i * 16)
                        nc.scalar.activation(parts[:, z, k, 0], turned[:, z], ACT.Copy).then_inc(high_ready[z], 1)
                    for z in range(2):
                        act.wait_ge(rest_ready[z], i * 2 + k + 1)
                        nc.scalar.activation(parts[:, z, k, 1], rest[:, z], ACT.Copy).then_inc(mid_ready[z], 1)
                    if not last:
                        act.wait_ge(v_projected, i * 2 + k + 1)
                        act.dma_start(xt[:, k], io["xT"][:, bass.ds((i + 1) * (2 * N) + k * N, N)]).then_inc(x_loaded[k], 16)

            with act.Fori(0, TILES // 2 - 1) as i:
                pair(i, False)
            pair(TILES // 2 - 1, True)

        @block.tensor
        def _(pe):
            pe.wait_ge(consts_loaded, 5 * 16)
            with pe.Fori(0, TILES // 2) as i:
                for k in range(2):
                    pe.wait_ge(x_loaded[k], i * 16 + 16)
                    for z in range(2):
                        pe.wait_ge(angled[z], START + i * 2 + k)
                        nc.tensor.matmul(ps[:, 2 * z], w[:, 2 * z], xt[:, k], start=True, stop=True)
                        nc.tensor.matmul(ps[:, 2 * z + 1], w[:, 2 * z + 1], xt[:, k],
                                         start=True, stop=True).then_inc(projected[z], 1)
                    pe.wait_ge(v_read, START + i * 2 + k)
                    for c in range(CPT):
                        last = nc.tensor.matmul(ps[:, 4, c * P:(c + 1) * P], xt[:, k, c * P:(c + 1) * P], w[:, 4],
                                                start=True, stop=True)
                    last.then_inc(v_projected, 1)

        @block.vector
        def _(dve):
            dve.wait_ge(consts_loaded, 5 * 16)
            dve.wait_ge(ones_set, 1)
            with dve.Fori(0, TILES // 2) as i:
                for k in range(2):
                    at = slice(k * N, (k + 1) * N)
                    for z in range(2):
                        dve.wait_ge(projected[z], i * 2 + k + 1)
                        nc.vector.scalar_tensor_tensor(out=cos_part[:, z], in0=ps[:, 2 * z], scalar=bias[:, 2 * z:2 * z + 1],
                                                       in1=cos[:, at], op0=ALU.add, op1=ALU.mult)
                        nc.vector.scalar_tensor_tensor(out=sin_part[:, z], in0=ps[:, 2 * z + 1],
                                                       scalar=bias[:, 2 * z + 1:2 * z + 2], in1=sin[:, at],
                                                       op0=ALU.add, op1=ALU.mult).then_inc(angled[z], 1)
                    dve.wait_ge(v_projected, i * 2 + k + 1)
                    dve.wait_ge(vals_stored[k], START + i * 16)
                    nc.vector.tensor_tensor(vals[:, k, :, :, 0:HD], ps[:, 4].rearrange("p (c h d) -> p c h d", c=CPT, d=HD),
                                            bv[:].rearrange("p (c h d) -> p c h d", c=CPT, d=HD), ALU.add).then_inc(v_read, 1)
                    for z in range(2):
                        dve.wait_ge(high_ready[z], i * 2 + k + 1)
                        nc.vector.tensor_tensor(rest[:, z], turned[:, z], parts[:, z, k, 0],
                                                ALU.subtract).then_inc(rest_ready[z], 1)


def attend(nc, io, scr):
    LEAD = 5
    QBLOCKS = SEQ // P
    HALVES = SEQ // N
    PER_HEAD = QBLOCKS * HALVES
    BANKS = 3
    PROBS = 8
    LOADS = 2 * PARTS * PARTS + 1
    ITEMS = HEADS * PER_HEAD + GROUPS
    LEAD_ITEMS = LEAD * PER_HEAD + 1
    TILES_B = HEADS * PER_HEAD
    LATER = 4
    SPLIT_STEPS = 4
    STORES = GH * 2 * 16
    with ExitStack() as ctx:
        def sb(name, shape, dt=F32):
            return ctx.enter_context(nc.sbuf_tensor(name, shape, dt))

        def sem(name):
            return ctx.enter_context(nc.semaphore(name))

        max_ps = ctx.enter_context(nc.psum_tensor("b_max_ps", [P, BANKS, N], F32))
        score_ps = ctx.enter_context(nc.psum_tensor("b_score_ps", [P, BANKS, N], F32))
        out_ps = ctx.enter_context(nc.psum_tensor("b_out_ps", [P, HALVES, N], F32))
        q = sb("b_q", [P, GROUPS, GH, SEQ], BF16)
        k_ = sb("b_k", [P, GROUPS, GH, SEQ], BF16)
        v = sb("b_v", [P, GROUPS, QBLOCKS, GH * VW])
        ident, identf = sb("b_ident", [P, P], BF16), sb("b_identf", [P, P])
        probs = sb("b_probs", [P, PROBS, N])
        half_max = sb("b_half_max", [P, GROUPS, GH, QBLOCKS, HALVES])
        full_max, mid_rest, low_rest = (sb(f"b_{n}", [P, GH, QBLOCKS]) for n in ("full_max", "mid_rest", "low_rest"))
        shift = sb("b_shift", [P, QBLOCKS, GH, PARTS], BF16)
        shift_t = sb("b_shift_t", [GH * PARTS, 2, SEQ], BF16)
        outs = sb("b_outs", [P, 2, HALVES, N])

        ident_loaded, ident_ready = sem("b_ident_loaded"), sem("b_ident_ready")
        zeros_set = sem("b_zeros_set")
        operands_loaded = [sem(f"b_operands_loaded{j}") for j in range(GROUPS)]
        shift_loaded = [sem(f"b_shift_loaded{j}") for j in range(GROUPS)]
        max_scored = sem("b_max_scored")
        max_read = sem("b_max_read")
        chain = sem("b_chain")
        shift_ready = sem("b_shift_ready")
        scored = sem("b_scored")
        probs_ready = sem("b_probs_ready")
        probs_used = sem("b_probs_used")
        out_read = sem("b_out_read")
        outs_stored = [sem(f"b_outs_stored{g}") for g in range(2)]
        passed = sem("b_passed")
        block = ctx.enter_context(nc.Block())

        def tokens(b):
            return slice(b * SEQ, (b + 1) * SEQ) if isinstance(b, int) else bass.ds(b * SEQ, SEQ)

        def items(first, last):
            out = []
            turn = None
            for head in range(first, last):
                for t in range(PER_HEAD):
                    if turn is not None and t == LATER:
                        out.append(("turn", turn, 0))
                        turn = None
                    out.append(("tile", head, t))
                if head % GH == GH - 1:
                    turn = head // GH % GROUPS
            if turn is not None:
                out.append(("turn", turn, 0))
            return out

        def load_group(sp, b, j):
            for z, dst in ((0, q), (1, k_)):
                for t in range(PARTS * PARTS):
                    part = t // PARTS if z == 0 else t % PARTS
                    src = scr["parts"][z][part].rearrange("(h d) t -> d h t", d=HD)[:, j * GH:(j + 1) * GH, tokens(b)]
                    sp.dma_start(dst[t * HD:(t + 1) * HD, j], src).then_inc(operands_loaded[j], 16)
            sp.dma_start(v[:, j], scr["vals"][tokens(b), j * GH * VW:(j + 1) * GH * VW]
                         .rearrange("(k p) w -> p k w", p=P)).then_inc(operands_loaded[j], 16)

        @block.sync
        def _(sp):
            sp.dma_start(identf[:], io["ident"]).then_inc(ident_loaded, 16)
            sp.wait_ge(zeros_set, 3)
            for j in range(GROUPS):
                load_group(sp, 0, j)

            def batch(b, last):
                for j in range(GROUPS):
                    wait_apart(sp, out_read, b * (GROUPS * HALVES) + HALVES * (j + 1) + HALVES, passed)
                    rows = outs[:, j % 2].rearrange("p a n -> p (a n)")
                    at = tokens(b)
                    for h in range(GH):
                        head = j * GH + h
                        sp.dma_start(scr["o"][head * HD:(head + 1) * HD, at], rows[32 * h:32 * h + HD]).then_inc(outs_stored[j % 2], 16)
                        sp.dma_start(scr["z"][head:head + 1, at], rows[32 * h + HD:32 * h + HD + 1]).then_inc(outs_stored[j % 2], 16)
                    if not last:
                        load_group(sp, b + 1, j)

            with sp.Fori(0, BATCH - 1) as b:
                batch(b, False)
            batch(BATCH - 1, True)
            for g in range(2):
                sp.wait_ge(outs_stored[g], START + BATCH * GROUPS // 2 * GH * 2 * 16)

        @block.gpsimd
        def _(pool):
            for primed in (probs_used, *outs_stored, probs_ready):
                pool.sem_inc(primed, START)
            def move_shift(count, j):
                wait_apart(pool, max_read, count, passed)
                for h in range(GH):
                    pool.dma_start(q[MAX_ROWS:SHIFT_ROWS, j, h], shift_t[PARTS * h:PARTS * (h + 1), j % 2]).then_inc(shift_loaded[j], 16)

            for n, (kind, a, _) in enumerate(items(0, LEAD)):
                if kind == "turn":
                    move_shift(n + 1, a)

            def batch(b, last):
                for n, (kind, a, _) in enumerate(items(LEAD, last)):
                    if kind == "turn":
                        move_shift(b * ITEMS + LEAD_ITEMS + n + 1, a)

            with pool.Fori(0, BATCH - 1) as b:
                batch(b, HEADS + LEAD)
            batch(BATCH - 1, HEADS)
            for j in range(GROUPS):
                pool.wait_ge(shift_loaded[j], BATCH * GH * 16)

        @block.scalar
        def _(act):
            def read_out(b, j):
                for half in range(HALVES):
                    step = PER_HEAD - HALVES + half
                    act.wait_ge(probs_used, START + b * TILES_B + (j * PER_HEAD + step + 1) * GH)
                    act.wait_ge(outs_stored[j % 2], START + (b * (2 * STORES) + (STORES if j >= 2 else 0)))
                    nc.scalar.activation(outs[:, j % 2, half], out_ps[:, half], ACT.Copy).then_inc(out_read, 1)

            with act.Fori(0, BATCH) as b:
                for j in range(GROUPS):
                    for step in range(PER_HEAD):
                        for h in range(GH):
                            n = (j * PER_HEAD + step) * GH + h
                            act.wait_ge(scored, b * TILES_B + n + 1)
                            act.wait_ge(probs_used, START + b * TILES_B + max(n - PROBS + 1, 0))
                            nc.scalar.activation(probs[:, n % PROBS], score_ps[:, n % BANKS], ACT.Exp,
                                                 scale=float(1.0 / np.sqrt(np.float32(HD)))).then_inc(probs_ready, 1)
                        if step == 0 and j > 0:
                            read_out(b, j - 1)
                read_out(b, GROUPS - 1)

        @block.vector
        def _(dve):
            nc.vector.memset(q[:].bitcast(F32), 0.0).then_inc(zeros_set, 1)
            nc.vector.memset(k_[0:MAX_ROWS].bitcast(F32), 0.0).then_inc(zeros_set, 1)
            nc.vector.memset(k_[MAX_ROWS:P], 1.0).then_inc(zeros_set, 1)
            for half in range(HALVES):
                nc.vector.memset(out_ps[:, half], 0.0).then_inc(out_read, 1)
            dve.wait_ge(ident_loaded, 16)
            nc.vector.tensor_copy(ident[:], identf[:]).then_inc(ident_ready, 1)

            def split(group, read, splits):
                chained = Count(splits * SPLIT_STEPS)
                part = [shift[:, :, :, s].rearrange("p q h -> p h q") for s in range(PARTS)]
                dve.wait_ge(max_read, read)
                nc.vector.tensor_tensor(full_max[:], half_max[:, group, :, :, 0], half_max[:, group, :, :, 1],
                                        ALU.max).then_inc(chain, 1)
                dve.wait_ge(chain, chained.next())
                nc.vector.tensor_scalar(part[0], full_max[:], -1.0, None, ALU.mult).then_inc(chain, 1)
                dve.wait_ge(chain, chained.next())
                nc.vector.scalar_tensor_tensor(out=mid_rest[:], in0=full_max[:], scalar=-1.0, in1=part[0],
                                               op0=ALU.mult, op1=ALU.subtract).then_inc(chain, 1)
                dve.wait_ge(chain, chained.next())
                nc.vector.tensor_copy(part[1], mid_rest[:]).then_inc(chain, 1)
                dve.wait_ge(chain, chained.next())
                nc.vector.tensor_tensor(part[2], mid_rest[:], part[1], ALU.subtract).then_inc(shift_ready, 1)

            def read_items(todo, base, splits):
                for n, (kind, a, t) in enumerate(todo):
                    dve.wait_ge(max_scored, base + n + 1)
                    if kind == "tile":
                        group = a // GH % GROUPS
                        nc.vector.tensor_reduce(half_max[:, group, a % GH, t // HALVES, t % HALVES:t % HALVES + 1],
                                                max_ps[:, n % BANKS], AX.X, ALU.max).then_inc(max_read, 1)
                        if a % GH == GH - 1 and t == PER_HEAD - 1:
                            split(group, base + n + 1, splits)
                            splits = splits + 1
                    else:
                        nc.vector.tensor_copy(shift_t[:, a % 2],
                                              max_ps[0:GH * PARTS, n % BANKS].bitcast(BF16)).then_inc(max_read, 1)

            read_items(items(0, LEAD), 0, 0)

            def batch(b, last):
                read_items(items(LEAD, last), b * ITEMS + LEAD_ITEMS, b * GROUPS + 1)

            with dve.Fori(0, BATCH - 1) as b:
                batch(b, HEADS + LEAD)
            batch(BATCH - 1, HEADS)

        @block.tensor
        def _(pe):
            pe.wait_ge(ident_ready, 1)

            def max_item(item, n, base, loaded, splits):
                kind, a, t = item
                if n >= BANKS:
                    pe.wait_ge(max_read, base + (n - BANKS + 1))
                else:
                    pe.wait_ge(max_read, base)
                if kind == "tile":
                    group, h = a // GH % GROUPS, a % GH
                    qb, half = t // HALVES, t % HALVES
                    if t == 0 and h == 0:
                        pe.wait_ge(operands_loaded[group], loaded(a))
                    nc.tensor.matmul(max_ps[:, n % BANKS], q[0:MAX_ROWS, group, h, qb * P:(qb + 1) * P],
                                     k_[0:MAX_ROWS, group, h, half * N:(half + 1) * N],
                                     start=True, stop=True).then_inc(max_scored, 1)
                else:
                    pe.wait_ge(shift_ready, splits)
                    for qb in range(QBLOCKS):
                        last = nc.tensor.transpose(max_ps[0:GH * PARTS, n % BANKS].bitcast(BF16)[:, qb * P:(qb + 1) * P],
                                                   shift[:, qb].rearrange("p h s -> p (h s)"), ident[:])
                    last.then_inc(max_scored, 1)

            for n, item in enumerate(items(0, LEAD)):
                max_item(item, n, 0, lambda head: LOADS * 16, 1)

            def apply(b, j, step):
                kb, half = step // HALVES, step % HALVES
                if kb == 0:
                    pe.wait_ge(out_read, b * (GROUPS * HALVES) + j * HALVES + half + 1)
                for h in range(GH):
                    n = (j * PER_HEAD + step) * GH + h
                    pe.wait_ge(probs_ready, START + b * TILES_B + n + 1)
                    nc.tensor.matmul(out_ps[32 * h:32 * h + VW, half], v[:, j, kb, h * VW:(h + 1) * VW],
                                     probs[:, n % PROBS], start=(kb == 0), stop=(kb == QBLOCKS - 1)).then_inc(probs_used, 1)

            def batch(b, last):
                todo = items(LEAD, last)
                base = b * ITEMS + LEAD_ITEMS
                splits = 1
                done = 0
                for j in range(GROUPS):
                    pe.wait_ge(shift_loaded[j], b * (GH * 16) + GH * 16)
                    for step in range(PER_HEAD):
                        kb, half = step // HALVES, step % HALVES
                        for h in range(GH):
                            n = (j * PER_HEAD + step) * GH + h
                            pe.wait_ge(probs_ready, START + b * TILES_B + max(n - BANKS + 1, 0))
                            nc.tensor.matmul(score_ps[:, n % BANKS], k_[0:SHIFT_ROWS, j, h, kb * P:(kb + 1) * P],
                                             q[0:SHIFT_ROWS, j, h, half * N:(half + 1) * N],
                                             start=True, stop=True).then_inc(scored, 1)
                            for item in todo[done:done + (2 if todo[done:done + 1] and todo[done][0] == "turn" else 1)]:
                                splits += item[0] == "turn"
                                max_item(item, done, base,
                                         lambda head: b * (LOADS * 16) + (LOADS * 16 if head < HEADS else 2 * LOADS * 16),
                                         b * GROUPS + splits)
                                done += 1
                        if step > 0:
                            apply(b, j, step - 1)
                        elif j > 0:
                            apply(b, j - 1, PER_HEAD - 1)
                apply(b, GROUPS - 1, PER_HEAD - 1)
                assert done == len(todo)

            with pe.Fori(0, BATCH - 1) as b:
                batch(b, HEADS + LEAD)
            batch(BATCH - 1, HEADS)


def norm_stats(dve, y, stats, mean_var, chain, chained, done, passed):
    for c in range(CPT):
        last = dve.bn_stats(stats[:, c], y[:, c])
    last.then_inc(chain, 1)
    wait_apart(dve, chain, chained.next(), passed)
    for c in range(CPT):
        last = dve.bn_aggr(mean_var[:, c], stats[:, c])
    last.then_inc(done, 1)


def norm_apply(dve, y, out, deviation, inverse, mean_var, chain, chained, done):
    dve.reciprocal(inverse, deviation).then_inc(chain, 1)
    dve.wait_ge(chain, chained.next())
    for c in range(CPT):
        last = dve.tensor_scalar(out[:, c], y[:, c], mean_var[:, c, 0:1], inverse[:, c:c + 1],
                                 ALU.subtract, ALU.mult)
    last.then_inc(done, 1)


def project_out_and_ffn(nc, io, scr):
    FB = INTER // P
    with ExitStack() as ctx:
        def sb(name, shape, dt=F32):
            return ctx.enter_context(nc.sbuf_tensor(name, shape, dt))

        def sem(name):
            return ctx.enter_context(nc.semaphore(name))

        wo_ps, y_ps, turn1_ps, turn2_ps = (ctx.enter_context(nc.psum_tensor(f"c_{n}", [P, N], F32))
                                           for n in ("wo_ps", "y_ps", "turn1_ps", "turn2_ps"))
        h_ps = ctx.enter_context(nc.psum_tensor("c_h_ps", [P, FB, N], F32))
        ident, wo = sb("c_ident", [P, P]), sb("c_wo", [P, P])
        w1, b1, w2 = sb("c_w1", [P, INTER]), sb("c_b1", [P, FB]), sb("c_w2", [P, FB, P])
        bo, b2 = sb("c_bo", [P, CPT, P]), sb("c_b2", [P, CPT, P])
        sums, eps = sb("c_sums", [P, HEADS * TOKENS // P]), sb("c_eps", [P, 1])
        o, rz, x = sb("c_o", [P, 2, N]), sb("c_rz", [P, 2, N]), sb("c_x", [P, 2, CPT, P])
        a, xb = sb("c_a", [P, 2, N]), sb("c_xb", [P, 2, CPT, P])
        y1, x1, x1b = sb("c_y1", [P, CPT, P]), sb("c_x1", [P, 2, CPT, P]), sb("c_x1b", [P, 2, CPT, P])
        x1t, h = sb("c_x1t", [P, 2, N]), sb("c_h", [P, FB, N])
        y2, x2, x2t = sb("c_y2", [P, CPT, P]), sb("c_x2", [P, 2, CPT, P]), sb("c_x2t", [P, 2, N])
        stats = [sb(f"c_stats{s}", [P, CPT, 6]) for s in range(2)]
        mean_var = [sb(f"c_mean_var{s}", [P, CPT, 2]) for s in range(2)]
        deviation = [sb(f"c_deviation{s}", [P, CPT]) for s in range(2)]
        inverse = [sb(f"c_inverse{s}", [P, CPT]) for s in range(2)]

        consts_loaded, eps_set = sem("c_consts_loaded"), sem("c_eps_set")
        sums_loaded, sums_inverted, inverses_stored = sem("c_sums_loaded"), sem("c_sums_inverted"), sem("c_inverses_stored")
        tile_loaded = [sem(f"c_tile_loaded{k}") for k in range(2)]
        a_ready, xb_ready, x1b_ready = sem("c_a_ready"), sem("c_xb_ready"), sem("c_x1b_ready")
        wo_done, h_done, y_done = sem("c_wo_done"), sem("c_h_done"), sem("c_y_done")
        turned = [sem(f"c_turned{s}") for s in range(2)]
        chain = sem("c_chain")
        stats_ready = [sem(f"c_stats_ready{s}") for s in range(2)]
        deviation_ready = [sem(f"c_deviation_ready{s}") for s in range(2)]
        normed = [sem(f"c_normed{s}") for s in range(2)]
        h_ready = sem("c_h_ready")
        x1t_ready, x2t_ready = sem("c_x1t_ready"), sem("c_x2t_ready")
        y_read = [sem(f"c_y_read{s}") for s in range(2)]
        stored = [sem(f"c_stored{k}") for k in range(2)]
        stored_t = [sem(f"c_stored_t{k}") for k in range(2)]
        passed = sem("c_passed")
        block = ctx.enter_context(nc.Block())

        def tile(t):
            return slice(t * N, (t + 1) * N) if isinstance(t, int) else bass.ds(t * N, N)

        @block.sync
        def _(sp):
            sp.dma_start(sums[:], scr["z"].rearrange("h (a t) -> (h a) t", a=P // HEADS)).then_inc(sums_loaded, 16)
            sp.wait_ge(sums_inverted, 1)
            sp.dma_start(scr["rz"].rearrange("h (a t) -> (h a) t", a=P // HEADS), sums[:]).then_inc(inverses_stored, 16)
            sp.wait_ge(inverses_stored, 16)

            def load(t, k):
                sp.dma_start(o[:, k], scr["o"][:, tile(t)]).then_inc(tile_loaded[k], 16)
                sp.dma_start(rz[:, k], scr["rz"][:, tile(t)].unsqueeze(1).broadcast_to([HEADS, HD, N])).then_inc(tile_loaded[k], 16)
                sp.dma_start(x[:, k], io["x"][tile(t)].rearrange("(c p) d -> p c d", p=P)).then_inc(tile_loaded[k], 16)

            def store(t, k):
                wait_apart(sp, normed[1], t + 1, passed)
                sp.dma_start(scr["x2"][tile(t)].rearrange("(c p) d -> p c d", p=P), x2[:, k]).then_inc(stored[k], 16)
                wait_apart(sp, x2t_ready, t + 1, passed)
                sp.dma_start(scr["x2T"][:, tile(t)], x2t[:, k]).then_inc(stored_t[k], 16)

            for k in range(2):
                load(k, k)
            with sp.Fori(0, TILES // 2 - 1) as i:
                for k in range(2):
                    wait_apart(sp, xb_ready, i * 2 + k + 1, passed)
                    load(i * 2 + (2 + k), k)
                    store(i * 2 + k, k)
            for k in range(2):
                store(TILES - 2 + k, k)
            for k in range(2):
                sp.wait_ge(stored[k], START + TILES // 2 * 16)
                sp.wait_ge(stored_t[k], START + TILES // 2 * 16)

        @block.gpsimd
        def _(pool):
            for primed in (*y_read, *stored, *stored_t):
                pool.sem_inc(primed, START)
            nc.gpsimd.memset(eps[:], EPS).then_inc(eps_set, 1)
            pool.wait_ge(consts_loaded, 7 * 16)
            with pool.Fori(0, TILES // 2) as i:
                for k in range(2):
                    pool.wait_ge(tile_loaded[k], i * 48 + 48)
                    pool.wait_ge(y_read[0], START + (i * 2 + (k - 1 if k else 0)))
                    nc.gpsimd.tensor_tensor(a[:, k], o[:, k], rz[:, k], ALU.mult).then_inc(a_ready, 1)
                    nc.gpsimd.tensor_tensor(xb[:, k], x[:, k], bo[:], ALU.add).then_inc(xb_ready, 1)
                    pool.wait_ge(normed[0], i * 2 + k + 1)
                    pool.wait_ge(y_read[1], START + (i * 2 + (k - 1 if k else 0)))
                    nc.gpsimd.tensor_tensor(x1b[:, k], x1[:, k], b2[:], ALU.add).then_inc(x1b_ready, 1)

        @block.scalar
        def _(act):
            for t, name in ((ident, "ident"), (wo, "woT"), (w1, "w1"), (b1, "b1"), (w2, "w2")):
                act.dma_start(t[:], io[name]).then_inc(consts_loaded, 16)
            for t, name in ((bo, "bo"), (b2, "b2")):
                act.dma_start(t[:].rearrange("p c d -> p (c d)"), io[name]).then_inc(consts_loaded, 16)
            act.wait_ge(eps_set, 1)

            def root(s, t):
                act.wait_ge(stats_ready[s], t + 1)
                nc.scalar.activation(deviation[s][:], mean_var[s][:, :, 1], ACT.Sqrt, bias=eps[:, 0:1]).then_inc(deviation_ready[s], 1)

            def read_turn1(t, k):
                act.wait_ge(turned[0], t + 1)
                nc.scalar.activation(x1t[:, k], turn1_ps[:], ACT.Copy).then_inc(x1t_ready, 1)

            def read_turn2(t, k, i2):
                act.wait_ge(turned[1], t + 1)
                act.wait_ge(stored_t[k], START + i2 * 16)
                nc.scalar.activation(x2t[:, k], turn2_ps[:], ACT.Copy).then_inc(x2t_ready, 1)

            def relu(t, f):
                act.wait_ge(h_done, t * FB + f + 1)
                act.wait_ge(y_done, t)
                nc.scalar.activation(h[:, f], h_ps[:, f], ACT.Relu, bias=b1[:, f:f + 1]).then_inc(h_ready, 1)

            def step(t, k, i2, first=False, last=False):
                for f in range(2):
                    relu(t, f)
                if not last:
                    root(0, t + 1)
                for f in range(2, FB):
                    relu(t, f)
                if not first:
                    read_turn2(t - 1, 1 - k, i2)
                if not last:
                    read_turn1(t + 1, 1 - k)
                root(1, t)

            root(0, 0)
            read_turn1(0, 0)
            step(0, 0, 0, first=True)
            with act.Fori(0, TILES // 2 - 1) as i:
                step(i * 2 + 1, 1, i)
                step(i * 2 + 2, 0, i)
            step(TILES - 1, 1, TILES // 2 - 1, last=True)
            read_turn2(TILES - 1, 1, TILES // 2 - 1)

        @block.tensor
        def _(pe):
            pe.wait_ge(consts_loaded, 7 * 16)

            def project(t, k):
                pe.wait_ge(a_ready, t + 1)
                pe.wait_ge(y_read[0], START + t)
                for c in range(CPT):
                    last = nc.tensor.matmul(wo_ps[:, c * P:(c + 1) * P], a[:, k, c * P:(c + 1) * P], wo[:], start=True, stop=True)
                last.then_inc(wo_done, 1)

            def turn(s, t, k):
                pe.wait_ge(normed[s], t + 1)
                pe.wait_ge((x1t_ready, x2t_ready)[s], t)
                for c in range(CPT):
                    last = nc.tensor.transpose((turn1_ps, turn2_ps)[s][:, c * P:(c + 1) * P], (x1, x2)[s][:, k, c], ident[:])
                last.then_inc(turned[s], 1)

            def step(t, k, first=False, last=False):
                if not last:
                    project(t + 1, 1 - k)
                pe.wait_ge(x1t_ready, t + 1)
                for f in range(FB):
                    pe.wait_ge(h_ready, t * FB)
                    nc.tensor.matmul(h_ps[:, f], w1[:, f * P:(f + 1) * P], x1t[:, k], start=True, stop=True).then_inc(h_done, 1)
                if not first:
                    turn(1, t - 1, 1 - k)
                pe.wait_ge(h_ready, t * FB + FB)
                pe.wait_ge(y_read[1], START + t)
                for c in range(CPT):
                    for f in range(FB):
                        prod = nc.tensor.matmul(y_ps[:, c * P:(c + 1) * P], h[:, f, c * P:(c + 1) * P], w2[:, f],
                                                start=(f == 0), stop=(f == FB - 1))
                prod.then_inc(y_done, 1)
                if not last:
                    turn(0, t + 1, 1 - k)

            project(0, 0)
            turn(0, 0, 0)
            step(0, 0, first=True)
            with pe.Fori(0, TILES // 2 - 1) as i:
                step(i * 2 + 1, 1)
                step(i * 2 + 2, 0)
            step(TILES - 1, 1, last=True)
            turn(1, TILES - 1, 1)

        @block.vector
        def _(dve):
            CHAIN = 2
            dve.wait_ge(sums_loaded, 16)
            nc.vector.reciprocal(sums[:], sums[:]).then_inc(sums_inverted, 1)

            def norm(s, t, k, nth, i2):
                product, base, y, out = ((wo_done, xb_ready, y1, x1), (y_done, x1b_ready, y2, x2))[s]
                chained = Count(nth * CHAIN)
                dve.wait_ge(product, t + 1)
                dve.wait_ge(base, t + 1)
                nc.vector.tensor_tensor(y[:], (wo_ps, y_ps)[s][:].rearrange("p (c d) -> p c d", c=CPT),
                                        (xb, x1b)[s][:, k], ALU.add).then_inc(y_read[s], 1)
                dve.wait_ge(y_read[s], START + t + 1)
                norm_stats(nc.vector, y, stats[s], mean_var[s], chain, chained, stats_ready[s], passed)
                dve.wait_ge(deviation_ready[s], t + 1)
                if s == 1:
                    dve.wait_ge(stored[k], START + i2 * 16)
                norm_apply(nc.vector, y, out[:, k], deviation[s][:], inverse[s][:], mean_var[s], chain, chained, normed[s])

            norm(0, 0, 0, 0, 0)

            def step(t, k, i2, last=False):
                if not last:
                    norm(0, t + 1, 1 - k, t * 2 + 1, None)
                norm(1, t, k, t * 2 + 2 - (1 if last else 0), i2)

            step(0, 0, 0)
            with dve.Fori(0, TILES // 2 - 1) as i:
                step(i * 2 + 1, 1, i)
                step(i * 2 + 2, 0, i + 1)
            step(TILES - 1, 1, TILES // 2 - 1, last=True)


def retain(nc, io, scr):
    RW = RHEADS * DIM
    HB = N // DIM
    with ExitStack() as ctx:
        def sb(name, shape, dt=F32):
            return ctx.enter_context(nc.sbuf_tensor(name, shape, dt))

        def sem(name):
            return ctx.enter_context(nc.semaphore(name))

        pair = [ctx.enter_context(nc.psum_tensor(f"d_pair{n}", [P, RHEADS, DIM], F32)) for n in range(3)]
        out_ps = ctx.enter_context(nc.psum_tensor("d_out_ps", [P, N], F32))
        w = sb("d_w", [P, 3, RW])
        cos, sin = sb("d_cos", [P, CPB, ROPE_DIM]), sb("d_sin", [P, CPB, ROPE_DIM])
        ident, mask, decay, keep = sb("d_ident", [P, P]), sb("d_mask", [P, P]), sb("d_decay", [P, 2]), sb("d_keep", [P, CPB])
        xt = sb("d_xt", [P, 2, P])
        by_cos, by_sin = sb("d_by_cos", [P, 2, RHEADS, ROPE_DIM]), sb("d_by_sin", [P, 2, RHEADS, ROPE_DIM])
        turned = sb("d_turned", [P, 2, RHEADS, ROPE_DIM])
        qkv = sb("d_qkv", [P, 3, 2, RHEADS, DIM])
        qd = sb("d_qd", [P, RHEADS, DIM])
        qkt = sb("d_qkt", [P, 2, RHEADS, P])
        am = sb("d_am", [P, RHEADS, P])
        state = sb("d_state", [P, RHEADS, DIM])
        ret = sb("d_ret", [P, 2, P])

        consts_loaded = sem("d_consts_loaded")
        x_loaded = [sem(f"d_x_loaded{k}") for k in range(2)]
        projected = [sem(f"d_projected{z}") for z in range(3)]
        roped = [sem(f"d_roped{z}") for z in range(2)]
        rotated = [sem(f"d_rotated{z}") for z in range(2)]
        silu_done = [sem(f"d_silu_done{z}") for z in range(3)]
        qd_ready = sem("d_qd_ready")
        flipped = [sem(f"d_flipped{z}") for z in range(2)]
        flip_read = [sem(f"d_flip_read{z}") for z in range(2)]
        a_done, a_masked = sem("d_a_done"), sem("d_a_masked")
        out_done, out_read = sem("d_out_done"), sem("d_out_read")
        gain_done, state_ready = sem("d_gain_done"), sem("d_state_ready")
        stored = [sem(f"d_stored{k}") for k in range(2)]
        passed = sem("d_passed")
        block = ctx.enter_context(nc.Block())

        def chunks(engine, chunk):
            with engine.Fori(0, BATCH) as b:
                for k in range(2):
                    chunk(b, k, b * CPB + k, k, b * (CPB // 2))
                with engine.Fori(1, CPB // 2) as i:
                    for k in range(2):
                        chunk(b, i * 2 + k, b * CPB + i * 2 + k, k, b * (CPB // 2) + i)

        def place(c):
            return slice(c, c + 1) if isinstance(c, int) else bass.ds(c, 1)

        def tokens(b, c):
            return bass.ds(b * SEQ + (CPB - 1) * P - c * P, P)

        @block.sync
        def _(sp):
            def chunk(b, c, n, k, half):
                wait_apart(sp, projected[2], START + (n - 1 if k else n), passed)
                sp.dma_start(xt[:, k], scr["x2T"][:, tokens(b, c)]).then_inc(x_loaded[k], 16)

            chunks(sp, chunk)

        @block.gpsimd
        def _(pool):
            for primed in (*stored, *projected, *flip_read, a_masked, out_read):
                pool.sem_inc(primed, START)
            nc.gpsimd.memset(state[:], 0.0).then_inc(state_ready, 1)

            def chunk(b, c, n, k, half):
                for z in range(2):
                    pool.wait_ge(roped[z], n + 1)
                    e, o = slice(0, ROPE_DIM // 2), slice(ROPE_DIM // 2, ROPE_DIM)
                    nc.gpsimd.tensor_tensor(turned[:, z, :, e], by_cos[:, z, :, e], by_sin[:, z, :, o], ALU.add)
                    nc.gpsimd.tensor_tensor(turned[:, z, :, o], by_cos[:, z, :, o], by_sin[:, z, :, e],
                                            ALU.add).then_inc(rotated[z], 1)

            chunks(pool, chunk)

        @block.scalar
        def _(act):
            act.dma_start(w[:], io["wqkv"]).then_inc(consts_loaded, 16)
            for t, name in ((cos, "cos1"), (sin, "sin1"), (ident, "ident"), (mask, "mask"), (decay, "decay"), (keep, "keep")):
                act.dma_start(t[:], io[name]).then_inc(consts_loaded, 16)

            def chunk(b, c, n, k, half):
                for z in range(2):
                    act.wait_ge(roped[z], n + 1)
                    nc.scalar.activation(qkv[:, z, k, :, ROPE_DIM:], pair[z][:, :, ROPE_DIM:], ACT.Silu)
                    act.wait_ge(rotated[z], n + 1)
                    nc.scalar.activation(qkv[:, z, k, :, 0:ROPE_DIM], turned[:, z], ACT.Silu).then_inc(silu_done[z], 1)
                act.wait_ge(projected[2], START + n + 1)
                nc.scalar.activation(qkv[:, 2, k], pair[2][:], ACT.Silu).then_inc(silu_done[2], 1)
                for z in range(2):
                    act.wait_ge(flipped[z], n + 1)
                    nc.scalar.activation(qkt[:, z], pair[z][:], ACT.Copy).then_inc(flip_read[z], 1)
                act.wait_ge(out_done, n + 1)
                act.wait_ge(stored[k], START + half * 16)
                nc.scalar.activation(ret[:, k], out_ps[:, 0:P], ACT.Copy, scale=decay[:, 1:2]).then_inc(out_read, 1)
                act.wait_ge(out_read, START + n + 1)
                act.dma_start(scr["ret"][tokens(b, c)], ret[:, k]).then_inc(stored[k], 16)

            chunks(act, chunk)
            for k in range(2):
                act.wait_ge(stored[k], START + CHUNKS // 2 * 16)

        @block.vector
        def _(dve):
            dve.wait_ge(consts_loaded, 7 * 16)

            def chunk(b, c, n, k, half):
                for z in range(2):
                    dve.wait_ge(projected[z], START + n + 1)
                    angles = [t[:, place(c)].broadcast_to([P, RHEADS, ROPE_DIM]) for t in (cos, sin)]
                    nc.vector.tensor_tensor(by_cos[:, z], pair[z][:, :, 0:ROPE_DIM], angles[0], ALU.mult)
                    nc.vector.tensor_tensor(by_sin[:, z], pair[z][:, :, 0:ROPE_DIM], angles[1], ALU.mult).then_inc(roped[z], 1)
                dve.wait_ge(silu_done[0], n + 1)
                nc.vector.tensor_scalar(qd[:], qkv[:, 0, k], decay[:, 0:1], None, ALU.mult).then_inc(qd_ready, 1)
                dve.wait_ge(a_done, n + 1)
                nc.vector.tensor_tensor(am[:], pair[2][:], mask[:].unsqueeze(1).broadcast_to([P, RHEADS, P]),
                                        ALU.mult).then_inc(a_masked, 1)
                dve.wait_ge(gain_done, n + 1)
                dve.wait_ge(state_ready, n + 1)
                nc.vector.scalar_tensor_tensor(out=state[:].rearrange("p h v -> p (h v)"), in0=state[:].rearrange("p h v -> p (h v)"),
                                               scalar=keep[:, place(c)], in1=pair[0][:].rearrange("p h v -> p (h v)"),
                                               op0=ALU.mult, op1=ALU.add).then_inc(state_ready, 1)

            chunks(dve, chunk)

        @block.tensor
        def _(pe):
            pe.wait_ge(consts_loaded, 7 * 16)

            def chunk(b, c, n, k, half):
                pe.wait_ge(x_loaded[k], half * 16 + 16)
                for z in range(3):
                    if z == 0:
                        pe.wait_ge(state_ready, n + 1)
                    elif z == 1:
                        pe.wait_ge(flip_read[1], START + n)
                    else:
                        pe.wait_ge(a_masked, START + n)
                    for g in range(RHEADS // HB):
                        last = nc.tensor.matmul(pair[z][:, g * HB:(g + 1) * HB].rearrange("p h v -> p (h v)"), xt[:, k],
                                                w[:, z, g * N:(g + 1) * N], start=True, stop=True)
                    last.then_inc(projected[z], 1)
                for z in range(2):
                    pe.wait_ge(silu_done[z], n + 1)
                    for h in range(RHEADS):
                        last = nc.tensor.transpose(pair[z][:, h], qkv[:, z, k, h], ident[:])
                    last.then_inc(flipped[z], 1)
                pe.wait_ge(silu_done[2], n + 1)
                for z in range(2):
                    pe.wait_ge(flip_read[z], START + n + 1)
                for h in range(RHEADS):
                    last = nc.tensor.matmul(pair[2][:, h], qkt[:, 0, h], qkt[:, 1, h], start=True, stop=True)
                last.then_inc(a_done, 1)
                pe.wait_ge(out_read, START + n)
                first = isinstance(c, int) and c == 0
                if not first:
                    for h in range(RHEADS):
                        nc.tensor.matmul(out_ps[:, 0:P], qkt[:, 1, h], state[:, h], start=(h == 0), stop=False)
                pe.wait_ge(a_masked, START + n + 1)
                for h in range(RHEADS):
                    last = nc.tensor.matmul(out_ps[:, 0:P], am[:, h], qkv[:, 2, k, h], start=(first and h == 0), stop=(h == RHEADS - 1))
                last.then_inc(out_done, 1)
                pe.wait_ge(qd_ready, n + 1)
                for h in range(RHEADS):
                    last = nc.tensor.matmul(pair[0][:, h], qd[:, h], qkv[:, 2, k, h], start=True, stop=True)
                last.then_inc(gain_done, 1)

            chunks(pe, chunk)


def group_norm(nc, io, scr, x3, xc):
    with ExitStack() as ctx:
        def sb(name, shape, dt=F32):
            return ctx.enter_context(nc.sbuf_tensor(name, shape, dt))

        def sem(name):
            return ctx.enter_context(nc.semaphore(name))

        r, x2 = sb("e_r", [P, CHUNKS, DIM]), sb("e_x2", [P, CHUNKS, DIM])
        gw, gb, eps = sb("e_gw", [P, DIM]), sb("e_gb", [P, DIM]), sb("e_eps", [P, 1])
        G = CPB * GN
        means, sums = sb("e_means", [P, G]), sb("e_sums", [P, G])
        centred, squares, scaled, x2b = (sb(f"e_{n}", [P, CPB, DIM]) for n in ("centred", "squares", "scaled", "x2b"))
        weighted, y = sb("e_weighted", [P, CPB, DIM]), sb("e_y", [P, CPB, DIM])
        squared, deviation, inverse = (sb(f"e_{n}", [P, G]) for n in ("squared", "deviation", "inverse"))
        stats, mean_var = sb("e_stats", [P, CPB, 6]), sb("e_mean_var", [P, CPB, 2])
        spread, shrink = sb("e_spread", [P, CPB]), sb("e_shrink", [P, CPB])

        loaded, eps_set = sem("e_loaded"), sem("e_eps_set")
        means_ready, centred_ready, squares_ready = sem("e_means_ready"), sem("e_centred_ready"), sem("e_squares_ready")
        squared_ready, deviation_ready = sem("e_squared_ready"), sem("e_deviation_ready")
        scaled_ready, weighted_ready, base_ready = sem("e_scaled_ready"), sem("e_weighted_ready"), sem("e_base_ready")
        stats_ready, spread_ready, chain = sem("e_stats_ready"), sem("e_spread_ready"), sem("e_chain")
        x3_ready, copied = sem("e_x3_ready"), sem("e_copied")
        passed = sem("e_passed")
        block = ctx.enter_context(nc.Block())

        @block.sync
        def _(sp):
            sp.dma_start(r[:], scr["ret"].rearrange("(c p) d -> p c d", p=P)).then_inc(loaded, 16)
            sp.dma_start(x2[:], scr["x2"].rearrange("(c p) d -> p c d", p=P)).then_inc(loaded, 16)
            sp.dma_start(gw[:], io["gn_w"]).then_inc(loaded, 16)
            sp.dma_start(gb[:], io["gn_b"]).then_inc(loaded, 16)

        def groups(t):
            return t.rearrange("p c (g w) -> p (c g) w", w=GW)

        @block.gpsimd
        def _(pool):
            for primed in (x3_ready,):
                pool.sem_inc(primed, START)
            nc.gpsimd.memset(eps[:], EPS).then_inc(eps_set, 1)
            pool.wait_ge(loaded, 64)
            with pool.Fori(0, BATCH) as b:
                at = bass.ds(b * CPB, CPB)
                pool.wait_ge(x3_ready, START + b)
                nc.gpsimd.tensor_tensor(x2b[:], x2[:, at], gb[:].unsqueeze(1).broadcast_to([P, CPB, DIM]), ALU.add).then_inc(base_ready, 1)
                pool.wait_ge(means_ready, b + 1)
                nc.gpsimd.tensor_tensor(groups(centred[:]), groups(r[:, at]), means[:].unsqueeze(2).broadcast_to([P, G, GW]),
                                        ALU.subtract).then_inc(centred_ready, 1)
                pool.wait_ge(scaled_ready, b + 1)
                nc.gpsimd.tensor_tensor(weighted[:], scaled[:], gw[:].unsqueeze(1).broadcast_to([P, CPB, DIM]), ALU.mult).then_inc(weighted_ready, 1)

        @block.scalar
        def _(act):
            act.wait_ge(eps_set, 1)
            with act.Fori(0, BATCH) as b:
                act.wait_ge(centred_ready, b + 1)
                nc.scalar.activation(squares[:], centred[:], ACT.Square).then_inc(squares_ready, 1)
                act.wait_ge(squared_ready, b + 1)
                nc.scalar.activation(deviation[:], squared[:], ACT.Sqrt, scale=1.0 / GW, bias=eps[:, 0:1]).then_inc(deviation_ready, 1)
                act.wait_ge(stats_ready, b + 1)
                nc.scalar.activation(spread[:], mean_var[:, :, 1], ACT.Sqrt, bias=eps[:, 0:1]).then_inc(spread_ready, 1)
                act.wait_ge(x3_ready, START + b + 1)
                nc.scalar.activation(xc[:, bass.ds(b * CPB, CPB)], x3[:, bass.ds(b * CPB, CPB)], ACT.Copy).then_inc(copied, 1)

        @block.vector
        def _(dve):
            CHAIN = 5
            dve.wait_ge(loaded, 64)
            with dve.Fori(0, BATCH) as b:
                at = bass.ds(b * CPB, CPB)
                chained = Count(b * CHAIN)
                nc.vector.tensor_reduce(sums[:], groups(r[:, at]), AX.X, ALU.add).then_inc(chain, 1)
                dve.wait_ge(chain, chained.next())
                nc.vector.tensor_scalar(means[:], sums[:], 1.0 / GW, None, ALU.mult).then_inc(means_ready, 1)
                dve.wait_ge(squares_ready, b + 1)
                nc.vector.tensor_reduce(squared[:], groups(squares[:]), AX.X, ALU.add).then_inc(squared_ready, 1)
                dve.wait_ge(deviation_ready, b + 1)
                nc.vector.reciprocal(inverse[:], deviation[:]).then_inc(chain, 1)
                dve.wait_ge(chain, chained.next())
                nc.vector.tensor_tensor(groups(scaled[:]), groups(centred[:]), inverse[:].unsqueeze(2).broadcast_to([P, G, GW]),
                                        ALU.mult).then_inc(scaled_ready, 1)
                dve.wait_ge(base_ready, b + 1)
                dve.wait_ge(weighted_ready, b + 1)
                nc.vector.tensor_tensor(y[:], weighted[:], x2b[:], ALU.add).then_inc(chain, 1)
                dve.wait_ge(chain, chained.next())
                for c in range(CPB):
                    last = nc.vector.bn_stats(stats[:, c], y[:, c])
                last.then_inc(chain, 1)
                wait_apart(dve, chain, chained.next(), passed)
                for c in range(CPB):
                    last = nc.vector.bn_aggr(mean_var[:, c], stats[:, c])
                last.then_inc(stats_ready, 1)
                dve.wait_ge(spread_ready, b + 1)
                nc.vector.reciprocal(shrink[:], spread[:]).then_inc(chain, 1)
                dve.wait_ge(chain, chained.next())
                for c in range(CPB):
                    last = nc.vector.tensor_scalar(x3[:, bass.ds(b * CPB + c, 1)], y[:, c:c + 1], mean_var[:, c, 0:1],
                                                   shrink[:, c:c + 1], ALU.subtract, ALU.mult)
                last.then_inc(x3_ready, 1)


def couple(nc, io, x3, xc):
    SETS = TILES // 4
    with ExitStack() as ctx:
        def sb(name, shape, dt=F32):
            return ctx.enter_context(nc.sbuf_tensor(name, shape, dt))

        def sem(name):
            return ctx.enter_context(nc.semaphore(name))

        def psum(name, shape):
            return ctx.enter_context(nc.psum_tensor(name, shape, F32))

        turn_ps, l1_ps, l2_ps = psum("f_turn_ps", [P, 2, N]), psum("f_l1_ps", [P, 2, N]), psum("f_l2_ps", [P, 2, N])
        l3_ps, l4_ps = psum("f_l3_ps", [P, N]), psum("f_l4_ps", [P, N])
        ident, mean, sign, cb = sb("f_ident", [P, P]), sb("f_mean", [P, 1]), sb("f_sign", [P, 4]), sb("f_cb", [P, 6])
        w1, w2, w3, w4 = sb("f_w1", [P, P]), sb("f_w2", [P, 64]), sb("f_w3", [P, 64]), sb("f_w4", [P, 4])
        gw1, gw2, gw3 = sb("f_gw1", [P, 64]), sb("f_gw2", [64, 32]), sb("f_gw3", [32, P])
        gb1, gb2 = sb("f_gb1", [64, 1]), sb("f_gb2", [32, 1])
        half_b = sb("f_half_b", [P, 2])
        ranges = sb("f_ranges", [P, 2])
        ctx_sb, g1s, g2s, tanh_g = sb("f_ctx", [P, BATCH]), sb("f_g1s", [64, BATCH]), sb("f_g2s", [32, BATCH]), sb("f_tanh_g", [P, BATCH])
        by_batch, base = sb("f_by_batch", [P, BATCH]), sb("f_base", [P, SETS, CPT, 4])
        xt, g1, g2, g3 = sb("f_xt", [P, 2, N]), sb("f_g1", [P, 2, N]), sb("f_g2", [P, 2, N]), sb("f_g3", [P, N])
        tanh_t, coupling, signed = sb("f_tanh_t", [P, SETS, CPT, 4]), sb("f_coupling", [P, CPT, 4]), sb("f_signed", [P, 4, CPT, 4])
        twisted = sb("f_twisted", [P, 16, 4, 32])

        loaded, small_ready = sem("f_loaded"), sem("f_small_ready")
        mean_done, ctx_ready, global_done, global_read = sem("f_mean_done"), sem("f_ctx_ready"), sem("f_global_done"), sem("f_global_read")
        chain, base_ready = sem("f_chain"), sem("f_base_ready")
        turned, turn_read = sem("f_turned"), sem("f_turn_read")
        l1_done, l2_done, l3_done, l4_done = (sem(f"f_l{n}_done") for n in range(1, 5))
        g1_ready, g2_ready, g3_ready, tanh_ready = (sem(f"f_{n}_ready") for n in ("g1", "g2", "g3", "tanh"))
        signed_ready, twist_ready, updated = sem("f_signed_ready"), sem("f_twist_ready"), sem("f_updated")
        CONSTS = 13
        passed = sem("f_passed")
        block = ctx.enter_context(nc.Block())

        @block.sync
        def _(sp):
            for t, name in ((ident, "ident"), (mean, "mean"), (sign, "sign"), (cb, "cb"), (w1, "cw1"), (w2, "cw2"), (w3, "cw3"),
                            (w4, "cw4"), (gw1, "gw1"), (gw2, "gw2"), (gw3, "gw3"), (gb1, "gb1"), (gb2, "gb2")):
                sp.dma_start(t[:], io[name]).then_inc(loaded, 16)

        def groups(t):
            return t.rearrange("p c (g w) -> p c g w", g=4)

        @block.gpsimd
        def _(pool):
            for primed in (updated, turn_read, g1_ready, g2_ready, g3_ready, tanh_ready, l1_done):
                pool.sem_inc(primed, START)
            with pool.Fori(0, CYCLES) as cycle:
                for s in range(SETS):
                    pool.wait_ge(signed_ready, cycle * SETS + s + 1)
                    old = groups(xc[:, s * 16:(s + 1) * 16])
                    nc.gpsimd.tensor_tensor(twisted[:, :, 2:4], old[:, :, 0:2],
                                            signed[:].rearrange("p q c g -> p (q c) g")[:, :, 2:4].unsqueeze(3).broadcast_to([P, 16, 2, 32]),
                                            ALU.mult).then_inc(twist_ready, 1)

        @block.scalar
        def _(act):
            act.wait_ge(small_ready, 1)
            act.wait_ge(global_done, 1)
            nc.scalar.activation(g1s[:], l1_ps[0:64, 0, 0:BATCH], ACT.Gelu, bias=gb1[:, 0:1]).then_inc(global_read, 1)
            act.wait_ge(global_done, 2)
            nc.scalar.activation(g2s[:], l2_ps[0:32, 0, 0:BATCH], ACT.Gelu, bias=gb2[:, 0:1]).then_inc(global_read, 1)
            act.wait_ge(global_done, 3)
            nc.scalar.activation(tanh_g[:], l3_ps[:, 0:BATCH], ACT.Tanh, scale=0.5, bias=half_b[:, 1:2]).then_inc(global_read, 1)
            with act.Fori(0, CYCLES) as cycle:
                for s in range(SETS):
                    def gelu1(q):
                        n = s * 4 + q
                        act.wait_ge(l1_done, START + cycle * TILES + n + 1)
                        nc.scalar.activation(g1[:, q % 2], l1_ps[:, q % 2], ACT.Gelu, bias=cb[:, 0:1]).then_inc(g1_ready, 1)

                    def gelu2(pair):
                        act.wait_ge(l2_done, cycle * TILES + s * 4 + pair * 2 + 2)
                        nc.scalar.activation(g2[:, pair], l2_ps[:, pair], ACT.Gelu, bias=cb[:, 1:2]).then_inc(g2_ready, 1)

                    for q in range(4):
                        gelu1(q)
                        if q == 2:
                            gelu2(0)
                    gelu2(1)
                    act.wait_ge(l3_done, cycle * (SETS * 2) + s * 2 + 2)
                    nc.scalar.activation(g3[:], l3_ps[:], ACT.Gelu, bias=cb[:, 2:3]).then_inc(g3_ready, 1)
                    act.wait_ge(l4_done, cycle * SETS + s + 1)
                    nc.scalar.activation(tanh_t[:, s].rearrange("p c q -> p (c q)"), l4_ps[:, 0:16], ACT.Tanh, scale=0.5,
                                         bias=half_b[:, 0:1]).then_inc(tanh_ready, 1)

        @block.tensor
        def _(pe):
            pe.wait_ge(loaded, CONSTS * 16)
            for b in range(BATCH):
                for c in range(CPB):
                    last = nc.tensor.matmul(turn_ps[:, 0, b:b + 1], x3[:, b * CPB + c], mean[:], start=(c == 0), stop=(c == CPB - 1))
            last.then_inc(mean_done, 1)
            pe.wait_ge(ctx_ready, 1)
            nc.tensor.matmul(l1_ps[0:64, 0, 0:BATCH], gw1[:], ctx_sb[:], start=True, stop=True).then_inc(global_done, 1)
            pe.wait_ge(global_read, 1)
            nc.tensor.matmul(l2_ps[0:32, 0, 0:BATCH], gw2[:], g1s[:], start=True, stop=True).then_inc(global_done, 1)
            pe.wait_ge(global_read, 2)
            nc.tensor.matmul(l3_ps[:, 0:BATCH], gw3[:], g2s[:], start=True, stop=True).then_inc(global_done, 1)
            pe.wait_ge(global_read, 3)
            with pe.Fori(0, CYCLES) as cycle:
                for s in range(SETS):
                    def turn(q):
                        n = s * 4 + q
                        if q == 0:
                            pe.wait_ge(updated, START + cycle * SETS)
                        pe.wait_ge(turn_read, START + cycle * TILES + max(n - 1, 0))
                        for c in range(CPT):
                            last = nc.tensor.transpose(turn_ps[:, q % 2, c * P:(c + 1) * P], xc[:, n * CPT + c], ident[:])
                        last.then_inc(turned, 1)

                    def layer1(q):
                        n = s * 4 + q
                        pe.wait_ge(turn_read, START + cycle * TILES + n + 1)
                        pe.wait_ge(g1_ready, START + cycle * TILES + max(n - 1, 0))
                        nc.tensor.matmul(l1_ps[:, q % 2], w1[:], xt[:, q % 2], start=True, stop=True).then_inc(l1_done, 1)

                    def layer2(q):
                        n = s * 4 + q
                        pe.wait_ge(g1_ready, START + cycle * TILES + n + 1)
                        pe.wait_ge(g2_ready, START + cycle * (SETS * 2) + s * 2)
                        half = slice(64 * (q % 2), 64 * (q % 2) + 64)
                        nc.tensor.matmul(l2_ps[half, q // 2], w2[:], g1[:, q % 2], start=True, stop=True).then_inc(l2_done, 1)

                    def layer3(pair):
                        pe.wait_ge(g2_ready, START + cycle * (SETS * 2) + s * 2 + pair + 1)
                        pe.wait_ge(g3_ready, START + cycle * SETS + s)
                        nc.tensor.matmul(l3_ps[64 * pair:64 * pair + 64], w3[:], g2[:, pair], start=True, stop=True).then_inc(l3_done, 1)

                    turn(0)
                    turn(1)
                    layer1(0)
                    layer1(1)
                    turn(2)
                    layer2(0)
                    layer1(2)
                    layer2(1)
                    turn(3)
                    layer1(3)
                    layer3(0)
                    layer2(2)
                    layer2(3)
                    layer3(1)
                    pe.wait_ge(g3_ready, START + cycle * SETS + s + 1)
                    pe.wait_ge(tanh_ready, START + cycle * SETS + s)
                    for c in range(CPT):
                        last = nc.tensor.matmul(l4_ps[:, c * 4:c * 4 + 4], g3[:, c * P:(c + 1) * P], w4[:], start=True, stop=True)
                    last.then_inc(l4_done, 1)

        @block.vector
        def _(dve):
            dve.wait_ge(loaded, CONSTS * 16)
            nc.vector.tensor_scalar(half_b[:], cb[:, 3:5], 0.5, None, ALU.mult)
            nc.vector.tensor_scalar(ranges[:, 0:1], cb[:, 5:6], 0.3, None, ALU.mult)
            nc.vector.tensor_scalar(ranges[:, 1:2], cb[:, 5:6], 0.7, None, ALU.mult).then_inc(small_ready, 1)
            dve.wait_ge(mean_done, 1)
            nc.vector.tensor_copy(ctx_sb[:], turn_ps[:, 0, 0:BATCH]).then_inc(ctx_ready, 1)
            dve.wait_ge(global_read, 3)
            dve.wait_ge(small_ready, 1)
            nc.vector.tensor_scalar(by_batch[:], tanh_g[:], ranges[:, 1:2], BASE_COUPLING, ALU.mult, ALU.add).then_inc(base_ready, 1)
            dve.wait_ge(base_ready, 1)
            for s in range(SETS):
                last = nc.vector.tensor_copy(base[:, s].rearrange("p c (b q) -> p c b q", b=2),
                                             by_batch[:, 2 * s:2 * s + 2].unsqueeze(1).unsqueeze(3).broadcast_to([P, CPT, 2, 2]))
            last.then_inc(base_ready, 1)
            dve.wait_ge(base_ready, 2)
            CHAIN = 2
            with dve.Fori(0, CYCLES) as cycle:
                for s in range(SETS):
                    chained = Count(cycle * (SETS * CHAIN) + s * CHAIN)
                    for q in range(4):
                        n = s * 4 + q
                        dve.wait_ge(turned, cycle * TILES + n + 1)
                        dve.wait_ge(l1_done, START + cycle * TILES + max(n - 1, 0))
                        nc.vector.tensor_copy(xt[:, q % 2], turn_ps[:, q % 2]).then_inc(turn_read, 1)
                    dve.wait_ge(tanh_ready, START + cycle * SETS + s + 1)
                    nc.vector.scalar_tensor_tensor(out=coupling[:], in0=tanh_t[:, s], scalar=ranges[:, 0:1], in1=base[:, s],
                                                   op0=ALU.mult, op1=ALU.add).then_inc(chain, 1)
                    dve.wait_ge(chain, chained.next())
                    nc.vector.tensor_tensor(signed[:], coupling[:].rearrange("p c q -> p q c").unsqueeze(3).broadcast_to([P, 4, CPT, 4]),
                                            sign[:].unsqueeze(1).unsqueeze(1).broadcast_to([P, 4, CPT, 4]), ALU.mult).then_inc(signed_ready, 1)
                    dve.wait_ge(signed_ready, cycle * SETS + s + 1)
                    old = groups(xc[:, s * 16:(s + 1) * 16])
                    nc.vector.tensor_tensor(twisted[:, :, 0:2], old[:, :, 2:4],
                                            signed[:].rearrange("p q c g -> p (q c) g")[:, :, 0:2].unsqueeze(3).broadcast_to([P, 16, 2, 32]),
                                            ALU.mult).then_inc(chain, 1)
                    dve.wait_ge(chain, chained.next())
                    dve.wait_ge(twist_ready, cycle * SETS + s + 1)
                    nc.vector.tensor_tensor(xc[:, s * 16:(s + 1) * 16], xc[:, s * 16:(s + 1) * 16],
                                            twisted[:].rearrange("p c g w -> p c (g w)"), ALU.add).then_inc(updated, 1)


def last_norm(nc, x3, xc, out):
    with ExitStack() as ctx:
        def sb(name, shape, dt=F32):
            return ctx.enter_context(nc.sbuf_tensor(name, shape, dt))

        def sem(name):
            return ctx.enter_context(nc.semaphore(name))

        y, normed = sb("g_y", [P, 2, CPT, DIM]), sb("g_normed", [P, 2, CPT, DIM])
        stats, mean_var, eps = sb("g_stats", [P, CPT, 6]), sb("g_mean_var", [P, CPT, 2]), sb("g_eps", [P, 1])
        deviation, inverse = sb("g_deviation", [P, CPT]), sb("g_inverse", [P, CPT])
        eps_set, y_ready, chain, stats_ready = sem("g_eps_set"), sem("g_y_ready"), sem("g_chain"), sem("g_stats_ready")
        deviation_ready, done = sem("g_deviation_ready"), sem("g_done")
        stored = [sem(f"g_stored{k}") for k in range(2)]
        passed = sem("g_passed")
        block = ctx.enter_context(nc.Block())

        @block.sync
        def _(sp):
            with sp.Fori(0, TILES // 2) as i:
                for k in range(2):
                    wait_apart(sp, done, START + i * 2 + k + 1, passed)
                    sp.dma_start(out[bass.ds((i * 2 + k) * N, N)].rearrange("(c p) d -> p c d", p=P), normed[:, k]).then_inc(stored[k], 16)
            for k in range(2):
                sp.wait_ge(stored[k], START + TILES // 2 * 16)

        @block.gpsimd
        def _(pool):
            for primed in (done, *stored):
                pool.sem_inc(primed, START)
            nc.gpsimd.memset(eps[:], EPS).then_inc(eps_set, 1)
            with pool.Fori(0, TILES // 2) as i:
                for k in range(2):
                    at = bass.ds((i * 2 + k) * CPT, CPT)
                    pool.wait_ge(done, START + i * 2)
                    nc.gpsimd.tensor_tensor(y[:, k], x3[:, at], xc[:, at], ALU.add).then_inc(y_ready, 1)

        @block.scalar
        def _(act):
            act.wait_ge(eps_set, 1)
            with act.Fori(0, TILES) as t:
                act.wait_ge(stats_ready, t + 1)
                nc.scalar.activation(deviation[:], mean_var[:, :, 1], ACT.Sqrt, bias=eps[:, 0:1]).then_inc(deviation_ready, 1)

        @block.vector
        def _(dve):
            with dve.Fori(0, TILES // 2) as i:
                for k in range(2):
                    t = i * 2 + k
                    chained = Count(t * 2)
                    dve.wait_ge(y_ready, t + 1)
                    norm_stats(nc.vector, y[:, k], stats, mean_var, chain, chained, stats_ready, passed)
                    dve.wait_ge(deviation_ready, t + 1)
                    dve.wait_ge(stored[k], START + i * 16)
                    norm_apply(nc.vector, y[:, k], normed[:, k], deviation[:], inverse[:], mean_var, chain, chained, done)


def scratch(nc):
    def dram(name, shape, dt=F32):
        return nc.dram_tensor(f"scratch_{name}", shape, dt, kind="Internal").ap()

    return {
        "parts": [dram(f"parts{z}", (PARTS, DIM, TOKENS), BF16) for z in range(2)],
        "vals": dram("vals", (TOKENS, HEADS * VW)),
        "o": dram("o", (DIM, TOKENS)),
        "z": dram("z", (HEADS, TOKENS)),
        "rz": dram("rz", (HEADS, TOKENS)),
        "x2": dram("x2", (TOKENS, DIM)),
        "x2T": dram("x2T", (DIM, TOKENS)),
        "ret": dram("ret", (TOKENS, DIM)),
    }


def build(nc, io, out):
    scr = scratch(nc)
    project_and_split(nc, io, scr)
    attend(nc, io, scr)
    project_out_and_ffn(nc, io, scr)
    retain(nc, io, scr)
    with ExitStack() as ctx:
        x3 = ctx.enter_context(nc.sbuf_tensor("x3", [P, CHUNKS, DIM], F32))
        xc = ctx.enter_context(nc.sbuf_tensor("xc", [P, CHUNKS, DIM], F32))
        group_norm(nc, io, scr, x3, xc)
        couple(nc, io, x3, xc)
        last_norm(nc, x3, xc, out)


def _layout(x):
    import numpy as _np

    f = _np.float32
    a = {k: _np.asarray(v) for k, v in x.items()}
    col = lambda v: _np.ascontiguousarray(v.reshape(-1, 1))
    arrays = {"x": a["L0_attn_x"].reshape(TOKENS, DIM)}
    arrays["xT"] = _np.ascontiguousarray(arrays["x"].T)
    other = _np.arange(DIM).reshape(HEADS, 2, HD // 2)[:, ::-1].reshape(-1)
    wq, wk, wv = a["L0_attn_wq"], a["L0_attn_wk"], a["L0_attn_wv"]
    arrays["w0"] = _np.stack([wq.T, wq[other].T, wk.T, wk[other].T, wv.T], 1)
    bq, bk = a["L0_attn_bq"], a["L0_attn_bk"]
    arrays["bias0"] = _np.stack([bq, bq[other], bk, bk[other]], 1)
    arrays["bv"] = _np.tile(a["L0_attn_bv"], (P, CPT))
    theta = f(10000.0) ** (f(-2.0) * _np.arange(HD // 2, dtype=f) / f(HD))
    angle = _np.repeat(_np.arange(SEQ, dtype=f)[:, None] * theta[None, :], 2, -1).T
    sign = _np.where(_np.arange(HD) < HD // 2, -1, 1)[:, None]
    arrays["cos0"] = _np.tile(_np.cos(angle), (HEADS, 1)).astype(f)
    arrays["sin0"] = _np.tile(_np.sin(angle) * sign, (HEADS, 1)).astype(f)
    arrays["ident"] = _np.eye(P, dtype=f)
    arrays["woT"] = _np.ascontiguousarray(a["L0_attn_wo"].T)
    arrays["bo"] = _np.tile(a["L0_attn_bo"], (P, CPT))
    arrays["w1"] = a["L0_ffn_W1"]
    arrays["b1"] = _np.ascontiguousarray(a["L0_ffn_b1"].reshape(INTER // P, P).T)
    arrays["w2"] = _np.ascontiguousarray(a["L0_ffn_W2"].reshape(INTER // P, P, DIM).transpose(1, 0, 2))
    arrays["b2"] = _np.tile(a["L0_ffn_b2"], (P, CPT))
    order = _np.concatenate([_np.arange(0, ROPE_DIM, 2), _np.arange(1, ROPE_DIM, 2), _np.arange(ROPE_DIM, DIM)])
    heads = (_np.arange(RHEADS)[:, None] * DIM + order).reshape(-1)
    arrays["wqkv"] = _np.stack([a["L1_attn_W_Q"][:, heads], a["L1_attn_W_K"][:, heads], a["L1_attn_W_V"]], 1)
    inv = f(1.0) / f(10000.0) ** (_np.arange(0, ROPE_DIM, 2, dtype=f) / f(ROPE_DIM))
    angle = _np.arange(SEQ, dtype=f)[:, None] * inv[None, :]
    turn = lambda v: _np.ascontiguousarray(v.reshape(CPB, P, ROPE_DIM)[::-1].transpose(1, 0, 2).astype(f))
    arrays["cos1"] = turn(_np.concatenate([_np.cos(angle)] * 2, -1))
    arrays["sin1"] = turn(_np.concatenate([_np.sin(angle), -_np.sin(angle)], -1))
    n = _np.arange(P)
    arrays["mask"] = _np.where(n[:, None] >= n[None, :], GAMMA ** (n[:, None] - float(P)), 0.0).astype(f)
    arrays["decay"] = _np.stack([GAMMA ** n.astype(_np.float64), GAMMA ** (P - n.astype(_np.float64))], 1).astype(f)
    keep = _np.full((P, CPB), GAMMA ** float(P))
    keep[:, 0] = 0.0
    arrays["keep"] = keep.astype(f)
    arrays["gn_w"] = _np.tile(a["L1_attn_gn_weight"], (P, 1))
    arrays["gn_b"] = _np.tile(a["L1_attn_gn_bias"], (P, 1))
    arrays["cw1"] = a["L1_ffn_cn_w1"]
    arrays["cw2"] = a["L1_ffn_cn_w2"]
    w3, w4 = a["L1_ffn_cn_w3"], a["L1_ffn_cn_w4"]
    blocks = _np.zeros((P, 64), f)
    blocks[:64, :32] = w3
    blocks[64:, 32:] = w3
    arrays["cw3"] = blocks
    blocks = _np.zeros((P, 4), f)
    for q in range(4):
        blocks[32 * q:32 * q + 32, q:q + 1] = w4
    arrays["cw4"] = blocks
    arrays["cb"] = _np.stack([a["L1_ffn_cn_b1"], _np.tile(a["L1_ffn_cn_b2"], 2), _np.tile(a["L1_ffn_cn_b3"], 4),
                              _np.tile(a["L1_ffn_cn_b4"], P), _np.tile(a["L1_ffn_gc_b3"], P),
                              _np.tile(a["L1_ffn_adaptive_range"], P)], 1)
    arrays["gw1"] = a["L1_ffn_gc_w1"]
    arrays["gw2"] = a["L1_ffn_gc_w2"]
    arrays["gw3"] = _np.tile(a["L1_ffn_gc_w3"], (1, P))
    arrays["gb1"] = col(a["L1_ffn_gc_b1"])
    arrays["gb2"] = col(a["L1_ffn_gc_b2"])
    arrays["mean"] = _np.full((P, 1), 1.0 / SEQ, f)
    arrays["sign"] = _np.tile(_np.array([1, -1, -1, 1], f), (P, 1))
    return {k: _np.ascontiguousarray(v) for k, v in arrays.items()}


def kernel(**inputs):
    import concourse.bacc as _bacc
    from concourse import mybir as _mybir
    from concourse.bass_utils import run_bass_kernel_spmd as _run

    nc = _bacc.Bacc("TRN2", target_bir_lowering=False, num_devices=1)
    arrays = {f"in_{k}": v for k, v in _layout(inputs).items()}
    io = {k[3:]: nc.dram_tensor(k, v.shape, _mybir.dt.from_np(v.dtype), kind="ExternalInput").ap()
          for k, v in arrays.items()}
    out = nc.dram_tensor("out", (TOKENS, DIM), F32, kind="ExternalOutput").ap()
    build(nc, io, out)
    r = _run(nc, [arrays], core_ids=[0])
    return r.results[0]["out"].reshape(BATCH, SEQ, DIM)
```

```python
from contextlib import ExitStack

import numpy as np

import concourse.bass as bass
from concourse import mybir

F32 = mybir.dt.float32
BF16 = mybir.dt.bfloat16
ALU = mybir.AluOpType
ACT = mybir.ActivationFunctionType
AX = mybir.AxisListType

BATCH, SEQ, DIM = 4, 1024, 128
TOKENS = BATCH * SEQ
P = 128
N = 512
CPT = N // P
TILES = TOKENS // N
CHUNKS = TOKENS // P
CPB = SEQ // P
EPS = 1e-5
START = 1

HEADS, HD = 16, 8
GH = 4
GROUPS = HEADS // GH
PARTS = 3
TERM_ROWS = PARTS * PARTS * HD
LOADS = PARTS * PARTS + PARTS + 1
TWO_ONES = 1.0019378662109375
MAX_ROWS = 96
SHIFT_ROWS = MAX_ROWS + PARTS
VW = HD + 1
INTER = 512

RHEADS = 8
ROPE_DIM = 64
GAMMA = 0.96875
GN = 16
GW = DIM // GN
BASE_COUPLING = 0.1
CYCLES = 3


class Count:

    def __init__(self, base=0):
        self.base, self.n = base, 0

    def next(self):
        self.n += 1
        return self.base + self.n


def wait_apart(engine, sem, value, passed):
    engine.wait_ge(sem, value)
    engine.sem_inc(passed, 1)


def load_group(sp, scr, held, tokens, j, loaded):
    heads = slice(j * GH, (j + 1) * GH) if isinstance(j, int) else bass.ds(j * GH, GH)
    group = j if isinstance(j, int) else bass.ds(j, 1)
    by_row = [scr["parts"][z].rearrange("(r h) t -> r h t", h=HEADS)[:, heads, tokens] for z in range(2)]
    for i in range(PARTS):
        for m in range(PARTS):
            at = (PARTS * i + m) * HD
            sp.dma_start(held["q"][at:at + HD, group], by_row[0][i * HD:(i + 1) * HD]).then_inc(loaded, 16)
        at = PARTS * i * HD
        sp.dma_start(held["k"][at:at + PARTS * HD, group], by_row[1]).then_inc(loaded, 16)
    columns = slice(j * GH * VW, (j + 1) * GH * VW) if isinstance(j, int) else bass.ds(j * (GH * VW), GH * VW)
    sp.dma_start(held["v"][:, group], scr["vals"][tokens, columns].rearrange("(k p) w -> p k w", p=P)).then_inc(loaded, 16)


def project_and_split(nc, io, scr, held):
    with ExitStack() as ctx:
        def sb(name, shape, dt=F32):
            return ctx.enter_context(nc.sbuf_tensor(name, shape, dt))

        def sem(name):
            return ctx.enter_context(nc.semaphore(name))

        ps = ctx.enter_context(nc.psum_tensor("a_ps", [P, 5, N], F32))
        w = sb("a_w", [P, 5, P])
        bias = sb("a_bias", [P, 4])
        bv = sb("a_bv", [P, N])
        cos, sin = sb("a_cos", [P, SEQ]), sb("a_sin", [P, SEQ])
        xt = sb("a_xt", [P, 2, N])
        cos_part, sin_part = sb("a_cos_part", [P, 2, N]), sb("a_sin_part", [P, 2, N])
        turned, rest = sb("a_turned", [P, 2, N]), sb("a_rest", [P, 2, N])
        parts = sb("a_parts", [P, 2, 2, PARTS, N], BF16)
        vals = sb("a_vals", [P, 2, CPT, HEADS, VW])

        consts_loaded = sem("a_consts_loaded")
        x_loaded = [sem(f"a_x_loaded{k}") for k in range(2)]
        projected = [sem(f"a_projected{z}") for z in range(2)]
        v_projected = sem("a_v_projected")
        v_read = sem("a_v_read")
        ones_set = sem("a_ones_set")
        angled = [sem(f"a_angled{z}") for z in range(2)]
        turned_ready = [sem(f"a_turned_ready{z}") for z in range(2)]
        high_ready = [sem(f"a_high_ready{z}") for z in range(2)]
        rest_ready = [sem(f"a_rest_ready{z}") for z in range(2)]
        mid_ready = [sem(f"a_mid_ready{z}") for z in range(2)]
        low_ready = [sem(f"a_low_ready{z}") for z in range(2)]
        parts_stored = [[sem(f"a_parts_stored{z}{k}") for k in range(2)] for z in range(2)]
        vals_stored = [sem(f"a_vals_stored{k}") for k in range(2)]
        rows_set, group_loaded = sem("a_rows_set"), sem("a_group_loaded")
        passed = sem("a_passed")
        block = ctx.enter_context(nc.Block())

        @block.sync
        def _(sp):
            for k in range(2):
                sp.dma_start(xt[:, k], io["xT"][:, k * N:(k + 1) * N]).then_inc(x_loaded[k], 16)

            def store(i):
                for k in range(2):
                    for z in range(2):
                        sp.wait_ge(mid_ready[z], i * 2 + k + 1)
                        wait_apart(sp, low_ready[z], i * 2 + k + 1, passed)
                        sp.dma_start(scr["parts"][z].rearrange("(s p) t -> p s t", p=DIM)[:, :, bass.ds(i * (2 * N) + k * N, N)],
                                     parts[:, z, k]).then_inc(parts_stored[z][k], 16)
                    wait_apart(sp, v_read, START + i * 2 + k + 1, passed)
                    sp.dma_start(scr["vals"].rearrange("(t c p) w -> t p c w", c=CPT, p=P)[i * 2 + k],
                                 vals[:, k].rearrange("p c h w -> p c (h w)")).then_inc(vals_stored[k], 16)

            store(0)
            sp.wait_ge(rows_set, 2)
            for k in range(2):
                sp.wait_ge(vals_stored[k], START + 16)
                for z in range(2):
                    sp.wait_ge(parts_stored[z][k], START + 16)
            load_group(sp, scr, held, slice(0, SEQ), 0, group_loaded)
            with sp.Fori(1, TILES // 2) as i:
                store(i)
                load_group(sp, scr, held, slice(0, SEQ), i, group_loaded)
            sp.wait_ge(group_loaded, GROUPS * LOADS * 16)
            for k in range(2):
                sp.wait_ge(vals_stored[k], START + 16 * TILES // 2)
                for z in range(2):
                    sp.wait_ge(parts_stored[z][k], START + 16 * TILES // 2)

        @block.gpsimd
        def _(pool):
            for primed in (*angled, v_read, *(s for pair in parts_stored for s in pair), *vals_stored):
                pool.sem_inc(primed, START)
            nc.gpsimd.memset(vals[:], 1.0).then_inc(ones_set, 1)
            nc.gpsimd.memset(held["k"][:].bitcast(F32), TWO_ONES).then_inc(rows_set, 1)
            with pool.Fori(0, TILES // 2) as i:
                for k in range(2):
                    for z in range(2):
                        pool.wait_ge(angled[z], START + i * 2 + k + 1)
                        nc.gpsimd.tensor_tensor(turned[:, z], cos_part[:, z], sin_part[:, z],
                                                ALU.add).then_inc(turned_ready[z], 1)
                    for z in range(2):
                        pool.wait_ge(mid_ready[z], i * 2 + k + 1)
                        nc.gpsimd.tensor_tensor(parts[:, z, k, 2], rest[:, z], parts[:, z, k, 1],
                                                ALU.subtract).then_inc(low_ready[z], 1)

        @block.scalar
        def _(act):
            for t, name in ((w, "w0"), (bias, "bias0"), (cos, "cos0"), (sin, "sin0"), (bv, "bv"), (held["ident"], "ident")):
                act.dma_start(t[:], io[name]).then_inc(consts_loaded, 16)

            def pair(i, last):
                for k in range(2):
                    for z in range(2):
                        act.wait_ge(turned_ready[z], i * 2 + k + 1)
                        act.wait_ge(parts_stored[z][k], START + i * 16)
                        nc.scalar.activation(parts[:, z, k, 0], turned[:, z], ACT.Copy).then_inc(high_ready[z], 1)
                    for z in range(2):
                        act.wait_ge(rest_ready[z], i * 2 + k + 1)
                        nc.scalar.activation(parts[:, z, k, 1], rest[:, z], ACT.Copy).then_inc(mid_ready[z], 1)
                    if not last:
                        act.wait_ge(v_projected, i * 2 + k + 1)
                        act.dma_start(xt[:, k], io["xT"][:, bass.ds((i + 1) * (2 * N) + k * N, N)]).then_inc(x_loaded[k], 16)

            with act.Fori(0, TILES // 2 - 1) as i:
                pair(i, False)
            pair(TILES // 2 - 1, True)

        @block.tensor
        def _(pe):
            pe.wait_ge(consts_loaded, 6 * 16)
            with pe.Fori(0, TILES // 2) as i:
                for k in range(2):
                    pe.wait_ge(x_loaded[k], i * 16 + 16)
                    for z in range(2):
                        pe.wait_ge(angled[z], START + i * 2 + k)
                        nc.tensor.matmul(ps[:, 2 * z], w[:, 2 * z], xt[:, k], start=True, stop=True)
                        nc.tensor.matmul(ps[:, 2 * z + 1], w[:, 2 * z + 1], xt[:, k],
                                         start=True, stop=True).then_inc(projected[z], 1)
                    pe.wait_ge(v_read, START + i * 2 + k)
                    for c in range(CPT):
                        last = nc.tensor.matmul(ps[:, 4, c * P:(c + 1) * P], xt[:, k, c * P:(c + 1) * P], w[:, 4],
                                                start=True, stop=True)
                    last.then_inc(v_projected, 1)

        @block.vector
        def _(dve):
            nc.vector.memset(held["q"][P // 2:P].bitcast(F32), 0.0).then_inc(rows_set, 1)
            dve.wait_ge(consts_loaded, 6 * 16)
            dve.wait_ge(ones_set, 1)
            with dve.Fori(0, TILES // 2) as i:
                for k in range(2):
                    at = slice(k * N, (k + 1) * N)
                    for z in range(2):
                        dve.wait_ge(projected[z], i * 2 + k + 1)
                        nc.vector.scalar_tensor_tensor(out=cos_part[:, z], in0=ps[:, 2 * z], scalar=bias[:, 2 * z:2 * z + 1],
                                                       in1=cos[:, at], op0=ALU.add, op1=ALU.mult)
                        nc.vector.scalar_tensor_tensor(out=sin_part[:, z], in0=ps[:, 2 * z + 1],
                                                       scalar=bias[:, 2 * z + 1:2 * z + 2], in1=sin[:, at],
                                                       op0=ALU.add, op1=ALU.mult).then_inc(angled[z], 1)
                    dve.wait_ge(v_projected, i * 2 + k + 1)
                    dve.wait_ge(vals_stored[k], START + i * 16)
                    nc.vector.tensor_tensor(vals[:, k, :, :, 0:HD], ps[:, 4].rearrange("p (c h d) -> p c h d", c=CPT, d=HD),
                                            bv[:].rearrange("p (c h d) -> p c h d", c=CPT, d=HD), ALU.add).then_inc(v_read, 1)
                    for z in range(2):
                        dve.wait_ge(high_ready[z], i * 2 + k + 1)
                        nc.vector.tensor_tensor(rest[:, z], turned[:, z], parts[:, z, k, 0],
                                                ALU.subtract).then_inc(rest_ready[z], 1)


def attend(nc, io, scr, held):
    LEAD = 5
    QBLOCKS = SEQ // P
    HALVES = SEQ // N
    PER_HEAD = QBLOCKS * HALVES
    BANKS = 3
    PROBS = 8
    ITEMS = HEADS * PER_HEAD + GROUPS
    LEAD_ITEMS = LEAD * PER_HEAD + 1
    TILES_B = HEADS * PER_HEAD
    LATER = 4
    SPLIT_STEPS = 4
    STORES = GH * 2 * 16
    with ExitStack() as ctx:
        def sb(name, shape, dt=F32):
            return ctx.enter_context(nc.sbuf_tensor(name, shape, dt))

        def sem(name):
            return ctx.enter_context(nc.semaphore(name))

        max_ps = ctx.enter_context(nc.psum_tensor("b_max_ps", [P, BANKS, N], F32))
        score_ps = ctx.enter_context(nc.psum_tensor("b_score_ps", [P, BANKS, N], F32))
        out_ps = ctx.enter_context(nc.psum_tensor("b_out_ps", [P, HALVES, N], F32))
        q, k_, v, identf = held["q"], held["k"], held["v"], held["ident"]
        ident = sb("b_ident", [P, P], BF16)
        sums = sb("b_sums", [P, (BATCH - 1) * SEQ * HEADS // P])
        probs = sb("b_probs", [P, PROBS, N])
        half_max = sb("b_half_max", [P, GROUPS, GH, QBLOCKS, HALVES])
        full_max, mid_rest, low_rest = (sb(f"b_{n}", [P, GH, QBLOCKS]) for n in ("full_max", "mid_rest", "low_rest"))
        shift = sb("b_shift", [P, QBLOCKS, GH, PARTS], BF16)
        shift_t = sb("b_shift_t", [GH * PARTS, 2, SEQ], BF16)
        outs = sb("b_outs", [P, 2, HALVES, N])

        ident_ready, consts_loaded = sem("b_ident_ready"), sem("b_consts_loaded")
        sums_loaded, sums_inverted, inverses_stored = sem("b_sums_loaded"), sem("b_sums_inverted"), sem("b_inverses_stored")
        operands_loaded = [sem(f"b_operands_loaded{j}") for j in range(GROUPS)]
        shift_loaded = [sem(f"b_shift_loaded{j}") for j in range(GROUPS)]
        max_scored = sem("b_max_scored")
        max_read = sem("b_max_read")
        chain = sem("b_chain")
        shift_ready = sem("b_shift_ready")
        scored = sem("b_scored")
        probs_ready = sem("b_probs_ready")
        probs_used = sem("b_probs_used")
        out_read = sem("b_out_read")
        outs_stored = [sem(f"b_outs_stored{g}") for g in range(2)]
        passed = sem("b_passed")
        block = ctx.enter_context(nc.Block())

        def tokens(b):
            return slice(b * SEQ, (b + 1) * SEQ) if isinstance(b, int) else bass.ds(b * SEQ, SEQ)

        def items(first, last):
            out = []
            turn = None
            for head in range(first, last):
                for t in range(PER_HEAD):
                    if turn is not None and t == LATER:
                        out.append(("turn", turn, 0))
                        turn = None
                    out.append(("tile", head, t))
                if head % GH == GH - 1:
                    turn = head // GH % GROUPS
            if turn is not None:
                out.append(("turn", turn, 0))
            return out

        @block.sync
        def _(sp):
            later = [name for name in held if name in io and name != "ident"]
            for name in later:
                sp.dma_start(held[name][:], io[name]).then_inc(consts_loaded, 16)
            early = (BATCH - 1) * SEQ

            def batch(b, last):
                if last:
                    for g in range(2):
                        sp.wait_ge(outs_stored[g], START + (BATCH - 1) * 2 * STORES)
                    sp.dma_start(sums[:], scr["z"][:, 0:early].rearrange("h (a t) -> h a t", a=P // HEADS)).then_inc(sums_loaded, 16)
                for j in range(GROUPS):
                    if last and j == GROUPS - 1:
                        sp.wait_ge(sums_inverted, 1)
                        sp.dma_start(scr["rz"][:, 0:early].rearrange("h (a t) -> h a t", a=P // HEADS),
                                     sums[:]).then_inc(inverses_stored, 16)
                    wait_apart(sp, out_read, b * (GROUPS * HALVES) + HALVES * (j + 1) + HALVES, passed)
                    rows = outs[:, j % 2].rearrange("p a n -> p (a n)")
                    at = tokens(b)
                    for h in range(GH):
                        head = j * GH + h
                        sp.dma_start(scr["o"][head * HD:(head + 1) * HD, at], rows[32 * h:32 * h + HD]).then_inc(outs_stored[j % 2], 16)
                        sp.dma_start(scr["z"][head:head + 1, at], rows[32 * h + HD:32 * h + HD + 1]).then_inc(outs_stored[j % 2], 16)
                    if not last:
                        load_group(sp, scr, held, tokens(b + 1), j, operands_loaded[j])

            with sp.Fori(0, BATCH - 1) as b:
                batch(b, False)
            batch(BATCH - 1, True)
            for g in range(2):
                sp.wait_ge(outs_stored[g], START + BATCH * GROUPS // 2 * GH * 2 * 16)
            sp.wait_ge(inverses_stored, 16)
            sp.wait_ge(consts_loaded, len(later) * 16)

        @block.gpsimd
        def _(pool):
            for primed in (probs_used, *outs_stored, probs_ready, *operands_loaded):
                pool.sem_inc(primed, START)
            def move_shift(count, j):
                wait_apart(pool, max_read, count, passed)
                for h in range(GH):
                    pool.dma_start(q[MAX_ROWS:SHIFT_ROWS, j, h], shift_t[PARTS * h:PARTS * (h + 1), j % 2]).then_inc(shift_loaded[j], 16)

            for n, (kind, a, _) in enumerate(items(0, LEAD)):
                if kind == "turn":
                    move_shift(n + 1, a)

            def batch(b, last):
                for n, (kind, a, _) in enumerate(items(LEAD, last)):
                    if kind == "turn":
                        move_shift(b * ITEMS + LEAD_ITEMS + n + 1, a)

            with pool.Fori(0, BATCH - 1) as b:
                batch(b, HEADS + LEAD)
            batch(BATCH - 1, HEADS)
            for j in range(GROUPS):
                pool.wait_ge(shift_loaded[j], BATCH * GH * 16)

        @block.scalar
        def _(act):
            def read_out(b, j):
                for half in range(HALVES):
                    step = PER_HEAD - HALVES + half
                    act.wait_ge(probs_used, START + b * TILES_B + (j * PER_HEAD + step + 1) * GH)
                    act.wait_ge(outs_stored[j % 2], START + (b * (2 * STORES) + (STORES if j >= 2 else 0)))
                    nc.scalar.activation(outs[:, j % 2, half], out_ps[:, half], ACT.Copy).then_inc(out_read, 1)

            with act.Fori(0, BATCH) as b:
                for j in range(GROUPS):
                    for step in range(PER_HEAD):
                        for h in range(GH):
                            n = (j * PER_HEAD + step) * GH + h
                            act.wait_ge(scored, b * TILES_B + n + 1)
                            act.wait_ge(probs_used, START + b * TILES_B + max(n - PROBS + 1, 0))
                            nc.scalar.activation(probs[:, n % PROBS], score_ps[:, n % BANKS], ACT.Exp,
                                                 scale=float(1.0 / np.sqrt(np.float32(HD)))).then_inc(probs_ready, 1)
                        if step == 0 and j > 0:
                            read_out(b, j - 1)
                read_out(b, GROUPS - 1)

        @block.vector
        def _(dve):
            for half in range(HALVES):
                nc.vector.memset(out_ps[:, half], 0.0).then_inc(out_read, 1)
            nc.vector.tensor_copy(ident[:], identf[:]).then_inc(ident_ready, 1)

            def split(group, read, splits):
                chained = Count(splits * SPLIT_STEPS)
                part = [shift[:, :, :, s].rearrange("p q h -> p h q") for s in range(PARTS)]
                dve.wait_ge(max_read, read)
                nc.vector.tensor_tensor(full_max[:], half_max[:, group, :, :, 0], half_max[:, group, :, :, 1],
                                        ALU.max).then_inc(chain, 1)
                dve.wait_ge(chain, chained.next())
                nc.vector.tensor_scalar(part[0], full_max[:], -1.0, None, ALU.mult).then_inc(chain, 1)
                dve.wait_ge(chain, chained.next())
                nc.vector.scalar_tensor_tensor(out=mid_rest[:], in0=full_max[:], scalar=-1.0, in1=part[0],
                                               op0=ALU.mult, op1=ALU.subtract).then_inc(chain, 1)
                dve.wait_ge(chain, chained.next())
                nc.vector.tensor_copy(part[1], mid_rest[:]).then_inc(chain, 1)
                dve.wait_ge(chain, chained.next())
                nc.vector.tensor_tensor(part[2], mid_rest[:], part[1], ALU.subtract).then_inc(shift_ready, 1)

            def read_items(todo, base, splits):
                for n, (kind, a, t) in enumerate(todo):
                    dve.wait_ge(max_scored, base + n + 1)
                    if kind == "tile":
                        group = a // GH % GROUPS
                        nc.vector.tensor_reduce(half_max[:, group, a % GH, t // HALVES, t % HALVES:t % HALVES + 1],
                                                max_ps[:, n % BANKS], AX.X, ALU.max).then_inc(max_read, 1)
                        if a % GH == GH - 1 and t == PER_HEAD - 1:
                            split(group, base + n + 1, splits)
                            splits = splits + 1
                    else:
                        nc.vector.tensor_copy(shift_t[:, a % 2],
                                              max_ps[0:GH * PARTS, n % BANKS].bitcast(BF16)).then_inc(max_read, 1)

            read_items(items(0, LEAD), 0, 0)

            def batch(b, last):
                read_items(items(LEAD, last), b * ITEMS + LEAD_ITEMS, b * GROUPS + 1)

            with dve.Fori(0, BATCH - 1) as b:
                batch(b, HEADS + LEAD)
            batch(BATCH - 1, HEADS)
            dve.wait_ge(sums_loaded, 16)
            nc.vector.reciprocal(sums[:], sums[:]).then_inc(sums_inverted, 1)

        @block.tensor
        def _(pe):
            pe.wait_ge(ident_ready, 1)

            def max_item(item, n, base, loaded, splits):
                kind, a, t = item
                if n >= BANKS:
                    pe.wait_ge(max_read, base + (n - BANKS + 1))
                else:
                    pe.wait_ge(max_read, base)
                if kind == "tile":
                    group, h = a // GH % GROUPS, a % GH
                    qb, half = t // HALVES, t % HALVES
                    if t == 0 and h == 0 and loaded is not None:
                        pe.wait_ge(operands_loaded[group], loaded(a))
                    nc.tensor.matmul(max_ps[:, n % BANKS], q[0:MAX_ROWS, group, h, qb * P:(qb + 1) * P],
                                     k_[0:MAX_ROWS, group, h, half * N:(half + 1) * N],
                                     start=True, stop=True).then_inc(max_scored, 1)
                else:
                    pe.wait_ge(shift_ready, splits)
                    for qb in range(QBLOCKS):
                        last = nc.tensor.transpose(max_ps[0:GH * PARTS, n % BANKS].bitcast(BF16)[:, qb * P:(qb + 1) * P],
                                                   shift[:, qb].rearrange("p h s -> p (h s)"), ident[:])
                    last.then_inc(max_scored, 1)

            for n, item in enumerate(items(0, LEAD)):
                max_item(item, n, 0, None, 1)

            def apply(b, j, step):
                kb, half = step // HALVES, step % HALVES
                if kb == 0:
                    pe.wait_ge(out_read, b * (GROUPS * HALVES) + j * HALVES + half + 1)
                for h in range(GH):
                    n = (j * PER_HEAD + step) * GH + h
                    pe.wait_ge(probs_ready, START + b * TILES_B + n + 1)
                    nc.tensor.matmul(out_ps[32 * h:32 * h + VW, half], v[:, j, kb, h * VW:(h + 1) * VW],
                                     probs[:, n % PROBS], start=(kb == 0), stop=(kb == QBLOCKS - 1)).then_inc(probs_used, 1)

            def batch(b, last):
                todo = items(LEAD, last)
                base = b * ITEMS + LEAD_ITEMS
                splits = 1
                done = 0
                for j in range(GROUPS):
                    pe.wait_ge(shift_loaded[j], b * (GH * 16) + GH * 16)
                    for step in range(PER_HEAD):
                        kb, half = step // HALVES, step % HALVES
                        for h in range(GH):
                            n = (j * PER_HEAD + step) * GH + h
                            pe.wait_ge(probs_ready, START + b * TILES_B + max(n - BANKS + 1, 0))
                            nc.tensor.matmul(score_ps[:, n % BANKS], k_[0:SHIFT_ROWS, j, h, kb * P:(kb + 1) * P],
                                             q[0:SHIFT_ROWS, j, h, half * N:(half + 1) * N],
                                             start=True, stop=True).then_inc(scored, 1)
                            for item in todo[done:done + (2 if todo[done:done + 1] and todo[done][0] == "turn" else 1)]:
                                splits += item[0] == "turn"
                                max_item(item, done, base,
                                         lambda head: START + b * (LOADS * 16) + (0 if head < HEADS else LOADS * 16),
                                         b * GROUPS + splits)
                                done += 1
                        if step > 0:
                            apply(b, j, step - 1)
                        elif j > 0:
                            apply(b, j - 1, PER_HEAD - 1)
                apply(b, GROUPS - 1, PER_HEAD - 1)
                assert done == len(todo)

            with pe.Fori(0, BATCH - 1) as b:
                batch(b, HEADS + LEAD)
            batch(BATCH - 1, HEADS)


def norm_stats(dve, y, stats, mean_var, chain, chained, done, passed):
    for c in range(CPT):
        last = dve.bn_stats(stats[:, c], y[:, c])
    last.then_inc(chain, 1)
    wait_apart(dve, chain, chained.next(), passed)
    for c in range(CPT):
        last = dve.bn_aggr(mean_var[:, c], stats[:, c])
    last.then_inc(done, 1)


def norm_apply(dve, y, out, deviation, inverse, mean_var, chain, chained, done):
    dve.reciprocal(inverse, deviation).then_inc(chain, 1)
    dve.wait_ge(chain, chained.next())
    for c in range(CPT):
        last = dve.tensor_scalar(out(c), y[:, c:c + 1], mean_var[:, c, 0:1], inverse[:, c:c + 1],
                                 ALU.subtract, ALU.mult)
    last.then_inc(done, 1)


def project_out_and_ffn(nc, io, scr, held):
    FB = INTER // P
    with ExitStack() as ctx:
        def sb(name, shape, dt=F32):
            return ctx.enter_context(nc.sbuf_tensor(name, shape, dt))

        def sem(name):
            return ctx.enter_context(nc.semaphore(name))

        wo_ps, y_ps, turn1_ps, turn2_ps = (ctx.enter_context(nc.psum_tensor(f"c_{n}", [P, N], F32))
                                           for n in ("wo_ps", "y_ps", "turn1_ps", "turn2_ps"))
        h_ps = ctx.enter_context(nc.psum_tensor("c_h_ps", [P, FB, N], F32))
        ident, wo, w1, b1, w2 = (held[n] for n in ("ident", "woT", "w1", "b1", "w2"))
        bo, b2 = (held[n][:].rearrange("p (c d) -> p c d", c=CPT) for n in ("bo", "b2"))
        x2b, x2t, gb = held["x2b"], held["x2T"], held["gn_b"]
        sums, eps = sb("c_sums", [P, HEADS * SEQ // P]), sb("c_eps", [P, 1])
        o, rz, x = sb("c_o", [P, 2, N]), sb("c_rz", [P, 2, N]), sb("c_x", [P, 2, CPT, P])
        a, xb = sb("c_a", [P, 2, N]), sb("c_xb", [P, 2, CPT, P])
        y1, x1, x1b = sb("c_y1", [P, CPT, P]), sb("c_x1", [P, 2, CPT, P]), sb("c_x1b", [P, 2, CPT, P])
        x1t, h = sb("c_x1t", [P, 2, N]), sb("c_h", [P, FB, N])
        y2, x2 = sb("c_y2", [P, CPT, P]), sb("c_x2", [P, 2, CPT, P])
        stats = [sb(f"c_stats{s}", [P, CPT, 6]) for s in range(2)]
        mean_var = [sb(f"c_mean_var{s}", [P, CPT, 2]) for s in range(2)]
        deviation = [sb(f"c_deviation{s}", [P, CPT]) for s in range(2)]
        inverse = [sb(f"c_inverse{s}", [P, CPT]) for s in range(2)]

        eps_set = sem("c_eps_set")
        sums_loaded, sums_inverted, inverses_stored = sem("c_sums_loaded"), sem("c_sums_inverted"), sem("c_inverses_stored")
        tile_loaded = [sem(f"c_tile_loaded{k}") for k in range(2)]
        a_ready, xb_ready, x1b_ready = sem("c_a_ready"), sem("c_xb_ready"), sem("c_x1b_ready")
        wo_done, h_done, y_done = sem("c_wo_done"), sem("c_h_done"), sem("c_y_done")
        turned = [sem(f"c_turned{s}") for s in range(2)]
        chain = [sem(f"c_chain{s}") for s in range(2)]
        stats_ready = [sem(f"c_stats_ready{s}") for s in range(2)]
        deviation_ready = [sem(f"c_deviation_ready{s}") for s in range(2)]
        normed = [sem(f"c_normed{s}") for s in range(2)]
        h_ready = sem("c_h_ready")
        x1t_ready, x2t_ready = sem("c_x1t_ready"), sem("c_x2t_ready")
        y_read = [sem(f"c_y_read{s}") for s in range(2)]
        x2_kept = sem("c_x2_kept")
        passed = sem("c_passed")
        block = ctx.enter_context(nc.Block())

        def tile(t):
            return slice(t * N, (t + 1) * N) if isinstance(t, int) else bass.ds(t * N, N)

        @block.sync
        def _(sp):
            late = slice((BATCH - 1) * SEQ, TOKENS)
            sp.dma_start(sums[:], scr["z"][:, late].rearrange("h (a t) -> h a t", a=P // HEADS)).then_inc(sums_loaded, 16)

            def load(t, k):
                if not (isinstance(t, int) and t < 2):
                    wait_apart(sp, xb_ready, t - 1, passed)
                sp.dma_start(o[:, k], scr["o"][:, tile(t)]).then_inc(tile_loaded[k], 16)
                sp.dma_start(rz[:, k], scr["rz"][:, tile(t)].unsqueeze(1).broadcast_to([HEADS, HD, N])).then_inc(tile_loaded[k], 16)
                sp.dma_start(x[:, k], io["x"][tile(t)].rearrange("(c p) d -> p c d", p=P)).then_inc(tile_loaded[k], 16)

            for t in range(2):
                load(t, t)
            sp.wait_ge(sums_inverted, 1)
            sp.dma_start(scr["rz"][:, late].rearrange("h (a t) -> h a t", a=P // HEADS), sums[:]).then_inc(inverses_stored, 16)
            sp.wait_ge(inverses_stored, 16)
            with sp.Fori(1, TILES // 2) as i:
                for k in range(2):
                    load(i * 2 + k, k)

        @block.gpsimd
        def _(pool):
            for primed in (*y_read, *normed, x2_kept, x1t_ready, x2t_ready):
                pool.sem_inc(primed, START)
            nc.gpsimd.memset(eps[:], EPS).then_inc(eps_set, 1)

            def scale(t, k, i):
                pool.wait_ge(tile_loaded[k], i * 48 + 48)
                if not (isinstance(t, int) and t < 2):
                    pool.wait_ge(y_read[0], START + t - 1)
                nc.gpsimd.tensor_tensor(a[:, k], o[:, k], rz[:, k], ALU.mult).then_inc(a_ready, 1)
                nc.gpsimd.tensor_tensor(xb[:, k], x[:, k], bo[:], ALU.add).then_inc(xb_ready, 1)

            def residual(t, k):
                pool.wait_ge(normed[0], START + t + 1)
                if not (isinstance(t, int) and t < 2):
                    pool.wait_ge(y_read[1], START + t - 1)
                nc.gpsimd.tensor_tensor(x1b[:, k], x1[:, k], b2[:], ALU.add).then_inc(x1b_ready, 1)

            def keep_x2(t, k):
                pool.wait_ge(normed[1], START + t + 1)
                at = slice(t * CPT, (t + 1) * CPT) if isinstance(t, int) else bass.ds(t * CPT, CPT)
                nc.gpsimd.tensor_tensor(x2b[:, at], x2[:, k], gb[:].unsqueeze(1).broadcast_to([P, CPT, DIM]), ALU.add).then_inc(x2_kept, 1)

            scale(0, 0, 0)
            scale(1, 1, 0)
            residual(0, 0)
            scale(2, 0, 1)
            residual(1, 1)
            with pool.Fori(0, TILES // 2 - 2) as i:
                scale(i * 2 + 3, 1, i + 1)
                residual(i * 2 + 2, 0)
                keep_x2(i * 2, 0)
                scale(i * 2 + 4, 0, i + 2)
                residual(i * 2 + 3, 1)
                keep_x2(i * 2 + 1, 1)
            scale(TILES - 1, 1, TILES // 2 - 1)
            residual(TILES - 2, 0)
            keep_x2(TILES - 4, 0)
            residual(TILES - 1, 1)
            for t in range(TILES - 3, TILES):
                keep_x2(t, t % 2)

        @block.scalar
        def _(act):
            act.wait_ge(eps_set, 1)

            def root(s, t):
                act.wait_ge(stats_ready[s], t + 1)
                nc.scalar.activation(deviation[s][:], mean_var[s][:, :, 1], ACT.Sqrt, bias=eps[:, 0:1]).then_inc(deviation_ready[s], 1)

            def read_turn1(t, k):
                act.wait_ge(turned[0], t + 1)
                nc.scalar.activation(x1t[:, k], turn1_ps[:], ACT.Copy).then_inc(x1t_ready, 1)

            def read_turn2(t):
                act.wait_ge(turned[1], t + 1)
                nc.scalar.activation(x2t[:, tile(t)], turn2_ps[:], ACT.Copy).then_inc(x2t_ready, 1)

            def relu(t, f):
                act.wait_ge(h_done, t * FB + f + 1)
                act.wait_ge(y_done, t)
                nc.scalar.activation(h[:, f], h_ps[:, f], ACT.Relu, bias=b1[:, f:f + 1]).then_inc(h_ready, 1)

            def step(t, k, first=False, last=False):
                relu(t, 0)
                if not first:
                    root(1, t - 1)
                relu(t, 1)
                if not last:
                    root(0, t + 1)
                for f in range(2, FB):
                    relu(t, f)
                if not last:
                    read_turn1(t + 1, 1 - k)
                if not first:
                    read_turn2(t - 1)

            root(0, 0)
            read_turn1(0, 0)
            step(0, 0, first=True)
            with act.Fori(0, TILES // 2 - 1) as i:
                step(i * 2 + 1, 1)
                step(i * 2 + 2, 0)
            step(TILES - 1, 1, last=True)
            root(1, TILES - 1)
            read_turn2(TILES - 1)

        @block.tensor
        def _(pe):
            def project(t, k):
                pe.wait_ge(a_ready, t + 1)
                pe.wait_ge(y_read[0], START + t)
                for c in range(CPT):
                    last = nc.tensor.matmul(wo_ps[:, c * P:(c + 1) * P], a[:, k, c * P:(c + 1) * P], wo[:], start=True, stop=True)
                last.then_inc(wo_done, 1)

            def turn(s, t, k):
                pe.wait_ge(normed[s], START + t + 1)
                pe.wait_ge((x1t_ready, x2t_ready)[s], START + t)
                for c in range(CPT):
                    last = nc.tensor.transpose((turn1_ps, turn2_ps)[s][:, c * P:(c + 1) * P],
                                               (x1, x2)[s][:, k, c], ident[:])
                last.then_inc(turned[s], 1)

            def step(t, k, first=False, last=False):
                if not last:
                    project(t + 1, 1 - k)
                pe.wait_ge(x1t_ready, START + t + 1)
                for f in range(FB):
                    pe.wait_ge(h_ready, t * FB)
                    nc.tensor.matmul(h_ps[:, f], w1[:, f * P:(f + 1) * P], x1t[:, k], start=True, stop=True).then_inc(h_done, 1)
                if not last:
                    turn(0, t + 1, 1 - k)
                pe.wait_ge(h_ready, t * FB + FB)
                pe.wait_ge(y_read[1], START + t)
                for c in range(CPT):
                    for f in range(FB):
                        prod = nc.tensor.matmul(y_ps[:, c * P:(c + 1) * P], h[:, f, c * P:(c + 1) * P], w2[:, f],
                                                start=(f == 0), stop=(f == FB - 1))
                prod.then_inc(y_done, 1)
                if not first:
                    turn(1, t - 1, 1 - k)

            project(0, 0)
            turn(0, 0, 0)
            step(0, 0, first=True)
            with pe.Fori(0, TILES // 2 - 1) as i:
                step(i * 2 + 1, 1)
                step(i * 2 + 2, 0)
            step(TILES - 1, 1, last=True)
            turn(1, TILES - 1, 1)

        @block.vector
        def _(dve):
            dve.wait_ge(sums_loaded, 16)
            nc.vector.reciprocal(sums[:], sums[:]).then_inc(sums_inverted, 1)

            def start(s, t, k, nth):
                product, base, y = ((wo_done, xb_ready, y1), (y_done, x1b_ready, y2))[s]
                dve.wait_ge(product, t + 1)
                dve.wait_ge(base, t + 1)
                if not (isinstance(t, int) and t == 0):
                    dve.wait_ge(normed[s], START + t)
                nc.vector.tensor_tensor(y[:], (wo_ps, y_ps)[s][:].rearrange("p (c d) -> p c d", c=CPT),
                                        (xb, x1b)[s][:, k], ALU.add).then_inc(y_read[s], 1)
                dve.wait_ge(y_read[s], START + t + 1)
                norm_stats(nc.vector, y, stats[s], mean_var[s], chain[0], Count(nth), stats_ready[s], passed)

            def finish(s, t, k, nth):
                dve.wait_ge(deviation_ready[s], t + 1)
                if s and not (isinstance(t, int) and t < 2):
                    dve.wait_ge(x2_kept, START + t - 1)
                norm_apply(nc.vector, (y1, y2)[s], lambda c: (x1, x2)[s][:, k, c:c + 1], deviation[s][:], inverse[s][:], mean_var[s],
                           chain[1], Count(nth), normed[s])

            def step(t, k, first=False, last=False):
                if not first:
                    start(1, t - 1, 1 - k, 2 * t)
                if not last:
                    start(0, t + 1, 1 - k, 1 if first else 2 * t + 1)
                    finish(0, t + 1, 1 - k, 1 if first else 2 * t)
                if not first:
                    finish(1, t - 1, 1 - k, 2 * t if last else 2 * t + 1)

            start(0, 0, 0, 0)
            finish(0, 0, 0, 0)
            step(0, 0, first=True)
            with dve.Fori(0, TILES // 2 - 1) as i:
                step(i * 2 + 1, 1)
                step(i * 2 + 2, 0)
            step(TILES - 1, 1, last=True)
            start(1, TILES - 1, 1, 2 * TILES - 1)
            finish(1, TILES - 1, 1, 2 * TILES - 1)


def retain(nc, held, r, x3, xc, chunk_sums):
    RW = RHEADS * DIM
    HB = N // DIM
    HALVES = RHEADS // HB
    ITEMS = ("a", "q", "k", "fq", "v", "fk", "g")
    BANKS = len(ITEMS)
    UPDATES = HALVES * (CPB - 1)
    with ExitStack() as ctx:
        def sb(name, shape, dt=F32):
            return ctx.enter_context(nc.sbuf_tensor(name, shape, dt))

        def sem(name):
            return ctx.enter_context(nc.semaphore(name))

        ps = ctx.enter_context(nc.psum_tensor("d_ps", [P, BANKS, HB, DIM], F32))
        out_ps = ctx.enter_context(nc.psum_tensor("d_out_ps", [P, N], F32))
        w, cos, sin, ident, mask, decay, keep = (held[n] for n in ("wqkv", "cos1", "sin1", "ident", "mask", "decay", "keep"))
        x2t = held["x2T"]
        xt = sb("d_xt", [P, 2, P])
        by_cos, by_sin = sb("d_by_cos", [P, 2, RHEADS, ROPE_DIM]), sb("d_by_sin", [P, 2, RHEADS, ROPE_DIM])
        rotated = sb("d_rotated", [P, 2, RHEADS, ROPE_DIM])
        qkv = sb("d_qkv", [P, 3, 2, RHEADS, DIM])
        qd = sb("d_qd", [P, RHEADS, DIM])
        qkt = sb("d_qkt", [P, 2, RHEADS, P])
        am = sb("d_am", [P, RHEADS, P])
        state = sb("d_state", [P, RHEADS, DIM])
        x2b, gw, eps = held["x2b"], held["gn_w"], sb("e_eps", [P, 1])
        G = CPB * GN
        means, sums = sb("e_means", [P, G]), sb("e_sums", [P, G])
        centred = sb("e_centred", [P, CPB, DIM])
        squares = sb("e_squares", [P, CPB, DIM])
        y = sb("e_y", [P, CPB, DIM])
        squared, deviation, inverse = (sb(f"e_{n}", [P, G]) for n in ("squared", "deviation", "inverse"))
        stats, mean_var = sb("e_stats", [P, CPB, 6]), sb("e_mean_var", [P, CPB, 2])
        spread, shrink = sb("e_spread", [P, CPB]), sb("e_shrink", [P, CPB])

        made = {kind: sem(f"d_made_{kind}") for kind in ITEMS}
        xt_ready = sem("d_xt_ready")
        roped = [sem(f"d_roped{z}") for z in range(2)]
        rotated_ready = [sem(f"d_rotated_ready{z}") for z in range(2)]
        passed_by = [sem(f"d_passed_by{z}") for z in range(2)]
        silu_done = [sem(f"d_silu_done{z}") for z in range(2)]
        v_ready = sem("d_v_ready")
        qd_ready = sem("d_qd_ready")
        flip_read = [sem(f"d_flip_read{z}") for z in range(2)]
        a_masked, state_ready = sem("d_a_masked"), sem("d_state_ready")
        out_done, out_read = sem("d_out_done"), sem("d_out_read")
        eps_set = sem("e_eps_set")
        means_ready, centred_ready, squares_ready = sem("e_means_ready"), sem("e_centred_ready"), sem("e_squares_ready")
        squared_ready, deviation_ready = sem("e_squared_ready"), sem("e_deviation_ready")
        scaled_ready, weighted_ready = sem("e_scaled_ready"), sem("e_weighted_ready")
        stats_ready, spread_ready, chain = sem("e_stats_ready"), sem("e_spread_ready"), sem("e_chain")
        x3_ready, copied = sem("e_x3_ready"), sem("e_copied")
        passed = sem("e_passed")
        block = ctx.enter_context(nc.Block())

        def bank(kind, half):
            return ps[:, (ITEMS.index(kind) * HALVES + half) % BANKS]

        def tokens(b, c):
            at = b * SEQ + (CPB - 1 - c) * P
            return slice(at, at + P) if isinstance(b, int) else bass.ds(at, P)

        def heads(half):
            return slice(half * HB, (half + 1) * HB)

        def span(b, at, count):
            return slice(at, at + count) if isinstance(b, int) else bass.ds(at, count)

        def groups(t):
            return t.rearrange("p c (g w) -> p (c g) w", w=GW)

        def batches(engine, batch, norm):
            batch(0, False)
            with engine.Fori(1, BATCH - 1) as b:
                batch(b, False)
            batch(BATCH - 1, True)
            for step in norm(BATCH - 1):
                step()

        @block.gpsimd
        def _(pool):
            for primed in (out_read,):
                pool.sem_inc(primed, START)
            even, odd = slice(0, ROPE_DIM // 2), slice(ROPE_DIM // 2, ROPE_DIM)

            def rotate(n):
                for z in range(2):
                    pool.wait_ge(roped[z], n * HALVES + HALVES)
                    nc.gpsimd.tensor_tensor(rotated[:, z, :, even], by_cos[:, z, :, even], by_sin[:, z, :, odd], ALU.add)
                    nc.gpsimd.tensor_tensor(rotated[:, z, :, odd], by_cos[:, z, :, odd], by_sin[:, z, :, even],
                                            ALU.add).then_inc(rotated_ready[z], 1)

            def fetch(b, c):
                nc.gpsimd.tensor_copy(xt[:, c % 2], x2t[:, tokens(b, c)]).then_inc(xt_ready, 1)

            nc.gpsimd.memset(eps[:], EPS).then_inc(eps_set, 1)
            fetch(0, 0)
            fetch(0, 1)

            def norm(b):
                at = span(b, b * CPB, CPB)

                def centre():
                    pool.wait_ge(means_ready, b + 1)
                    nc.gpsimd.tensor_tensor(groups(centred[:]), groups(r[:, at]), means[:].unsqueeze(2).broadcast_to([P, G, GW]),
                                            ALU.subtract).then_inc(centred_ready, 1)

                def weigh():
                    pool.wait_ge(scaled_ready, b + 1)
                    nc.gpsimd.tensor_tensor(y[:], squares[:], gw[:].unsqueeze(1).broadcast_to([P, CPB, DIM]),
                                            ALU.mult).then_inc(weighted_ready, 1)

                return centre, weigh

            def batch(b, last):
                centre, weigh = norm(b - 1)
                steps = {1: centre, 4: weigh} if not (isinstance(b, int) and b == 0) else {}
                for c in range(CPB):
                    n = b * CPB + c
                    rotate(n)
                    if c in steps:
                        steps[c]()
                    if not (last and c >= CPB - 2):
                        pool.wait_ge(made["v"], n * HALVES + HALVES)
                        fetch(b + (c + 2) // CPB, (c + 2) % CPB)

            batches(pool, batch, norm)

        @block.scalar
        def _(act):
            def activate(n, k, z):
                for half in range(HALVES):
                    act.wait_ge(roped[z], n * HALVES + half + 1)
                    nc.scalar.activation(qkv[:, z, k, heads(half), ROPE_DIM:], bank("qk"[z], half)[:, :, ROPE_DIM:],
                                         ACT.Silu).then_inc(passed_by[z], 1)
                act.wait_ge(rotated_ready[z], n + 1)
                nc.scalar.activation(qkv[:, z, k, :, 0:ROPE_DIM], rotated[:, z], ACT.Silu).then_inc(silu_done[z], 1)

            def read_flip(n, z):
                for half in range(HALVES):
                    act.wait_ge(made[("fq", "fk")[z]], n * HALVES + half + 1)
                    nc.scalar.activation(qkt[:, z, heads(half)], bank(("fq", "fk")[z], half), ACT.Copy).then_inc(flip_read[z], 1)

            def read_v(n, k):
                for half in range(HALVES):
                    act.wait_ge(made["v"], n * HALVES + half + 1)
                    nc.scalar.activation(qkv[:, 2, k, heads(half)], bank("v", half), ACT.Silu).then_inc(v_ready, 1)

            def norm(b):
                at = span(b, b * CPB, CPB)

                def square():
                    act.wait_ge(centred_ready, b + 1)
                    nc.scalar.activation(squares[:], centred[:], ACT.Square).then_inc(squares_ready, 1)

                def group_root():
                    act.wait_ge(squared_ready, b + 1)
                    nc.scalar.activation(deviation[:], squared[:], ACT.Sqrt, scale=1.0 / GW, bias=eps[:, 0:1]).then_inc(deviation_ready, 1)

                def root():
                    act.wait_ge(stats_ready, b + 1)
                    nc.scalar.activation(spread[:], mean_var[:, :, 1], ACT.Sqrt, bias=eps[:, 0:1]).then_inc(spread_ready, 1)

                def copy():
                    act.wait_ge(x3_ready, b + 1)
                    nc.scalar.activation(xc[:, at], x3[:, at], ACT.Copy).then_inc(copied, 1)

                return square, group_root, root, copy

            def batch(b, last):
                square, group_root, root, copy = norm(b - 1)
                steps = {1: square, 2: group_root, 4: root, 5: copy} if not (isinstance(b, int) and b == 0) else {}
                for c in range(CPB):
                    n, k = b * CPB + c, c % 2
                    ahead = not (last and c == CPB - 1)
                    if ahead:
                        activate(n + 1, 1 - k, 0)
                        activate(n + 1, 1 - k, 1)
                    act.wait_ge(out_done, n + 1)
                    nc.scalar.activation(r[:, span(b, b * CPB + (CPB - 1 - c), 1)], out_ps[:, 0:P].unsqueeze(1), ACT.Copy,
                                         scale=decay[:, 1:2]).then_inc(out_read, 1)
                    if ahead:
                        read_flip(n + 1, 0)
                        read_v(n + 1, 1 - k)
                        read_flip(n + 1, 1)
                    if c in steps:
                        steps[c]()

            act.wait_ge(eps_set, 1)
            activate(0, 0, 0)
            activate(0, 0, 1)
            read_flip(0, 0)
            read_v(0, 0)
            read_flip(0, 1)
            batches(act, batch, norm)

        @block.vector
        def _(dve):
            nc.vector.memset(state[:], 0.0).then_inc(state_ready, 1)

            def rope(n, c, z):
                for half in range(HALVES):
                    dve.wait_ge(made["qk"[z]], n * HALVES + half + 1)
                    src = bank("qk"[z], half)[:, :, 0:ROPE_DIM]
                    angles = [t[:, c:c + 1].broadcast_to([P, HB, ROPE_DIM]) for t in (cos, sin)]
                    nc.vector.tensor_tensor(by_cos[:, z, heads(half)], src, angles[0], ALU.mult)
                    nc.vector.tensor_tensor(by_sin[:, z, heads(half)], src, angles[1], ALU.mult).then_inc(roped[z], 1)

            def decay_q(n, k):
                dve.wait_ge(silu_done[0], n + 1)
                nc.vector.tensor_scalar(qd[:], qkv[:, 0, k], decay[:, 0:1], None, ALU.mult).then_inc(qd_ready, 1)

            for z in range(2):
                rope(0, 0, z)
            decay_q(0, 0)

            def norm(b):
                at = span(b, b * CPB, CPB)
                CHAIN = 5
                chained = Count(b * CHAIN)

                def mean():
                    dve.wait_ge(out_read, START + b * CPB + CPB)
                    nc.vector.tensor_reduce(sums[:], groups(r[:, at]), AX.X, ALU.add).then_inc(chain, 1)
                    dve.wait_ge(chain, chained.next())
                    nc.vector.tensor_scalar(means[:], sums[:], 1.0 / GW, None, ALU.mult).then_inc(means_ready, 1)

                def variance():
                    dve.wait_ge(squares_ready, b + 1)
                    nc.vector.tensor_reduce(squared[:], groups(squares[:]), AX.X, ALU.add).then_inc(squared_ready, 1)

                def invert():
                    dve.wait_ge(deviation_ready, b + 1)
                    nc.vector.reciprocal(inverse[:], deviation[:]).then_inc(chain, 1)
                    dve.wait_ge(chain, chained.next())
                    nc.vector.tensor_tensor(groups(squares[:]), groups(centred[:]), inverse[:].unsqueeze(2).broadcast_to([P, G, GW]),
                                            ALU.mult).then_inc(scaled_ready, 1)

                def residual():
                    dve.wait_ge(weighted_ready, b + 1)
                    nc.vector.tensor_tensor(y[:], y[:], x2b[:, at], ALU.add).then_inc(chain, 1)
                    dve.wait_ge(chain, chained.next())
                    for c in range(CPB):
                        last = nc.vector.bn_stats(stats[:, c], y[:, c])
                    last.then_inc(chain, 1)
                    wait_apart(dve, chain, chained.next(), passed)
                    for c in range(CPB):
                        last = nc.vector.bn_aggr(mean_var[:, c], stats[:, c])
                    last.then_inc(stats_ready, 1)

                def apply():
                    dve.wait_ge(spread_ready, b + 1)
                    nc.vector.reciprocal(shrink[:], spread[:]).then_inc(chain, 1)
                    dve.wait_ge(chain, chained.next())
                    for c in range(CPB):
                        last = nc.vector.tensor_scalar(x3[:, span(b, b * CPB + c, 1)], y[:, c:c + 1], mean_var[:, c, 0:1],
                                                       shrink[:, c:c + 1], ALU.subtract, ALU.mult)
                    last.then_inc(x3_ready, 1)

                def add_up():
                    dve.wait_ge(x3_ready, b + 1)
                    nc.vector.tensor_reduce(chunk_sums[:, span(b, b, 1)], x3[:, at].rearrange("p c d -> p d c"), AX.X, ALU.add)

                return mean, variance, invert, residual, apply, add_up

            def batch(b, last):
                steps = dict(zip((0, 2, 3, 4, 5, 6), norm(b - 1))) if not (isinstance(b, int) and b == 0) else {}
                for c in range(CPB):
                    n, k = b * CPB + c, c % 2
                    ahead = not (last and c == CPB - 1)
                    for half in range(HALVES):
                        dve.wait_ge(made["a"], n * HALVES + half + 1)
                        nc.vector.tensor_tensor(am[:, heads(half)], bank("a", half), mask[:].unsqueeze(1).broadcast_to([P, HB, P]),
                                                ALU.mult).then_inc(a_masked, 1)
                    if ahead:
                        for z in range(2):
                            rope(n + 1, (c + 1) % CPB, z)
                    if c in steps:
                        steps[c]()
                    for half in range(HALVES if c < CPB - 1 else 0):
                        dve.wait_ge(made["g"], b * UPDATES + (c * HALVES + half + 1))
                        dve.wait_ge(state_ready, b * UPDATES + (1 + c * HALVES))
                        flat = state[:, heads(half)].rearrange("p h v -> p (h v)")
                        nc.vector.scalar_tensor_tensor(out=flat, in0=flat, scalar=keep[:, c:c + 1],
                                                       in1=bank("g", half).rearrange("p h v -> p (h v)"),
                                                       op0=ALU.mult, op1=ALU.add).then_inc(state_ready, 1)
                    if ahead and c != CPB - 2:
                        decay_q(n + 1, 1 - k)

            batches(dve, batch, norm)

        @block.tensor
        def _(pe):
            def project(n, k, kind):
                for half in range(HALVES):
                    if kind == "q" and not (isinstance(n, int) and n == 0):
                        pe.wait_ge(v_ready, n * HALVES)
                    nc.tensor.matmul(bank(kind, half).rearrange("p h v -> p (h v)"), xt[:, k],
                                     w[:, "qkv".index(kind), half * N:(half + 1) * N], start=True, stop=True).then_inc(made[kind], 1)

            def flip(n, k, z):
                pe.wait_ge(passed_by[z], n * HALVES + HALVES)
                pe.wait_ge(silu_done[z], n + 1)
                for half in range(HALVES):
                    for h in range(HB):
                        last = nc.tensor.transpose(bank(("fq", "fk")[z], half)[:, h], qkv[:, z, k, half * HB + h], ident[:])
                    last.then_inc(made[("fq", "fk")[z]], 1)

            def products(n):
                for z in range(2):
                    pe.wait_ge(flip_read[z], n * HALVES + HALVES)
                for half in range(HALVES):
                    if half:
                        pe.wait_ge(v_ready, n * HALVES + 1)
                    for h in range(half * HB, (half + 1) * HB):
                        last = nc.tensor.matmul(bank("a", half)[:, h % HB], qkt[:, 0, h], qkt[:, 1, h], start=True, stop=True)
                    last.then_inc(made["a"], 1)

            pe.wait_ge(xt_ready, 1)
            project(0, 0, "q")
            project(0, 0, "k")
            flip(0, 0, 0)
            project(0, 0, "v")
            flip(0, 0, 1)

            def batch(b, last):
                for c in range(CPB):
                    n, k = b * CPB + c, c % 2
                    ahead = not (last and c == CPB - 1)
                    products(n)
                    if ahead:
                        pe.wait_ge(xt_ready, n + 2)
                        project(n + 1, 1 - k, "q")
                    pe.wait_ge(out_read, START + n)
                    if c:
                        pe.wait_ge(state_ready, b * UPDATES + (1 + c * HALVES))
                        for h in range(RHEADS):
                            nc.tensor.matmul(out_ps[:, 0:P], qkt[:, 1, h], state[:, h], start=(h == 0), stop=False)
                    if ahead:
                        project(n + 1, 1 - k, "k")
                    pe.wait_ge(a_masked, n * HALVES + HALVES)
                    for h in range(RHEADS):
                        prod = nc.tensor.matmul(out_ps[:, 0:P], am[:, h], qkv[:, 2, k, h],
                                                start=(c == 0 and h == 0), stop=(h == RHEADS - 1))
                    prod.then_inc(out_done, 1)
                    if ahead:
                        flip(n + 1, 1 - k, 0)
                        project(n + 1, 1 - k, "v")
                        flip(n + 1, 1 - k, 1)
                    if c < CPB - 1:
                        pe.wait_ge(qd_ready, b * (CPB - 1) + (c + 1))
                        for half in range(HALVES):
                            if half and ahead:
                                pe.wait_ge(flip_read[0], n * HALVES + (HALVES + 1))
                            for h in range(half * HB, (half + 1) * HB):
                                prod = nc.tensor.matmul(bank("g", half)[:, h % HB], qd[:, h], qkv[:, 2, k, h], start=True, stop=True)
                            prod.then_inc(made["g"], 1)

            batches(pe, batch, lambda b: ())


def couple(nc, held, x3, xc, chunk_sums, out):
    SETS = TILES // 4
    SC = CHUNKS // SETS
    with ExitStack() as ctx:
        def sb(name, shape, dt=F32):
            return ctx.enter_context(nc.sbuf_tensor(name, shape, dt))

        def sem(name):
            return ctx.enter_context(nc.semaphore(name))

        def psum(name, shape):
            return ctx.enter_context(nc.psum_tensor(name, shape, F32))

        turn_ps, l1_ps, l2_ps = psum("f_turn_ps", [P, 2, N]), psum("f_l1_ps", [P, 2, N]), psum("f_l2_ps", [P, 2, N])
        l3_ps, l4_ps = psum("f_l3_ps", [P, N]), psum("f_l4_ps", [P, N])
        mean_ps, g1_ps, g2_ps, g3_ps = (l4_ps[:, 64 + BATCH * n:64 + BATCH * (n + 1)] for n in range(4))
        ident, mean, sign, cb, w1, w2, w3, w4 = (held[n] for n in ("ident", "mean", "sign", "cb", "cw1", "cw2", "cw3", "cw4"))
        gw1, gw2, gw3, gb1, gb2 = (held[n] for n in ("gw1", "gw2", "gw3", "gb1", "gb2"))
        half_b = sb("f_half_b", [P, 2])
        ranges = sb("f_ranges", [P, 2])
        ctx_sb, g1s, g2s, tanh_g = sb("f_ctx", [P, BATCH]), sb("f_g1s", [64, BATCH]), sb("f_g2s", [32, BATCH]), sb("f_tanh_g", [P, BATCH])
        by_batch, base = sb("f_by_batch", [P, BATCH]), sb("f_base", [P, SETS, CPT, 4])
        xt, g1, g2, g3 = sb("f_xt", [P, 2, N]), sb("f_g1", [P, 2, N]), sb("f_g2", [P, 2, N]), sb("f_g3", [P, N])
        tanh_t, coupling, signed = sb("f_tanh_t", [P, SETS, CPT, 4]), sb("f_coupling", [P, CPT, 4]), sb("f_signed", [P, 4, CPT, 4])
        twisted = sb("f_twisted", [P, 16, 4, 32])
        stats, mean_var, eps = sb("g_stats", [P, SC, 6]), sb("g_mean_var", [P, SETS, SC, 2]), sb("g_eps", [P, 1])
        deviation, inverse = sb("g_deviation", [P, SETS, SC]), sb("g_inverse", [P, SETS, SC])

        small_ready, eps_set = sem("f_small_ready"), sem("g_eps_set")
        mean_done, ctx_ready, global_done, global_read = sem("f_mean_done"), sem("f_ctx_ready"), sem("f_global_done"), sem("f_global_read")
        chain, base_ready = sem("f_chain"), sem("f_base_ready")
        turned, turn_read = sem("f_turned"), sem("f_turn_read")
        l1_done, l2_done, l3_done, l4_done = (sem(f"f_l{n}_done") for n in range(1, 5))
        g1_ready, g2_ready, g3_ready, tanh_ready = (sem(f"f_{n}_ready") for n in ("g1", "g2", "g3", "tanh"))
        signed_ready, twist_ready, updated = sem("f_signed_ready"), sem("f_twist_ready"), sem("f_updated")
        sum_ready, stats_ready, deviation_ready = sem("g_sum_ready"), sem("g_stats_ready"), sem("g_deviation_ready")
        norm_chain, normed, stored = sem("g_norm_chain"), sem("g_normed"), sem("g_stored")
        block = ctx.enter_context(nc.Block())

        def cycles(engine, one):
            with engine.Fori(0, CYCLES - 1) as cycle:
                for s in range(SETS):
                    one(cycle, s, (cycle, s + 1) if s < SETS - 1 else (cycle + 1, 0))
            for s in range(SETS):
                one(CYCLES - 1, s, (CYCLES - 1, s + 1) if s < SETS - 1 else None)

        @block.sync
        def _(sp):
            for t in range(TILES):
                sp.wait_ge(normed, t + 1)
                sp.dma_start(out[t * N:(t + 1) * N].rearrange("(c p) d -> p c d", p=P), xc[:, t * CPT:(t + 1) * CPT]).then_inc(stored, 16)
            sp.wait_ge(stored, TILES * 16)

        def groups(t):
            return t.rearrange("p c (g w) -> p c g w", g=4)

        @block.gpsimd
        def _(pool):
            for primed in (turn_read, g1_ready, g2_ready, g3_ready, tanh_ready, l1_done):
                pool.sem_inc(primed, START)
            pool.sem_inc(updated, SETS)
            nc.gpsimd.memset(eps[:], EPS).then_inc(eps_set, 1)
            with pool.Fori(0, CYCLES) as cycle:
                for s in range(SETS):
                    pool.wait_ge(signed_ready, cycle * SETS + s + 1)
                    old = groups(xc[:, s * SC:(s + 1) * SC])
                    nc.gpsimd.tensor_tensor(twisted[:, :, 2:4], old[:, :, 0:2],
                                            signed[:].rearrange("p q c g -> p (q c) g")[:, :, 2:4].unsqueeze(3).broadcast_to([P, 16, 2, 32]),
                                            ALU.mult).then_inc(twist_ready, 1)

        @block.scalar
        def _(act):
            def gelu1(cycle, s, q):
                n = s * 4 + q
                act.wait_ge(l1_done, START + cycle * TILES + n + 1)
                nc.scalar.activation(g1[:, q % 2], l1_ps[:, q % 2], ACT.Gelu, bias=cb[:, 0:1]).then_inc(g1_ready, 1)

            def gelu2(cycle, s, pair):
                act.wait_ge(l2_done, cycle * TILES + s * 4 + pair * 2 + 2)
                nc.scalar.activation(g2[:, pair], l2_ps[:, pair], ACT.Gelu, bias=cb[:, 1:2]).then_inc(g2_ready, 1)

            def read_turn(cycle, s, q):
                n = s * 4 + q
                act.wait_ge(turned, cycle * TILES + n + 1)
                act.wait_ge(l1_done, START + cycle * TILES + max(n - 1, 0))
                nc.scalar.activation(xt[:, q % 2], turn_ps[:, q % 2], ACT.Copy).then_inc(turn_read, 1)

            def one(cycle, s, following):
                read_turn(cycle, s, 3)
                gelu1(cycle, s, 2)
                gelu2(cycle, s, 0)
                gelu1(cycle, s, 3)
                gelu2(cycle, s, 1)
                if following:
                    read_turn(*following, 0)
                    read_turn(*following, 1)
                act.wait_ge(l3_done, cycle * (SETS * 2) + s * 2 + 2)
                nc.scalar.activation(g3[:], l3_ps[:], ACT.Gelu, bias=cb[:, 2:3]).then_inc(g3_ready, 1)
                if following:
                    gelu1(*following, 0)
                    read_turn(*following, 2)
                act.wait_ge(l4_done, cycle * SETS + s + 1)
                nc.scalar.activation(tanh_t[:, s].rearrange("p c q -> p (c q)"), l4_ps[:, 0:16], ACT.Tanh, scale=0.5,
                                     bias=half_b[:, 0:1]).then_inc(tanh_ready, 1)
                if following:
                    gelu1(*following, 1)

            act.wait_ge(small_ready, 1)
            read_turn(0, 0, 0)
            act.wait_ge(global_done, 1)
            nc.scalar.activation(g1s[:], g1_ps[0:64], ACT.Gelu, bias=gb1[:, 0:1]).then_inc(global_read, 1)
            read_turn(0, 0, 1)
            act.wait_ge(global_done, 2)
            nc.scalar.activation(g2s[:], g2_ps[0:32], ACT.Gelu, bias=gb2[:, 0:1]).then_inc(global_read, 1)
            gelu1(0, 0, 0)
            act.wait_ge(global_done, 3)
            nc.scalar.activation(tanh_g[:], g3_ps, ACT.Tanh, scale=0.5, bias=half_b[:, 1:2]).then_inc(global_read, 1)
            read_turn(0, 0, 2)
            gelu1(0, 0, 1)
            cycles(act, one)
            act.wait_ge(eps_set, 1)
            for s in range(SETS):
                act.wait_ge(stats_ready, s + 1)
                nc.scalar.activation(deviation[:, s], mean_var[:, s, :, 1], ACT.Sqrt, bias=eps[:, 0:1]).then_inc(deviation_ready, 1)

        @block.tensor
        def _(pe):
            def turn(cycle, s, q):
                n = s * 4 + q
                if q == 0:
                    pe.wait_ge(updated, cycle * SETS + s + 1)
                pe.wait_ge(turn_read, START + cycle * TILES + max(n - 1, 0))
                for c in range(CPT):
                    last = nc.tensor.transpose(turn_ps[:, q % 2, c * P:(c + 1) * P], xc[:, n * CPT + c], ident[:])
                last.then_inc(turned, 1)

            def layer1(cycle, s, q):
                n = s * 4 + q
                pe.wait_ge(turn_read, START + cycle * TILES + n + 1)
                pe.wait_ge(g1_ready, START + cycle * TILES + max(n - 1, 0))
                nc.tensor.matmul(l1_ps[:, q % 2], w1[:], xt[:, q % 2], start=True, stop=True).then_inc(l1_done, 1)

            def layer2(cycle, s, q):
                n = s * 4 + q
                pe.wait_ge(g1_ready, START + cycle * TILES + n + 1)
                pe.wait_ge(g2_ready, START + cycle * (SETS * 2) + s * 2)
                half = slice(64 * (q % 2), 64 * (q % 2) + 64)
                nc.tensor.matmul(l2_ps[half, q // 2], w2[:], g1[:, q % 2], start=True, stop=True).then_inc(l2_done, 1)

            def layer3(cycle, s, pair):
                pe.wait_ge(g2_ready, START + cycle * (SETS * 2) + s * 2 + pair + 1)
                pe.wait_ge(g3_ready, START + cycle * SETS + s)
                nc.tensor.matmul(l3_ps[64 * pair:64 * pair + 64], w3[:], g2[:, pair], start=True, stop=True).then_inc(l3_done, 1)

            def one(cycle, s, following):
                turn(cycle, s, 3)
                layer2(cycle, s, 0)
                layer1(cycle, s, 2)
                layer2(cycle, s, 1)
                layer1(cycle, s, 3)
                layer3(cycle, s, 0)
                layer2(cycle, s, 2)
                layer2(cycle, s, 3)
                if following:
                    turn(*following, 0)
                    turn(*following, 1)
                layer3(cycle, s, 1)
                if following:
                    layer1(*following, 0)
                    turn(*following, 2)
                pe.wait_ge(g3_ready, START + cycle * SETS + s + 1)
                pe.wait_ge(tanh_ready, START + cycle * SETS + s)
                for c in range(CPT):
                    last = nc.tensor.matmul(l4_ps[:, c * 4:c * 4 + 4], g3[:, c * P:(c + 1) * P], w4[:], start=True, stop=True)
                last.then_inc(l4_done, 1)
                if following:
                    layer1(*following, 1)

            for b in range(BATCH):
                last = nc.tensor.matmul(mean_ps[:, b:b + 1], chunk_sums[:, b], mean[:], start=True, stop=True)
            last.then_inc(mean_done, 1)
            turn(0, 0, 0)
            turn(0, 0, 1)
            pe.wait_ge(ctx_ready, 1)
            nc.tensor.matmul(g1_ps[0:64], gw1[:], ctx_sb[:], start=True, stop=True).then_inc(global_done, 1)
            layer1(0, 0, 0)
            pe.wait_ge(global_read, 1)
            nc.tensor.matmul(g2_ps[0:32], gw2[:], g1s[:], start=True, stop=True).then_inc(global_done, 1)
            turn(0, 0, 2)
            pe.wait_ge(global_read, 2)
            nc.tensor.matmul(g3_ps, gw3[:], g2s[:], start=True, stop=True).then_inc(global_done, 1)
            layer1(0, 0, 1)
            cycles(pe, one)

        @block.vector
        def _(dve):
            nc.vector.tensor_scalar(half_b[:], cb[:, 3:5], 0.5, None, ALU.mult)
            nc.vector.tensor_scalar(ranges[:, 0:1], cb[:, 5:6], 0.3, None, ALU.mult)
            nc.vector.tensor_scalar(ranges[:, 1:2], cb[:, 5:6], 0.7, None, ALU.mult).then_inc(small_ready, 1)
            dve.wait_ge(mean_done, 1)
            nc.vector.tensor_copy(ctx_sb[:], mean_ps).then_inc(ctx_ready, 1)
            dve.wait_ge(global_read, 3)
            dve.wait_ge(small_ready, 1)
            nc.vector.tensor_scalar(by_batch[:], tanh_g[:], ranges[:, 1:2], BASE_COUPLING, ALU.mult, ALU.add).then_inc(base_ready, 1)
            dve.wait_ge(base_ready, 1)
            for s in range(SETS):
                last = nc.vector.tensor_copy(base[:, s].rearrange("p c (b q) -> p c b q", b=2),
                                             by_batch[:, 2 * s:2 * s + 2].unsqueeze(1).unsqueeze(3).broadcast_to([P, CPT, 2, 2]))
            last.then_inc(base_ready, 1)
            dve.wait_ge(base_ready, 2)
            CHAIN = 2

            def one(cycle, s, following):
                chained = Count(cycle * (SETS * CHAIN) + s * CHAIN)
                dve.wait_ge(tanh_ready, START + cycle * SETS + s + 1)
                nc.vector.scalar_tensor_tensor(out=coupling[:], in0=tanh_t[:, s], scalar=ranges[:, 0:1], in1=base[:, s],
                                               op0=ALU.mult, op1=ALU.add).then_inc(chain, 1)
                dve.wait_ge(chain, chained.next())
                nc.vector.tensor_tensor(signed[:], coupling[:].rearrange("p c q -> p q c").unsqueeze(3).broadcast_to([P, 4, CPT, 4]),
                                        sign[:].unsqueeze(1).unsqueeze(1).broadcast_to([P, 4, CPT, 4]), ALU.mult).then_inc(signed_ready, 1)
                dve.wait_ge(signed_ready, cycle * SETS + s + 1)
                at = slice(s * SC, (s + 1) * SC)
                nc.vector.tensor_tensor(twisted[:, :, 0:2], groups(xc[:, at])[:, :, 2:4],
                                        signed[:].rearrange("p q c g -> p (q c) g")[:, :, 0:2].unsqueeze(3).broadcast_to([P, 16, 2, 32]),
                                        ALU.mult).then_inc(chain, 1)
                dve.wait_ge(chain, chained.next())
                dve.wait_ge(twist_ready, cycle * SETS + s + 1)
                nc.vector.tensor_tensor(xc[:, at], xc[:, at], twisted[:].rearrange("p c g w -> p c (g w)"), ALU.add).then_inc(updated, 1)
                if isinstance(cycle, int):
                    dve.wait_ge(updated, CYCLES * SETS + s + 1)
                    nc.vector.tensor_tensor(x3[:, at], x3[:, at], xc[:, at], ALU.add).then_inc(sum_ready, 1)
                    dve.wait_ge(sum_ready, s + 1)
                    for c in range(SC):
                        last = nc.vector.bn_stats(stats[:, c], x3[:, s * SC + c])
                    last.then_inc(norm_chain, 1)
                    dve.wait_ge(norm_chain, s + 1)
                    for c in range(SC):
                        last = nc.vector.bn_aggr(mean_var[:, s, c], stats[:, c])
                    last.then_inc(stats_ready, 1)

            cycles(dve, one)
            for s in range(SETS):
                dve.wait_ge(deviation_ready, s + 1)
                nc.vector.reciprocal(inverse[:, s], deviation[:, s]).then_inc(norm_chain, 1)
                dve.wait_ge(norm_chain, SETS + s + 1)
                for c in range(SC):
                    last = nc.vector.tensor_scalar(xc[:, s * SC + c], x3[:, s * SC + c], mean_var[:, s, c, 0:1],
                                                   inverse[:, s, c:c + 1], ALU.subtract, ALU.mult)
                    if c % CPT == CPT - 1:
                        last.then_inc(normed, 1)


def scratch(nc):
    def dram(name, shape, dt=F32):
        return nc.dram_tensor(f"scratch_{name}", shape, dt, kind="Internal").ap()

    return {
        "parts": [dram(f"parts{z}", (PARTS * HD * HEADS, TOKENS), BF16) for z in range(2)],
        "vals": dram("vals", (TOKENS, HEADS * VW)),
        "o": dram("o", (DIM, TOKENS)),
        "z": dram("z", (HEADS, TOKENS)),
        "rz": dram("rz", (HEADS, TOKENS)),
    }


def build(nc, io, out):
    scr = scratch(nc)
    with ExitStack() as ctx:
        def sb(name, shape, dt=F32):
            return ctx.enter_context(nc.sbuf_tensor(name, shape, dt))

        names = ("ident", "woT", "w1", "b1", "w2", "bo", "b2", "wqkv", "cos1", "sin1", "mask", "decay", "keep", "gn_w", "gn_b",
                 "cw1", "cw2", "cw3", "cw4", "cb", "gw1", "gw2", "gw3", "gb1", "gb2", "mean", "sign")
        held = {name: sb(f"held_{name}", io[name].shape) for name in names}
        with ExitStack() as operands:
            def operand(name, shape, dt=F32):
                return operands.enter_context(nc.sbuf_tensor(name, shape, dt))

            held["q"] = operand("held_q", [P, GROUPS, GH, SEQ], BF16)
            held["k"] = operand("held_k", [P, GROUPS, GH, SEQ], BF16)
            held["v"] = operand("held_v", [P, GROUPS, CPB, GH * VW])
            project_and_split(nc, io, scr, held)
            attend(nc, io, scr, held)
        held["x2b"], held["x2T"] = sb("held_x2b", [P, CHUNKS, DIM]), sb("held_x2T", [P, TOKENS])
        project_out_and_ffn(nc, io, scr, held)
        r, x3, xc = (sb(name, [P, CHUNKS, DIM]) for name in ("r", "x3", "xc"))
        chunk_sums = sb("chunk_sums", [P, BATCH, DIM])
        retain(nc, held, r, x3, xc, chunk_sums)
        couple(nc, held, x3, xc, chunk_sums, out)


def _layout(x):
    import numpy as _np

    f = _np.float32
    a = {k: _np.asarray(v) for k, v in x.items()}
    col = lambda v: _np.ascontiguousarray(v.reshape(-1, 1))
    arrays = {"x": a["L0_attn_x"].reshape(TOKENS, DIM)}
    arrays["xT"] = _np.ascontiguousarray(arrays["x"].T)
    other = _np.arange(DIM).reshape(HEADS, 2, HD // 2)[:, ::-1].reshape(-1)
    wq, wk, wv = a["L0_attn_wq"], a["L0_attn_wk"], a["L0_attn_wv"]
    by_dim = _np.arange(DIM).reshape(HEADS, HD).T.reshape(-1)
    other = other[by_dim]
    arrays["w0"] = _np.stack([wq[by_dim].T, wq[other].T, wk[by_dim].T, wk[other].T, wv.T], 1)
    bq, bk = a["L0_attn_bq"], a["L0_attn_bk"]
    arrays["bias0"] = _np.stack([bq[by_dim], bq[other], bk[by_dim], bk[other]], 1)
    arrays["bv"] = _np.tile(a["L0_attn_bv"], (P, CPT))
    theta = f(10000.0) ** (f(-2.0) * _np.arange(HD // 2, dtype=f) / f(HD))
    angle = _np.repeat(_np.arange(SEQ, dtype=f)[:, None] * theta[None, :], 2, -1).T
    sign = _np.where(_np.arange(HD) < HD // 2, -1, 1)[:, None]
    arrays["cos0"] = _np.repeat(_np.cos(angle), HEADS, 0).astype(f)
    arrays["sin0"] = _np.repeat(_np.sin(angle) * sign, HEADS, 0).astype(f)
    arrays["ident"] = _np.eye(P, dtype=f)
    arrays["woT"] = _np.ascontiguousarray(a["L0_attn_wo"].T)
    arrays["bo"] = _np.tile(a["L0_attn_bo"], (P, CPT))
    arrays["w1"] = a["L0_ffn_W1"]
    arrays["b1"] = _np.ascontiguousarray(a["L0_ffn_b1"].reshape(INTER // P, P).T)
    arrays["w2"] = _np.ascontiguousarray(a["L0_ffn_W2"].reshape(INTER // P, P, DIM).transpose(1, 0, 2))
    arrays["b2"] = _np.tile(a["L0_ffn_b2"], (P, CPT))
    order = _np.concatenate([_np.arange(0, ROPE_DIM, 2), _np.arange(1, ROPE_DIM, 2), _np.arange(ROPE_DIM, DIM)])
    heads = (_np.arange(RHEADS)[:, None] * DIM + order).reshape(-1)
    arrays["wqkv"] = _np.stack([a["L1_attn_W_Q"][:, heads], a["L1_attn_W_K"][:, heads], a["L1_attn_W_V"]], 1)
    inv = f(1.0) / f(10000.0) ** (_np.arange(0, ROPE_DIM, 2, dtype=f) / f(ROPE_DIM))
    angle = _np.arange(SEQ, dtype=f)[:, None] * inv[None, :]
    turn = lambda v: _np.ascontiguousarray(v.reshape(CPB, P, ROPE_DIM)[::-1].transpose(1, 0, 2).astype(f))
    arrays["cos1"] = turn(_np.concatenate([_np.cos(angle)] * 2, -1))
    arrays["sin1"] = turn(_np.concatenate([_np.sin(angle), -_np.sin(angle)], -1))
    n = _np.arange(P)
    arrays["mask"] = _np.where(n[:, None] >= n[None, :], GAMMA ** (n[:, None] - float(P)), 0.0).astype(f)
    arrays["decay"] = _np.stack([GAMMA ** n.astype(_np.float64), GAMMA ** (P - n.astype(_np.float64))], 1).astype(f)
    keep = _np.full((P, CPB), GAMMA ** float(P))
    keep[:, 0] = 0.0
    arrays["keep"] = keep.astype(f)
    arrays["gn_w"] = _np.tile(a["L1_attn_gn_weight"], (P, 1))
    arrays["gn_b"] = _np.tile(a["L1_attn_gn_bias"], (P, 1))
    arrays["cw1"] = a["L1_ffn_cn_w1"]
    arrays["cw2"] = a["L1_ffn_cn_w2"]
    w3, w4 = a["L1_ffn_cn_w3"], a["L1_ffn_cn_w4"]
    blocks = _np.zeros((P, 64), f)
    blocks[:64, :32] = w3
    blocks[64:, 32:] = w3
    arrays["cw3"] = blocks
    blocks = _np.zeros((P, 4), f)
    for q in range(4):
        blocks[32 * q:32 * q + 32, q:q + 1] = w4
    arrays["cw4"] = blocks
    arrays["cb"] = _np.stack([a["L1_ffn_cn_b1"], _np.tile(a["L1_ffn_cn_b2"], 2), _np.tile(a["L1_ffn_cn_b3"], 4),
                              _np.tile(a["L1_ffn_cn_b4"], P), _np.tile(a["L1_ffn_gc_b3"], P),
                              _np.tile(a["L1_ffn_adaptive_range"], P)], 1)
    arrays["gw1"] = a["L1_ffn_gc_w1"]
    arrays["gw2"] = a["L1_ffn_gc_w2"]
    arrays["gw3"] = _np.tile(a["L1_ffn_gc_w3"], (1, P))
    arrays["gb1"] = col(a["L1_ffn_gc_b1"])
    arrays["gb2"] = col(a["L1_ffn_gc_b2"])
    arrays["mean"] = _np.full((P, 1), 1.0 / SEQ, f)
    arrays["sign"] = _np.tile(_np.array([1, -1, -1, 1], f), (P, 1))
    return {k: _np.ascontiguousarray(v) for k, v in arrays.items()}


def kernel(**inputs):
    import concourse.bacc as _bacc
    from concourse import mybir as _mybir
    from concourse.bass_utils import run_bass_kernel_spmd as _run

    nc = _bacc.Bacc("TRN2", target_bir_lowering=False, num_devices=1)
    arrays = {f"in_{k}": v for k, v in _layout(inputs).items()}
    io = {k[3:]: nc.dram_tensor(k, v.shape, _mybir.dt.from_np(v.dtype), kind="ExternalInput").ap()
          for k, v in arrays.items()}
    out = nc.dram_tensor("out", (TOKENS, DIM), F32, kind="ExternalOutput").ap()
    build(nc, io, out)
    r = _run(nc, [arrays], core_ids=[0])
    return r.results[0]["out"].reshape(BATCH, SEQ, DIM)
```

```python
from contextlib import ExitStack

import numpy as np

import concourse.bass as bass
from concourse import mybir

F32 = mybir.dt.float32
F32R = mybir.dt.float32r
BF16 = mybir.dt.bfloat16
ALU = mybir.AluOpType
ACT = mybir.ActivationFunctionType
AX = mybir.AxisListType

BATCH, SEQ, DIM = 4, 1024, 128
TOKENS = BATCH * SEQ
P = 128
N = 512
CPT = N // P
TILES = TOKENS // N
CHUNKS = TOKENS // P
CPB = SEQ // P
EPS = 1e-5
START = 1

HEADS, HD = 16, 8
GH = 4
GROUPS = HEADS // GH
PARTS = 3
LOADS = PARTS * PARTS + PARTS + 1
TWO_ONES = 1.0019378662109375
MAX_ROWS = 96
SHIFT_ROWS = MAX_ROWS + PARTS
VW = HD + 1
INTER = 512

RHEADS = 8
ROPE_DIM = 64
GAMMA = 0.96875
GN = 16
GW = DIM // GN
BASE_COUPLING = 0.1
CYCLES = 3


class Count:

    def __init__(self, base=0):
        self.base, self.n = base, 0

    def next(self):
        self.n += 1
        return self.base + self.n


def wait_apart(engine, sem, value, passed):
    engine.wait_ge(sem, value)
    engine.sem_inc(passed, 1)


def load_group(sp, scr, held, tokens, j, loaded):
    heads = slice(j * GH, (j + 1) * GH) if isinstance(j, int) else bass.ds(j * GH, GH)
    group = j if isinstance(j, int) else bass.ds(j, 1)
    by_row = [scr["parts"][z].rearrange("(r h) t -> r h t", h=HEADS)[:, heads, tokens] for z in range(2)]
    for i in range(PARTS):
        for m in range(PARTS):
            at = (PARTS * i + m) * HD
            sp.dma_start(held["q"][at:at + HD, group], by_row[0][i * HD:(i + 1) * HD]).then_inc(loaded, 16)
        at = PARTS * i * HD
        sp.dma_start(held["k"][at:at + PARTS * HD, group], by_row[1]).then_inc(loaded, 16)
    columns = slice(j * GH * VW, (j + 1) * GH * VW) if isinstance(j, int) else bass.ds(j * (GH * VW), GH * VW)
    sp.dma_start(held["v"][:, group], scr["vals"][tokens, columns].rearrange("(k p) w -> p k w", p=P)).then_inc(loaded, 16)


def project_and_split(nc, io, scr, held):
    with ExitStack() as ctx:
        def sb(name, shape, dt=F32):
            return ctx.enter_context(nc.sbuf_tensor(name, shape, dt))

        def sem(name):
            return ctx.enter_context(nc.semaphore(name))

        ps = ctx.enter_context(nc.psum_tensor("a_ps", [P, 5, N], F32))
        w = sb("a_w", [P, 5, P])
        bias = sb("a_bias", [P, 4])
        bv = sb("a_bv", [P, N])
        cos, sin = sb("a_cos", [P, SEQ]), sb("a_sin", [P, SEQ])
        xt = sb("a_xt", [P, 2, N])
        cos_part, sin_part = sb("a_cos_part", [P, 2, N]), sb("a_sin_part", [P, 2, N])
        turned, rest = sb("a_turned", [P, 2, N]), sb("a_rest", [P, 2, N])
        parts = sb("a_parts", [P, 2, 2, PARTS, N], BF16)
        vals = sb("a_vals", [P, 2, CPT, HEADS, VW])

        consts_loaded = sem("a_consts_loaded")
        x_loaded = [sem(f"a_x_loaded{k}") for k in range(2)]
        projected = [sem(f"a_projected{z}") for z in range(2)]
        v_projected = sem("a_v_projected")
        v_read = sem("a_v_read")
        ones_set = sem("a_ones_set")
        angled = [sem(f"a_angled{z}") for z in range(2)]
        turned_ready = [sem(f"a_turned_ready{z}") for z in range(2)]
        high_ready = [sem(f"a_high_ready{z}") for z in range(2)]
        rest_ready = [sem(f"a_rest_ready{z}") for z in range(2)]
        mid_ready = [sem(f"a_mid_ready{z}") for z in range(2)]
        low_ready = [sem(f"a_low_ready{z}") for z in range(2)]
        parts_stored = [[sem(f"a_parts_stored{z}{k}") for k in range(2)] for z in range(2)]
        vals_stored = [sem(f"a_vals_stored{k}") for k in range(2)]
        rows_set, group_loaded = sem("a_rows_set"), sem("a_group_loaded")
        passed = sem("a_passed")
        block = ctx.enter_context(nc.Block())

        @block.sync
        def _(sp):
            for k in range(2):
                sp.dma_start(xt[:, k], io["xT"][:, k * N:(k + 1) * N]).then_inc(x_loaded[k], 16)

            def store(i):
                for k in range(2):
                    for z in range(2):
                        sp.wait_ge(mid_ready[z], i * 2 + k + 1)
                        wait_apart(sp, low_ready[z], i * 2 + k + 1, passed)
                        sp.dma_start(scr["parts"][z].rearrange("(s p) t -> p s t", p=DIM)[:, :, bass.ds(i * (2 * N) + k * N, N)],
                                     parts[:, z, k]).then_inc(parts_stored[z][k], 16)
                    wait_apart(sp, v_read, START + i * 2 + k + 1, passed)
                    sp.dma_start(scr["vals"].rearrange("(t c p) w -> t p c w", c=CPT, p=P)[i * 2 + k],
                                 vals[:, k].rearrange("p c h w -> p c (h w)")).then_inc(vals_stored[k], 16)

            store(0)
            store(1)
            sp.wait_ge(rows_set, 2)
            for k in range(2):
                sp.wait_ge(vals_stored[k], START + 16)
                for z in range(2):
                    sp.wait_ge(parts_stored[z][k], START + 16)
            load_group(sp, scr, held, slice(0, SEQ), 0, group_loaded)
            with sp.Fori(2, TILES // 2) as i:
                store(i)
            sp.wait_ge(group_loaded, LOADS * 16)
            for k in range(2):
                sp.wait_ge(vals_stored[k], START + 16 * TILES // 2)
                for z in range(2):
                    sp.wait_ge(parts_stored[z][k], START + 16 * TILES // 2)

        @block.gpsimd
        def _(pool):
            for primed in (*angled, v_read, *(s for pair in parts_stored for s in pair), *vals_stored):
                pool.sem_inc(primed, START)
            nc.gpsimd.memset(vals[:], 1.0).then_inc(ones_set, 1)
            nc.gpsimd.memset(held["k"][:].bitcast(F32), TWO_ONES).then_inc(rows_set, 1)
            with pool.Fori(0, TILES // 2) as i:
                for k in range(2):
                    for z in range(2):
                        pool.wait_ge(angled[z], START + i * 2 + k + 1)
                        nc.gpsimd.tensor_tensor(turned[:, z], cos_part[:, z], sin_part[:, z],
                                                ALU.add).then_inc(turned_ready[z], 1)
                    for z in range(2):
                        pool.wait_ge(mid_ready[z], i * 2 + k + 1)
                        nc.gpsimd.tensor_tensor(parts[:, z, k, 2], rest[:, z], parts[:, z, k, 1],
                                                ALU.subtract).then_inc(low_ready[z], 1)

        @block.scalar
        def _(act):
            for t, name in ((w, "w0"), (bias, "bias0"), (cos, "cos0"), (sin, "sin0"), (bv, "bv"), (held["ident"], "ident")):
                act.dma_start(t[:], io[name]).then_inc(consts_loaded, 16)

            def pair(i, last):
                for k in range(2):
                    for z in range(2):
                        act.wait_ge(turned_ready[z], i * 2 + k + 1)
                        act.wait_ge(parts_stored[z][k], START + i * 16)
                        nc.scalar.activation(parts[:, z, k, 0], turned[:, z], ACT.Copy).then_inc(high_ready[z], 1)
                    for z in range(2):
                        act.wait_ge(rest_ready[z], i * 2 + k + 1)
                        nc.scalar.activation(parts[:, z, k, 1], rest[:, z], ACT.Copy).then_inc(mid_ready[z], 1)
                    if not last:
                        act.wait_ge(v_projected, i * 2 + k + 1)
                        act.dma_start(xt[:, k], io["xT"][:, bass.ds((i + 1) * (2 * N) + k * N, N)]).then_inc(x_loaded[k], 16)

            with act.Fori(0, TILES // 2 - 1) as i:
                pair(i, False)
            pair(TILES // 2 - 1, True)

        @block.tensor
        def _(pe):
            pe.wait_ge(consts_loaded, 6 * 16)
            with pe.Fori(0, TILES // 2) as i:
                for k in range(2):
                    pe.wait_ge(x_loaded[k], i * 16 + 16)
                    for z in range(2):
                        pe.wait_ge(angled[z], START + i * 2 + k)
                        nc.tensor.matmul(ps[:, 2 * z], w[:, 2 * z], xt[:, k], start=True, stop=True)
                        nc.tensor.matmul(ps[:, 2 * z + 1], w[:, 2 * z + 1], xt[:, k],
                                         start=True, stop=True).then_inc(projected[z], 1)
                    pe.wait_ge(v_read, START + i * 2 + k)
                    for c in range(CPT):
                        last = nc.tensor.matmul(ps[:, 4, c * P:(c + 1) * P], xt[:, k, c * P:(c + 1) * P], w[:, 4],
                                                start=True, stop=True)
                    last.then_inc(v_projected, 1)

        @block.vector
        def _(dve):
            nc.vector.memset(held["q"][P // 2:P].bitcast(F32), 0.0).then_inc(rows_set, 1)
            dve.wait_ge(consts_loaded, 6 * 16)
            dve.wait_ge(ones_set, 1)
            with dve.Fori(0, TILES // 2) as i:
                for k in range(2):
                    at = slice(k * N, (k + 1) * N)
                    for z in range(2):
                        dve.wait_ge(projected[z], i * 2 + k + 1)
                        nc.vector.scalar_tensor_tensor(out=cos_part[:, z], in0=ps[:, 2 * z], scalar=bias[:, 2 * z:2 * z + 1],
                                                       in1=cos[:, at], op0=ALU.add, op1=ALU.mult)
                        nc.vector.scalar_tensor_tensor(out=sin_part[:, z], in0=ps[:, 2 * z + 1],
                                                       scalar=bias[:, 2 * z + 1:2 * z + 2], in1=sin[:, at],
                                                       op0=ALU.add, op1=ALU.mult).then_inc(angled[z], 1)
                    dve.wait_ge(v_projected, i * 2 + k + 1)
                    dve.wait_ge(vals_stored[k], START + i * 16)
                    nc.vector.tensor_tensor(vals[:, k, :, :, 0:HD], ps[:, 4].rearrange("p (c h d) -> p c h d", c=CPT, d=HD),
                                            bv[:].rearrange("p (c h d) -> p c h d", c=CPT, d=HD), ALU.add).then_inc(v_read, 1)
                    for z in range(2):
                        dve.wait_ge(high_ready[z], i * 2 + k + 1)
                        nc.vector.tensor_tensor(rest[:, z], turned[:, z], parts[:, z, k, 0],
                                                ALU.subtract).then_inc(rest_ready[z], 1)


def attend(nc, io, scr, held):
    QBLOCKS = SEQ // P
    HALVES = SEQ // N
    UNITS = GROUPS * HALVES
    UQ = QBLOCKS // HALVES
    PER_HEAD = UQ * HALVES
    PER_UNIT = GH * PER_HEAD
    TILES_B = UNITS * PER_UNIT
    BANKS = 3
    PROBS = 8
    ITEMS = TILES_B + UNITS
    LATER = 6
    LEAD = 2 * PER_UNIT - 2
    LEAD_ITEMS = LEAD + 1
    SPLIT_STEPS = 4
    STORES = GH * 16
    with ExitStack() as ctx:
        def sb(name, shape, dt=F32):
            return ctx.enter_context(nc.sbuf_tensor(name, shape, dt))

        def sem(name):
            return ctx.enter_context(nc.semaphore(name))

        max_ps = ctx.enter_context(nc.psum_tensor("b_max_ps", [P, BANKS, N], F32))
        score_ps = ctx.enter_context(nc.psum_tensor("b_score_ps", [P, BANKS, N], F32))
        out_ps = ctx.enter_context(nc.psum_tensor("b_out_ps", [P, HALVES, N], F32))
        q, k_, v, identf = held["q"], held["k"], held["v"], held["ident"]
        ident = sb("b_ident", [P, P], BF16)
        sums = sb("b_sums", [P, (BATCH - 1) * SEQ * HEADS // P])
        wqkv = sb("b_wqkv", io["wqkv"].shape)
        w_high, w_low = held["w_high"], held["w_low"]
        probs = sb("b_probs", [P, PROBS, N])
        half_max = sb("b_half_max", [P, 2, GH, UQ, HALVES])
        full_max, mid_rest = (sb(f"b_{n}", [P, GH, UQ]) for n in ("full_max", "mid_rest"))
        shift = sb("b_shift", [P, UQ, PARTS, GH], BF16)
        shift_t = sb("b_shift_t", [GH * PARTS, 2, N], BF16)
        outs = sb("b_outs", [P, 2, HALVES, N])

        ident_ready, consts_loaded = sem("b_ident_ready"), sem("b_consts_loaded")
        w_loaded, w_split, tile_loaded = sem("b_w_loaded"), sem("b_w_split"), sem("b_tile_loaded")
        sums_loaded, sums_inverted, inverses_stored = sem("b_sums_loaded"), sem("b_sums_inverted"), sem("b_inverses_stored")
        operands_loaded = [sem(f"b_operands_loaded{j}") for j in range(GROUPS)]
        shift_loaded = [sem(f"b_shift_loaded{j}") for j in range(GROUPS)]
        max_scored = sem("b_max_scored")
        max_read = sem("b_max_read")
        chain = sem("b_chain")
        shift_ready = sem("b_shift_ready")
        scored = sem("b_scored")
        probs_ready = sem("b_probs_ready")
        probs_used = sem("b_probs_used")
        out_read = sem("b_out_read")
        outs_stored = [sem(f"b_outs_stored{g}") for g in range(2)]
        passed = sem("b_passed")
        block = ctx.enter_context(nc.Block())

        def tokens(b):
            return slice(b * SEQ, (b + 1) * SEQ) if isinstance(b, int) else bass.ds(b * SEQ, SEQ)

        def items(first, last):
            out = []
            for tile in range(first, last):
                if tile % PER_UNIT == LATER and tile > PER_UNIT:
                    out.append(("turn", tile // PER_UNIT - 1, 0))
                out.append(("tile", tile // PER_UNIT, tile % PER_UNIT))
            if last == TILES_B:
                out.append(("turn", UNITS - 1, 0))
            return out

        @block.sync
        def _(sp):
            for j in range(1, GROUPS):
                load_group(sp, scr, held, tokens(0), j, operands_loaded[j])
            later = [name for name in held if name in io and name != "ident"]
            sp.dma_start(wqkv[:], io["wqkv"]).then_inc(w_loaded, 16)
            for name in later:
                sp.dma_start(held[name][:], io[name]).then_inc(consts_loaded, 16)
            early = (BATCH - 1) * SEQ

            def batch(b, last):
                if last:
                    for g in range(2):
                        sp.wait_ge(outs_stored[g], START + (BATCH - 1) * 2 * STORES)
                    sp.dma_start(sums[:], scr["outs"][:, HD, 0:early].rearrange("h (a t) -> h a t", a=P // HEADS)).then_inc(sums_loaded, 16)
                for j in range(GROUPS):
                    if last and j == GROUPS - 1:
                        sp.wait_ge(sums_inverted, 1)
                        sp.dma_start(scr["rz"][:, 0:early].rearrange("h (a t) -> h a t", a=P // HEADS),
                                     sums[:]).then_inc(inverses_stored, 16)
                        sp.wait_ge(inverses_stored, 16)
                        for t in range(2):
                            load_tile(sp, io, scr, held, t, t, tile_loaded)
                    wait_apart(sp, out_read, b * (GROUPS * HALVES) + HALVES * (j + 1) + HALVES, passed)
                    rows = outs[:, j % 2].rearrange("p a n -> p (a n)")
                    at = tokens(b)
                    for h in range(GH):
                        head = j * GH + h
                        sp.dma_start(scr["outs"][head][:, at], rows[32 * h:32 * h + VW]).then_inc(outs_stored[j % 2], 16)
                    if not last:
                        load_group(sp, scr, held, tokens(b + 1), j, operands_loaded[j])

            with sp.Fori(0, BATCH - 1) as b:
                batch(b, False)
            batch(BATCH - 1, True)
            for g in range(2):
                sp.wait_ge(outs_stored[g], START + BATCH * GROUPS // 2 * STORES)
            sp.wait_ge(tile_loaded, 2 * 3 * 16)
            sp.wait_ge(consts_loaded, len(later) * 16)

        @block.gpsimd
        def _(pool):
            for primed in (probs_used, *outs_stored, probs_ready, *operands_loaded):
                pool.sem_inc(primed, START)
            pool.wait_ge(w_loaded, 16)
            nc.gpsimd.tensor_copy(w_high[:], wqkv[:]).then_inc(w_split, 1)
            pool.wait_ge(w_split, 1)
            nc.gpsimd.tensor_tensor(w_low[:], wqkv[:], w_high[:].bitcast(F32), ALU.subtract).then_inc(w_split, 1)

            def move_shift(count, unit):
                j, half = unit // HALVES % GROUPS, unit % HALVES
                wait_apart(pool, max_read, count, passed)
                for s in range(PARTS):
                    pool.dma_start(q[MAX_ROWS + s:MAX_ROWS + s + 1, j, :, half * N:(half + 1) * N],
                                   shift_t[GH * s:GH * (s + 1), unit % 2]).then_inc(shift_loaded[j], 16)

            for n, (kind, unit, _) in enumerate(items(0, LEAD)):
                if kind == "turn":
                    move_shift(n + 1, unit)

            def batch(b, last):
                for n, (kind, unit, _) in enumerate(items(LEAD, last)):
                    if kind == "turn":
                        move_shift(b * ITEMS + LEAD_ITEMS + n + 1, unit)

            with pool.Fori(0, BATCH - 1) as b:
                batch(b, TILES_B + LEAD)
            batch(BATCH - 1, TILES_B)
            for j in range(GROUPS):
                pool.wait_ge(shift_loaded[j], BATCH * HALVES * PARTS * 16)

        @block.scalar
        def _(act):
            def read_out(b, unit):
                j, half = unit // HALVES, unit % HALVES
                act.wait_ge(probs_used, START + b * TILES_B + (unit + 1) * PER_UNIT)
                if half == 0:
                    act.wait_ge(outs_stored[j % 2], START + (b * (2 * STORES) + (STORES if j >= 2 else 0)))
                nc.scalar.activation(outs[:, j % 2, half], out_ps[:, half], ACT.Copy).then_inc(out_read, 1)

            with act.Fori(0, BATCH) as b:
                for unit in range(UNITS):
                    for kb in range(QBLOCKS):
                        for h in range(GH):
                            n = unit * PER_UNIT + kb * GH + h
                            act.wait_ge(scored, b * TILES_B + n + 1)
                            act.wait_ge(probs_used, START + b * TILES_B + max(n - PROBS + 1, 0))
                            nc.scalar.activation(probs[:, n % PROBS], score_ps[:, n % BANKS], ACT.Exp,
                                                 scale=float(1.0 / np.sqrt(np.float32(HD)))).then_inc(probs_ready, 1)
                        if kb == 0 and unit > 0:
                            read_out(b, unit - 1)
                read_out(b, UNITS - 1)

        @block.vector
        def _(dve):
            for half in range(HALVES):
                nc.vector.memset(out_ps[:, half], 0.0).then_inc(out_read, 1)
            nc.vector.tensor_copy(ident[:], identf[:]).then_inc(ident_ready, 1)

            def split(unit, read, splits):
                chained = Count(splits * SPLIT_STEPS)
                part = [shift[:, :, s].rearrange("p q h -> p h q") for s in range(PARTS)]

                def whole():
                    dve.wait_ge(max_read, read)
                    nc.vector.tensor_tensor(full_max[:], half_max[:, unit % 2, :, :, 0], half_max[:, unit % 2, :, :, 1],
                                            ALU.max).then_inc(chain, 1)

                def high():
                    dve.wait_ge(chain, chained.next())
                    nc.vector.tensor_scalar(part[0], full_max[:], -1.0, None, ALU.mult).then_inc(chain, 1)

                def without_high():
                    dve.wait_ge(chain, chained.next())
                    nc.vector.scalar_tensor_tensor(out=mid_rest[:], in0=full_max[:], scalar=-1.0, in1=part[0],
                                                   op0=ALU.mult, op1=ALU.subtract).then_inc(chain, 1)

                def mid():
                    dve.wait_ge(chain, chained.next())
                    nc.vector.tensor_copy(part[1], mid_rest[:]).then_inc(chain, 1)

                def low():
                    dve.wait_ge(chain, chained.next())
                    nc.vector.tensor_tensor(part[2], mid_rest[:], part[1], ALU.subtract).then_inc(shift_ready, 1)

                return [whole, high, without_high, mid, low]

            def read_items(todo, base, splits):
                steps = []
                for n, (kind, unit, t) in enumerate(todo):
                    dve.wait_ge(max_scored, base + n + 1)
                    if kind == "tile":
                        h, qb, half = t // PER_HEAD, t % PER_HEAD // HALVES, t % HALVES
                        nc.vector.tensor_reduce(half_max[:, unit % 2, h, qb, half:half + 1],
                                                max_ps[:, n % BANKS], AX.X, ALU.max).then_inc(max_read, 1)
                        if steps:
                            steps.pop(0)()
                        if t == PER_UNIT - 1:
                            steps = split(unit, base + n + 1, splits)
                            splits = splits + 1
                            if unit == UNITS - 1 and n + 2 == len(todo):
                                while steps:
                                    steps.pop(0)()
                    else:
                        nc.vector.tensor_copy(shift_t[:, unit % 2],
                                              max_ps[0:GH * PARTS, n % BANKS].bitcast(BF16)[:, 0:N]).then_inc(max_read, 1)

            read_items(items(0, LEAD), 0, 0)

            def batch(b, last):
                read_items(items(LEAD, last), b * ITEMS + LEAD_ITEMS, b * UNITS + 1)

            with dve.Fori(0, BATCH - 1) as b:
                batch(b, TILES_B + LEAD)
            batch(BATCH - 1, TILES_B)
            dve.wait_ge(sums_loaded, 16)
            nc.vector.reciprocal(sums[:], sums[:]).then_inc(sums_inverted, 1)

        @block.tensor
        def _(pe):
            pe.wait_ge(ident_ready, 1)

            def max_item(item, n, base, loaded, splits):
                kind, unit, t = item
                j, half = unit // HALVES % GROUPS, unit % HALVES
                if n >= BANKS:
                    pe.wait_ge(max_read, base + (n - BANKS + 1))
                elif not (isinstance(base, int) and base == 0):
                    pe.wait_ge(max_read, base)
                if kind == "tile":
                    h, qb, keys = t // PER_HEAD, half * UQ + t % PER_HEAD // HALVES, t % HALVES
                    if t == 0 and half == 0 and loaded is not None:
                        pe.wait_ge(operands_loaded[j], loaded(unit))
                    nc.tensor.matmul(max_ps[:, n % BANKS], q[0:MAX_ROWS, j, h, qb * P:(qb + 1) * P],
                                     k_[0:MAX_ROWS, j, h, keys * N:(keys + 1) * N],
                                     start=True, stop=True).then_inc(max_scored, 1)
                else:
                    pe.wait_ge(shift_ready, splits)
                    for qb in range(UQ):
                        last = nc.tensor.transpose(max_ps[0:GH * PARTS, n % BANKS].bitcast(BF16)[:, qb * P:(qb + 1) * P],
                                                   shift[:, qb].rearrange("p s h -> p (s h)"), ident[:])
                    last.then_inc(max_scored, 1)

            for n, item in enumerate(items(0, LEAD)):
                max_item(item, n, 0, None, 1)

            def apply(b, unit, kb):
                j, half = unit // HALVES, unit % HALVES
                if kb == 0:
                    pe.wait_ge(out_read, b * (GROUPS * HALVES) + unit + 1)
                for h in range(GH):
                    n = unit * PER_UNIT + kb * GH + h
                    pe.wait_ge(probs_ready, START + b * TILES_B + n + 1)
                    nc.tensor.matmul(out_ps[32 * h:32 * h + VW, half], v[:, j, kb, h * VW:(h + 1) * VW],
                                     probs[:, n % PROBS], start=(kb == 0), stop=(kb == QBLOCKS - 1)).then_inc(probs_used, 1)

            def batch(b, last):
                todo = items(LEAD, last)
                base = b * ITEMS + LEAD_ITEMS
                splits = 1
                done = 0
                for unit in range(UNITS):
                    j, half = unit // HALVES, unit % HALVES
                    pe.wait_ge(shift_loaded[j], b * (HALVES * PARTS * 16) + (half + 1) * (PARTS * 16))
                    for kb in range(QBLOCKS):
                        for h in range(GH):
                            n = unit * PER_UNIT + kb * GH + h
                            pe.wait_ge(probs_ready, START + b * TILES_B + max(n - BANKS + 1, 0))
                            nc.tensor.matmul(score_ps[:, n % BANKS], k_[0:SHIFT_ROWS, j, h, kb * P:(kb + 1) * P],
                                             q[0:SHIFT_ROWS, j, h, half * N:(half + 1) * N],
                                             start=True, stop=True).then_inc(scored, 1)
                            for item in todo[done:done + (2 if todo[done:done + 1] and todo[done][0] == "turn" else 1)]:
                                splits += item[0] == "turn"
                                max_item(item, done, base,
                                         lambda unit: START + b * (LOADS * 16) + (0 if unit == 0 else LOADS * 16),
                                         b * UNITS + splits)
                                done += 1
                        if kb > 0:
                            apply(b, unit, kb - 1)
                        elif unit > 0:
                            apply(b, unit - 1, QBLOCKS - 1)
                apply(b, UNITS - 1, QBLOCKS - 1)
                assert done == len(todo)

            with pe.Fori(0, BATCH - 1) as b:
                batch(b, TILES_B + LEAD)
            batch(BATCH - 1, TILES_B)


def norm_stats(dve, y, stats, mean_var, chain, chained, done, passed):
    for c in range(CPT):
        last = dve.bn_stats(stats[:, c], y[:, c])
    last.then_inc(chain, 1)
    wait_apart(dve, chain, chained.next(), passed)
    for c in range(CPT):
        last = dve.bn_aggr(mean_var[:, c], stats[:, c])
    last.then_inc(done, 1)


def norm_apply(dve, y, out, deviation, inverse, mean_var, chain, chained, done):
    dve.reciprocal(inverse, deviation).then_inc(chain, 1)
    dve.wait_ge(chain, chained.next())
    for c in range(CPT):
        last = dve.tensor_scalar(out(c), y[:, c:c + 1], mean_var[:, c, 0:1], inverse[:, c:c + 1],
                                 ALU.subtract, ALU.mult)
    last.then_inc(done, 1)


def load_tile(sp, io, scr, held, t, k, loaded):
    at = slice(t * N, (t + 1) * N) if isinstance(t, int) else bass.ds(t * N, N)
    sp.dma_start(held["o"][:, k], scr["outs"][:, 0:HD, at]).then_inc(loaded, 16)
    sp.dma_start(held["rz"][:, k], scr["rz"][:, at].unsqueeze(1).broadcast_to([HEADS, HD, N])).then_inc(loaded, 16)
    sp.dma_start(held["residual"][:, k], io["x"][at].rearrange("(c p) d -> p c d", p=P)).then_inc(loaded, 16)


def project_out_and_ffn(nc, io, scr, held):
    FB = INTER // P
    with ExitStack() as ctx:
        def sb(name, shape, dt=F32):
            return ctx.enter_context(nc.sbuf_tensor(name, shape, dt))

        def sem(name):
            return ctx.enter_context(nc.semaphore(name))

        wo_ps, y_ps, turn1_ps, turn2_ps = (ctx.enter_context(nc.psum_tensor(f"c_{n}", [P, N], F32))
                                           for n in ("wo_ps", "y_ps", "turn1_ps", "turn2_ps"))
        h_ps = ctx.enter_context(nc.psum_tensor("c_h_ps", [P, FB, N], F32))
        ident, wo, w1, b1, w2 = (held[n] for n in ("ident", "woT", "w1", "b1", "w2"))
        bo, b2 = (held[n][:].rearrange("p (c d) -> p c d", c=CPT) for n in ("bo", "b2"))
        x2b, x2t, gb = held["x2b"], held["x2T"], held["gn_b"]
        sums, eps = sb("c_sums", [P, HEADS * SEQ // P]), sb("c_eps", [P, 1])
        o, rz, x = held["o"], held["rz"], held["residual"]
        a, xb = sb("c_a", [P, 2, N]), sb("c_xb", [P, 2, CPT, P])
        y1, x1, x1b = sb("c_y1", [P, CPT, P]), sb("c_x1", [P, 2, CPT, P]), sb("c_x1b", [P, 2, CPT, P])
        x1t, h = sb("c_x1t", [P, 2, N]), sb("c_h", [P, FB, N])
        y2, x2 = sb("c_y2", [P, CPT, P]), sb("c_x2", [P, 2, CPT, P])
        stats = [sb(f"c_stats{s}", [P, CPT, 6]) for s in range(2)]
        mean_var = [sb(f"c_mean_var{s}", [P, CPT, 2]) for s in range(2)]
        deviation = [sb(f"c_deviation{s}", [P, CPT]) for s in range(2)]
        inverse = [sb(f"c_inverse{s}", [P, CPT]) for s in range(2)]

        eps_set = sem("c_eps_set")
        sums_loaded, sums_inverted, inverses_stored = sem("c_sums_loaded"), sem("c_sums_inverted"), sem("c_inverses_stored")
        tile_loaded = [sem(f"c_tile_loaded{k}") for k in range(2)]
        a_ready, xb_ready, x1b_ready = sem("c_a_ready"), sem("c_xb_ready"), sem("c_x1b_ready")
        wo_done, h_done, y_done = sem("c_wo_done"), sem("c_h_done"), sem("c_y_done")
        turned = [sem(f"c_turned{s}") for s in range(2)]
        chain = [sem(f"c_chain{s}") for s in range(2)]
        stats_ready = [sem(f"c_stats_ready{s}") for s in range(2)]
        deviation_ready = [sem(f"c_deviation_ready{s}") for s in range(2)]
        normed = [sem(f"c_normed{s}") for s in range(2)]
        h_ready = sem("c_h_ready")
        x1t_ready, x2t_ready = sem("c_x1t_ready"), sem("c_x2t_ready")
        y_read = [sem(f"c_y_read{s}") for s in range(2)]
        x2_kept = sem("c_x2_kept")
        passed = sem("c_passed")
        block = ctx.enter_context(nc.Block())

        def tile(t):
            return slice(t * N, (t + 1) * N) if isinstance(t, int) else bass.ds(t * N, N)

        @block.sync
        def _(sp):
            late = slice((BATCH - 1) * SEQ, TOKENS)
            sp.dma_start(sums[:], scr["outs"][:, HD, late].rearrange("h (a t) -> h a t", a=P // HEADS)).then_inc(sums_loaded, 16)

            def load(t, k):
                wait_apart(sp, xb_ready, t - 1, passed)
                load_tile(sp, io, scr, held, t, k, tile_loaded[k])

            sp.wait_ge(sums_inverted, 1)
            sp.dma_start(scr["rz"][:, late].rearrange("h (a t) -> h a t", a=P // HEADS), sums[:]).then_inc(inverses_stored, 16)
            sp.wait_ge(inverses_stored, 16)
            with sp.Fori(1, TILES // 2) as i:
                for k in range(2):
                    load(i * 2 + k, k)

        @block.gpsimd
        def _(pool):
            for primed in (*y_read, *normed, x2_kept, x1t_ready, x2t_ready):
                pool.sem_inc(primed, START)
            nc.gpsimd.memset(eps[:], EPS).then_inc(eps_set, 1)

            def scale(t, k, i):
                if not (isinstance(t, int) and t < 2):
                    pool.wait_ge(tile_loaded[k], i * 48)
                if not (isinstance(t, int) and t < 2):
                    pool.wait_ge(y_read[0], START + t - 1)
                nc.gpsimd.tensor_tensor(a[:, k], o[:, k], rz[:, k], ALU.mult).then_inc(a_ready, 1)
                nc.gpsimd.tensor_tensor(xb[:, k], x[:, k], bo[:], ALU.add).then_inc(xb_ready, 1)

            def residual(t, k):
                pool.wait_ge(normed[0], START + t + 1)
                if not (isinstance(t, int) and t < 2):
                    pool.wait_ge(y_read[1], START + t - 1)
                nc.gpsimd.tensor_tensor(x1b[:, k], x1[:, k], b2[:], ALU.add).then_inc(x1b_ready, 1)

            def keep_x2(t, k):
                pool.wait_ge(normed[1], START + t + 1)
                at = slice(t * CPT, (t + 1) * CPT) if isinstance(t, int) else bass.ds(t * CPT, CPT)
                nc.gpsimd.tensor_tensor(x2b[:, at], x2[:, k], gb[:].unsqueeze(1).broadcast_to([P, CPT, DIM]), ALU.add).then_inc(x2_kept, 1)

            scale(0, 0, 0)
            scale(1, 1, 0)
            residual(0, 0)
            scale(2, 0, 1)
            residual(1, 1)
            with pool.Fori(0, TILES // 2 - 2) as i:
                scale(i * 2 + 3, 1, i + 1)
                residual(i * 2 + 2, 0)
                keep_x2(i * 2, 0)
                scale(i * 2 + 4, 0, i + 2)
                residual(i * 2 + 3, 1)
                keep_x2(i * 2 + 1, 1)
            scale(TILES - 1, 1, TILES // 2 - 1)
            residual(TILES - 2, 0)
            keep_x2(TILES - 4, 0)
            residual(TILES - 1, 1)
            for t in range(TILES - 3, TILES):
                keep_x2(t, t % 2)

        @block.scalar
        def _(act):
            act.wait_ge(eps_set, 1)

            def root(s, t):
                act.wait_ge(stats_ready[s], t + 1)
                nc.scalar.activation(deviation[s][:], mean_var[s][:, :, 1], ACT.Sqrt, bias=eps[:, 0:1]).then_inc(deviation_ready[s], 1)

            def read_turn1(t, k):
                act.wait_ge(turned[0], t + 1)
                nc.scalar.activation(x1t[:, k], turn1_ps[:], ACT.Copy).then_inc(x1t_ready, 1)

            def read_turn2(t):
                act.wait_ge(turned[1], t + 1)
                nc.scalar.activation(x2t[:, tile(t)], turn2_ps[:], ACT.Copy).then_inc(x2t_ready, 1)

            def relu(t, f):
                act.wait_ge(h_done, t * FB + f + 1)
                act.wait_ge(y_done, t)
                nc.scalar.activation(h[:, f], h_ps[:, f], ACT.Relu, bias=b1[:, f:f + 1]).then_inc(h_ready, 1)

            def step(t, k, first=False, last=False):
                relu(t, 0)
                relu(t, 1)
                if not last:
                    root(0, t + 1)
                for f in range(2, FB):
                    relu(t, f)
                if not first:
                    root(1, t - 1)
                if not last:
                    read_turn1(t + 1, 1 - k)
                if not first:
                    read_turn2(t - 1)

            root(0, 0)
            read_turn1(0, 0)
            step(0, 0, first=True)
            with act.Fori(0, TILES // 2 - 2) as i:
                step(i * 2 + 1, 1)
                step(i * 2 + 2, 0)
            step(TILES - 3, 1)
            step(TILES - 2, 0)
            step(TILES - 1, 1, last=True)
            root(1, TILES - 1)
            read_turn2(TILES - 1)

        @block.tensor
        def _(pe):
            def project(t, k):
                pe.wait_ge(a_ready, t + 1)
                pe.wait_ge(y_read[0], START + t)
                for c in range(CPT):
                    last = nc.tensor.matmul(wo_ps[:, c * P:(c + 1) * P], a[:, k, c * P:(c + 1) * P], wo[:], start=True, stop=True)
                last.then_inc(wo_done, 1)

            def turn(s, t, k):
                pe.wait_ge(normed[s], START + t + 1)
                pe.wait_ge((x1t_ready, x2t_ready)[s], START + t)
                for c in range(CPT):
                    last = nc.tensor.transpose((turn1_ps, turn2_ps)[s][:, c * P:(c + 1) * P],
                                               (x1, x2)[s][:, k, c], ident[:])
                last.then_inc(turned[s], 1)

            def step(t, k, first=False, last=False):
                pe.wait_ge(x1t_ready, START + t + 1)
                for f in range(FB):
                    pe.wait_ge(h_ready, t * FB)
                    nc.tensor.matmul(h_ps[:, f], w1[:, f * P:(f + 1) * P], x1t[:, k], start=True, stop=True).then_inc(h_done, 1)
                if not (isinstance(t, int) and t + 2 >= TILES):
                    project(t + 2, k)
                pe.wait_ge(h_ready, t * FB + FB)
                pe.wait_ge(y_read[1], START + t)
                for c in range(CPT):
                    for f in range(FB):
                        prod = nc.tensor.matmul(y_ps[:, c * P:(c + 1) * P], h[:, f, c * P:(c + 1) * P], w2[:, f],
                                                start=(f == 0), stop=(f == FB - 1))
                prod.then_inc(y_done, 1)
                if not last:
                    turn(0, t + 1, 1 - k)
                if not first:
                    turn(1, t - 1, 1 - k)

            project(0, 0)
            turn(0, 0, 0)
            project(1, 1)
            step(0, 0, first=True)
            with pe.Fori(0, TILES // 2 - 2) as i:
                step(i * 2 + 1, 1)
                step(i * 2 + 2, 0)
            step(TILES - 3, 1)
            step(TILES - 2, 0)
            step(TILES - 1, 1, last=True)
            turn(1, TILES - 1, 1)

        @block.vector
        def _(dve):
            dve.wait_ge(sums_loaded, 16)
            nc.vector.reciprocal(sums[:], sums[:]).then_inc(sums_inverted, 1)

            def start(s, t, k, nth):
                product, base, y = ((wo_done, xb_ready, y1), (y_done, x1b_ready, y2))[s]
                dve.wait_ge(product, t + 1)
                dve.wait_ge(base, t + 1)
                if not (isinstance(t, int) and t == 0):
                    dve.wait_ge(normed[s], START + t)
                nc.vector.tensor_tensor(y[:], (wo_ps, y_ps)[s][:].rearrange("p (c d) -> p c d", c=CPT),
                                        (xb, x1b)[s][:, k], ALU.add).then_inc(y_read[s], 1)
                dve.wait_ge(y_read[s], START + t + 1)
                norm_stats(nc.vector, y, stats[s], mean_var[s], chain[0], Count(nth), stats_ready[s], passed)

            def finish(s, t, k, nth):
                dve.wait_ge(deviation_ready[s], t + 1)
                if s and not (isinstance(t, int) and t < 2):
                    dve.wait_ge(x2_kept, START + t - 1)
                norm_apply(nc.vector, (y1, y2)[s], lambda c: (x1, x2)[s][:, k, c:c + 1], deviation[s][:], inverse[s][:], mean_var[s],
                           chain[1], Count(nth), normed[s])

            def step(t, k, first=False, last=False):
                if not last:
                    start(0, t + 1, 1 - k, 1 if first else 2 * t)
                if not first:
                    start(1, t - 1, 1 - k, 2 * t if last else 2 * t + 1)
                if not last:
                    finish(0, t + 1, 1 - k, 1 if first else 2 * t)
                if not first:
                    finish(1, t - 1, 1 - k, 2 * t if last else 2 * t + 1)

            start(0, 0, 0, 0)
            finish(0, 0, 0, 0)
            step(0, 0, first=True)
            with dve.Fori(0, TILES // 2 - 2) as i:
                step(i * 2 + 1, 1)
                step(i * 2 + 2, 0)
            step(TILES - 3, 1)
            step(TILES - 2, 0)
            step(TILES - 1, 1, last=True)
            start(1, TILES - 1, 1, 2 * TILES - 1)
            finish(1, TILES - 1, 1, 2 * TILES - 1)


def retain(nc, held, r, x3, chunk_sums):
    RW = RHEADS * DIM
    HB = N // DIM
    HALVES = RHEADS // HB
    ITEMS = ("a", "q", "k", "fq", "v", "fk", "g")
    BANKS = len(ITEMS)
    UPDATES = HALVES * (CPB - 1)
    with ExitStack() as ctx:
        def sb(name, shape, dt=F32):
            return ctx.enter_context(nc.sbuf_tensor(name, shape, dt))

        def sem(name):
            return ctx.enter_context(nc.semaphore(name))

        ps = ctx.enter_context(nc.psum_tensor("d_ps", [P, BANKS, HB, DIM], F32))
        out_ps = ctx.enter_context(nc.psum_tensor("d_out_ps", [P, N], F32))
        w_high, w_low, cos, sin, ident, mask, decay, keep = (held[n] for n in ("w_high", "w_low", "cos1", "sin1", "ident", "mask", "decay", "keep"))
        x2t = held["x2T"]
        xt_high, xt_low = sb("d_xt_high", [P, 2, P], F32R), sb("d_xt_low", [P, 2, P], F32R)
        by_cos, by_sin = sb("d_by_cos", [P, 2, RHEADS, ROPE_DIM]), sb("d_by_sin", [P, 2, RHEADS, ROPE_DIM])
        rotated = sb("d_rotated", [P, 2, RHEADS, ROPE_DIM])
        qkv = sb("d_qkv", [P, 3, 2, RHEADS, DIM])
        qd = sb("d_qd", [P, RHEADS, DIM])
        qkt = sb("d_qkt", [P, 2, RHEADS, P])
        am = sb("d_am", [P, RHEADS, P])
        state = sb("d_state", [P, RHEADS, DIM])
        x2b, gw, eps = held["x2b"], held["gn_w"], sb("e_eps", [P, 1])
        G = CPB * GN
        means, sums = sb("e_means", [P, G]), sb("e_sums", [P, G])
        centred = sb("e_centred", [P, CPB, DIM])
        squares = sb("e_squares", [P, CPB, DIM])
        y = sb("e_y", [P, CPB, DIM])
        squared, deviation, inverse = (sb(f"e_{n}", [P, G]) for n in ("squared", "deviation", "inverse"))
        stats, mean_var = sb("e_stats", [P, CPB, 6]), sb("e_mean_var", [P, CPB, 2])
        spread, shrink = sb("e_spread", [P, CPB]), sb("e_shrink", [P, CPB])

        made = {kind: sem(f"d_made_{kind}") for kind in ITEMS}
        xt_high_ready, xt_ready = sem("d_xt_high_ready"), sem("d_xt_ready")
        roped = [sem(f"d_roped{z}") for z in range(2)]
        rotated_ready = [sem(f"d_rotated_ready{z}") for z in range(2)]
        passed_by = [sem(f"d_passed_by{z}") for z in range(2)]
        silu_done = [sem(f"d_silu_done{z}") for z in range(2)]
        v_ready = sem("d_v_ready")
        qd_ready = sem("d_qd_ready")
        flip_read = [sem(f"d_flip_read{z}") for z in range(2)]
        a_masked, state_ready = sem("d_a_masked"), sem("d_state_ready")
        out_done, out_read = sem("d_out_done"), sem("d_out_read")
        eps_set = sem("e_eps_set")
        means_ready, centred_ready, squares_ready = sem("e_means_ready"), sem("e_centred_ready"), sem("e_squares_ready")
        squared_ready, deviation_ready = sem("e_squared_ready"), sem("e_deviation_ready")
        scaled_ready, weighted_ready = sem("e_scaled_ready"), sem("e_weighted_ready")
        stats_ready, spread_ready, chain = sem("e_stats_ready"), sem("e_spread_ready"), sem("e_chain")
        x3_ready = sem("e_x3_ready")
        tail_chain = [sem(f"e_tail_chain{m}") for m in range(2)]
        passed = sem("e_passed")
        block = ctx.enter_context(nc.Block())

        def bank(kind, half):
            return ps[:, (ITEMS.index(kind) * HALVES + half) % BANKS]

        def tokens(b, c):
            at = b * SEQ + (CPB - 1 - c) * P
            return slice(at, at + P) if isinstance(b, int) else bass.ds(at, P)

        def heads(half):
            return slice(half * HB, (half + 1) * HB)

        def span(b, at, count):
            return slice(at, at + count) if isinstance(b, int) else bass.ds(at, count)

        def groups(t):
            return t.rearrange("p c (g w) -> p (c g) w", w=GW)

        TAIL = ((BATCH - 1, CPB // 2), (BATCH, 0))

        def batches(engine, batch, tail=()):
            batch(0, False)
            with engine.Fori(1, BATCH - 1) as b:
                batch(b, False)
            batch(BATCH - 1, True)
            for step in tail:
                step()

        @block.gpsimd
        def _(pool):
            for primed in (out_read,):
                pool.sem_inc(primed, START)
            even, odd = slice(0, ROPE_DIM // 2), slice(ROPE_DIM // 2, ROPE_DIM)

            def rotate(n):
                for z in range(2):
                    pool.wait_ge(roped[z], n * HALVES + HALVES)
                    nc.gpsimd.tensor_tensor(rotated[:, z, :, even], by_cos[:, z, :, even], by_sin[:, z, :, odd], ALU.add)
                    nc.gpsimd.tensor_tensor(rotated[:, z, :, odd], by_cos[:, z, :, odd], by_sin[:, z, :, even],
                                            ALU.add).then_inc(rotated_ready[z], 1)

            def fetch(b, c):
                nc.gpsimd.tensor_copy(xt_high[:, c % 2], x2t[:, tokens(b, c)]).then_inc(xt_high_ready, 1)
                wait_apart(pool, xt_high_ready, b * CPB + c + 1, passed)
                nc.gpsimd.tensor_tensor(xt_low[:, c % 2], x2t[:, tokens(b, c)], xt_high[:, c % 2].bitcast(F32),
                                        ALU.subtract).then_inc(xt_ready, 1)

            nc.gpsimd.memset(eps[:], EPS).then_inc(eps_set, 1)
            fetch(0, 0)
            fetch(0, 1)

            def norm(b, nth, first=0, count=CPB):
                at, some, its = span(b, b * CPB + first, count), slice(first, first + count), slice(first * GN, (first + count) * GN)

                def centre():
                    pool.wait_ge(means_ready, nth + 1)
                    nc.gpsimd.tensor_tensor(groups(centred[:, some]), groups(r[:, at]),
                                            means[:, its].unsqueeze(2).broadcast_to([P, count * GN, GW]),
                                            ALU.subtract).then_inc(centred_ready, 1)

                def weigh():
                    pool.wait_ge(scaled_ready, nth + 1)
                    nc.gpsimd.tensor_tensor(y[:, some], squares[:, some], gw[:].unsqueeze(1).broadcast_to([P, count, DIM]),
                                            ALU.mult).then_inc(weighted_ready, 1)

                return centre, weigh

            tail = [norm(BATCH - 1, nth, first, CPB // 2) for nth, first in TAIL]

            def batch(b, last):
                centre, weigh = norm(b - 1, b - 1)
                steps = {1: centre, 4: weigh} if not (isinstance(b, int) and b == 0) else {}
                if last:
                    steps[7] = tail[0][0]
                for c in range(CPB):
                    n = b * CPB + c
                    rotate(n)
                    if c in steps:
                        steps[c]()
                    if not (last and c >= CPB - 2):
                        pool.wait_ge(made["v"], n * HALVES + HALVES)
                        fetch(b + (c + 2) // CPB, (c + 2) % CPB)

            batches(pool, batch, (tail[1][0], tail[0][1], tail[1][1]))

        @block.scalar
        def _(act):
            def activate(n, k, z):
                for half in range(HALVES):
                    act.wait_ge(roped[z], n * HALVES + half + 1)
                    nc.scalar.activation(qkv[:, z, k, heads(half), ROPE_DIM:], bank("qk"[z], half)[:, :, ROPE_DIM:],
                                         ACT.Silu).then_inc(passed_by[z], 1)
                act.wait_ge(rotated_ready[z], n + 1)
                nc.scalar.activation(qkv[:, z, k, :, 0:ROPE_DIM], rotated[:, z], ACT.Silu).then_inc(silu_done[z], 1)

            def read_flip(n, z):
                for half in range(HALVES):
                    act.wait_ge(made[("fq", "fk")[z]], n * HALVES + half + 1)
                    nc.scalar.activation(qkt[:, z, heads(half)], bank(("fq", "fk")[z], half), ACT.Copy).then_inc(flip_read[z], 1)

            def read_v(n, k):
                for half in range(HALVES):
                    act.wait_ge(made["v"], n * HALVES + half + 1)
                    nc.scalar.activation(qkv[:, 2, k, heads(half)], bank("v", half), ACT.Silu).then_inc(v_ready, 1)

            def norm(b, nth, first=0, count=CPB):
                at, some, its = span(b, b * CPB + first, count), slice(first, first + count), slice(first * GN, (first + count) * GN)

                def square():
                    act.wait_ge(centred_ready, nth + 1)
                    nc.scalar.activation(squares[:, some], centred[:, some], ACT.Square).then_inc(squares_ready, 1)

                def group_root():
                    act.wait_ge(squared_ready, nth + 1)
                    nc.scalar.activation(deviation[:, its], squared[:, its], ACT.Sqrt, scale=1.0 / GW,
                                         bias=eps[:, 0:1]).then_inc(deviation_ready, 1)

                def root():
                    act.wait_ge(stats_ready, nth + 1)
                    nc.scalar.activation(spread[:, some], mean_var[:, some, 1], ACT.Sqrt, bias=eps[:, 0:1]).then_inc(spread_ready, 1)

                def copy():
                    act.wait_ge(x3_ready, nth + 1)
                    nc.scalar.activation(r[:, at], x3[:, at], ACT.Copy)

                return square, group_root, root, copy

            tail = [norm(BATCH - 1, nth, first, CPB // 2) for nth, first in TAIL]

            def batch(b, last):
                square, group_root, root, copy = norm(b - 1, b - 1)
                steps = {1: square, 2: group_root, 4: root, 5: copy} if not (isinstance(b, int) and b == 0) else {}
                for c in range(CPB):
                    n, k = b * CPB + c, c % 2
                    ahead = not (last and c == CPB - 1)
                    if ahead:
                        activate(n + 1, 1 - k, 0)
                        activate(n + 1, 1 - k, 1)
                    act.wait_ge(out_done, n + 1)
                    nc.scalar.activation(r[:, span(b, b * CPB + (CPB - 1 - c), 1)], out_ps[:, 0:P].unsqueeze(1), ACT.Copy,
                                         scale=decay[:, 1:2]).then_inc(out_read, 1)
                    if ahead:
                        read_flip(n + 1, 0)
                        read_v(n + 1, 1 - k)
                        read_flip(n + 1, 1)
                    if c in steps:
                        steps[c]()

            act.wait_ge(eps_set, 1)
            activate(0, 0, 0)
            activate(0, 0, 1)
            read_flip(0, 0)
            read_v(0, 0)
            read_flip(0, 1)
            batches(act, batch, (tail[0][0], tail[0][1], tail[1][0], tail[1][1], tail[0][2], tail[1][2], tail[0][3], tail[1][3]))

        @block.vector
        def _(dve):
            nc.vector.memset(state[:], 0.0).then_inc(state_ready, 1)

            def rope(n, c, z):
                for half in range(HALVES):
                    dve.wait_ge(made["qk"[z]], n * HALVES + half + 1)
                    src = bank("qk"[z], half)[:, :, 0:ROPE_DIM]
                    angles = [t[:, c:c + 1].broadcast_to([P, HB, ROPE_DIM]) for t in (cos, sin)]
                    nc.vector.tensor_tensor(by_cos[:, z, heads(half)], src, angles[0], ALU.mult)
                    nc.vector.tensor_tensor(by_sin[:, z, heads(half)], src, angles[1], ALU.mult).then_inc(roped[z], 1)

            def decay_q(n, k):
                dve.wait_ge(silu_done[0], n + 1)
                nc.vector.tensor_scalar(qd[:], qkv[:, 0, k], decay[:, 0:1], None, ALU.mult).then_inc(qd_ready, 1)

            for z in range(2):
                rope(0, 0, z)
            decay_q(0, 0)

            def norm(b, nth, first=0, count=CPB, chain=chain, chained=None):
                at, some, its = span(b, b * CPB + first, count), slice(first, first + count), slice(first * GN, (first + count) * GN)
                CHAIN = 5
                chained = chained or Count(nth * CHAIN)

                def mean():
                    dve.wait_ge(out_read, START + b * CPB + CPB - first)
                    nc.vector.tensor_reduce(sums[:, its], groups(r[:, at]), AX.X, ALU.add).then_inc(chain, 1)
                    dve.wait_ge(chain, chained.next())
                    nc.vector.tensor_scalar(means[:, its], sums[:, its], 1.0 / GW, None, ALU.mult).then_inc(means_ready, 1)

                def variance():
                    dve.wait_ge(squares_ready, nth + 1)
                    nc.vector.tensor_reduce(squared[:, its], groups(squares[:, some]), AX.X, ALU.add).then_inc(squared_ready, 1)

                def invert():
                    dve.wait_ge(deviation_ready, nth + 1)
                    nc.vector.reciprocal(inverse[:, its], deviation[:, its]).then_inc(chain, 1)
                    dve.wait_ge(chain, chained.next())
                    nc.vector.tensor_tensor(groups(squares[:, some]), groups(centred[:, some]),
                                            inverse[:, its].unsqueeze(2).broadcast_to([P, count * GN, GW]), ALU.mult).then_inc(scaled_ready, 1)

                def residual():
                    dve.wait_ge(weighted_ready, nth + 1)
                    nc.vector.tensor_tensor(y[:, some], y[:, some], x2b[:, at], ALU.add).then_inc(chain, 1)
                    dve.wait_ge(chain, chained.next())
                    for c in range(first, first + count):
                        last = nc.vector.bn_stats(stats[:, c], y[:, c])
                    last.then_inc(chain, 1)
                    wait_apart(dve, chain, chained.next(), passed)
                    for c in range(first, first + count):
                        last = nc.vector.bn_aggr(mean_var[:, c], stats[:, c])
                    last.then_inc(stats_ready, 1)

                def apply():
                    dve.wait_ge(spread_ready, nth + 1)
                    nc.vector.reciprocal(shrink[:, some], spread[:, some]).then_inc(chain, 1)
                    dve.wait_ge(chain, chained.next())
                    for c in range(first, first + count):
                        last = nc.vector.tensor_scalar(x3[:, span(b, b * CPB + c, 1)], y[:, c:c + 1], mean_var[:, c, 0:1],
                                                       shrink[:, c:c + 1], ALU.subtract, ALU.mult)
                    last.then_inc(x3_ready, 1)

                def add_up():
                    dve.wait_ge(x3_ready, nth + 1)
                    nc.vector.tensor_reduce(chunk_sums[:, span(b, b, 1)], x3[:, span(b, b * CPB, CPB)].rearrange("p c d -> p d c"),
                                            AX.X, ALU.add)

                return mean, variance, invert, residual, apply, add_up

            one, two = (norm(BATCH - 1, nth, first, CPB // 2, tail_chain[m], Count(0)) for m, (nth, first) in enumerate(TAIL))

            def batch(b, last):
                steps = dict(zip((0, 2, 3, 4, 5, 6), norm(b - 1, b - 1))) if not (isinstance(b, int) and b == 0) else {}
                if last:
                    steps[7] = one[0]
                for c in range(CPB):
                    n, k = b * CPB + c, c % 2
                    ahead = not (last and c == CPB - 1)
                    for half in range(HALVES):
                        dve.wait_ge(made["a"], n * HALVES + half + 1)
                        nc.vector.tensor_tensor(am[:, heads(half)], bank("a", half), mask[:].unsqueeze(1).broadcast_to([P, HB, P]),
                                                ALU.mult).then_inc(a_masked, 1)
                    if ahead:
                        for z in range(2):
                            rope(n + 1, (c + 1) % CPB, z)
                    if c in steps:
                        steps[c]()
                    for half in range(HALVES if c < CPB - 1 else 0):
                        dve.wait_ge(made["g"], b * UPDATES + (c * HALVES + half + 1))
                        dve.wait_ge(state_ready, b * UPDATES + (1 + c * HALVES))
                        flat = state[:, heads(half)].rearrange("p h v -> p (h v)")
                        nc.vector.scalar_tensor_tensor(out=flat, in0=flat, scalar=keep[:, c:c + 1],
                                                       in1=bank("g", half).rearrange("p h v -> p (h v)"),
                                                       op0=ALU.mult, op1=ALU.add).then_inc(state_ready, 1)
                    if ahead and c != CPB - 2:
                        decay_q(n + 1, 1 - k)

            mean, variance, invert, residual, apply, add_up = range(6)
            batches(dve, batch, (two[mean], one[variance], one[invert], two[variance], two[invert], one[residual],
                                 two[residual], one[apply], two[apply], two[add_up]))

        @block.tensor
        def _(pe):
            def project(n, k, kind):
                for half in range(HALVES):
                    if kind == "q" and not (isinstance(n, int) and n == 0):
                        pe.wait_ge(v_ready, n * HALVES)
                    terms = ((xt_high, w_high), (xt_high, w_low), (xt_low, w_high))
                    for m, (x, w) in enumerate(terms):
                        last = nc.tensor.matmul(bank(kind, half).rearrange("p h v -> p (h v)"), x[:, k],
                                                w[:, "qkv".index(kind), half * N:(half + 1) * N],
                                                start=(m == 0), stop=(m == len(terms) - 1))
                    last.then_inc(made[kind], 1)

            def flip(n, k, z):
                pe.wait_ge(passed_by[z], n * HALVES + HALVES)
                pe.wait_ge(silu_done[z], n + 1)
                for half in range(HALVES):
                    for h in range(HB):
                        last = nc.tensor.transpose(bank(("fq", "fk")[z], half)[:, h], qkv[:, z, k, half * HB + h], ident[:])
                    last.then_inc(made[("fq", "fk")[z]], 1)

            def products(n):
                for z in range(2):
                    pe.wait_ge(flip_read[z], n * HALVES + HALVES)
                for half in range(HALVES):
                    if half:
                        pe.wait_ge(v_ready, n * HALVES + 1)
                    for h in range(half * HB, (half + 1) * HB):
                        last = nc.tensor.matmul(bank("a", half)[:, h % HB], qkt[:, 0, h], qkt[:, 1, h], start=True, stop=True)
                    last.then_inc(made["a"], 1)

            pe.wait_ge(xt_ready, 1)
            project(0, 0, "q")
            project(0, 0, "k")
            flip(0, 0, 0)
            project(0, 0, "v")
            flip(0, 0, 1)

            def batch(b, last):
                for c in range(CPB):
                    n, k = b * CPB + c, c % 2
                    ahead = not (last and c == CPB - 1)
                    products(n)
                    if ahead:
                        pe.wait_ge(xt_ready, n + 2)
                        project(n + 1, 1 - k, "q")
                    pe.wait_ge(out_read, START + n)
                    if c:
                        pe.wait_ge(state_ready, b * UPDATES + (1 + c * HALVES))
                        for h in range(RHEADS):
                            nc.tensor.matmul(out_ps[:, 0:P], qkt[:, 1, h], state[:, h], start=(h == 0), stop=False)
                    if ahead:
                        project(n + 1, 1 - k, "k")
                    pe.wait_ge(a_masked, n * HALVES + HALVES)
                    for h in range(RHEADS):
                        prod = nc.tensor.matmul(out_ps[:, 0:P], am[:, h], qkv[:, 2, k, h],
                                                start=(c == 0 and h == 0), stop=(h == RHEADS - 1))
                    prod.then_inc(out_done, 1)
                    if ahead:
                        flip(n + 1, 1 - k, 0)
                        project(n + 1, 1 - k, "v")
                        flip(n + 1, 1 - k, 1)
                    if c < CPB - 1:
                        pe.wait_ge(qd_ready, b * (CPB - 1) + (c + 1))
                        for half in range(HALVES):
                            if half and ahead:
                                pe.wait_ge(flip_read[0], n * HALVES + (HALVES + 1))
                            for h in range(half * HB, (half + 1) * HB):
                                prod = nc.tensor.matmul(bank("g", half)[:, h % HB], qd[:, h], qkv[:, 2, k, h], start=True, stop=True)
                            prod.then_inc(made["g"], 1)

            batches(pe, batch)


def couple(nc, held, x3, xc, chunk_sums, out):
    SETS = TILES // 4
    SC = CHUNKS // SETS
    with ExitStack() as ctx:
        def sb(name, shape, dt=F32):
            return ctx.enter_context(nc.sbuf_tensor(name, shape, dt))

        def sem(name):
            return ctx.enter_context(nc.semaphore(name))

        def psum(name, shape):
            return ctx.enter_context(nc.psum_tensor(name, shape, F32))

        turn_ps, l1_ps, l2_ps = psum("f_turn_ps", [P, 2, N]), psum("f_l1_ps", [P, 2, N]), psum("f_l2_ps", [P, 2, N])
        l3_ps, l4_ps = psum("f_l3_ps", [P, N]), psum("f_l4_ps", [P, N])
        mean_ps, g1_ps, g2_ps, g3_ps = (l4_ps[:, 64 + BATCH * n:64 + BATCH * (n + 1)] for n in range(4))
        ident, mean, sign, cb, w1, w2, w3, w4 = (held[n] for n in ("ident", "mean", "sign", "cb", "cw1", "cw2", "cw3", "cw4"))
        gw1, gw2, gw3, gb1, gb2 = (held[n] for n in ("gw1", "gw2", "gw3", "gb1", "gb2"))
        half_b = sb("f_half_b", [P, 2])
        ranges = sb("f_ranges", [P, 2])
        ctx_sb, g1s, g2s, tanh_g = sb("f_ctx", [P, BATCH]), sb("f_g1s", [64, BATCH]), sb("f_g2s", [32, BATCH]), sb("f_tanh_g", [P, BATCH])
        by_batch, base = sb("f_by_batch", [P, BATCH]), sb("f_base", [P, SETS, CPT, 4])
        xt, g1, g2, g3 = sb("f_xt", [P, 2, N]), sb("f_g1", [P, 2, N]), sb("f_g2", [P, 2, N]), sb("f_g3", [P, N])
        tanh_t, coupling, signed = sb("f_tanh_t", [P, SETS, CPT, 4]), sb("f_coupling", [P, CPT, 4]), sb("f_signed", [P, 4, CPT, 4])
        twisted = sb("f_twisted", [P, 16, 4, 32])
        stats, mean_var, eps = sb("g_stats", [P, SC, 6]), sb("g_mean_var", [P, SETS, SC, 2]), sb("g_eps", [P, 1])
        deviation, inverse, offset = (sb(f"g_{n}", [P, SETS, SC]) for n in ("deviation", "inverse", "offset"))

        small_ready, eps_set = sem("f_small_ready"), sem("g_eps_set")
        mean_done, ctx_ready, global_done, global_read = sem("f_mean_done"), sem("f_ctx_ready"), sem("f_global_done"), sem("f_global_read")
        chain, base_ready = sem("f_chain"), sem("f_base_ready")
        turned, turn_read = sem("f_turned"), sem("f_turn_read")
        l1_done, l2_done, l3_done, l4_done = (sem(f"f_l{n}_done") for n in range(1, 5))
        g1_ready, g2_ready, g3_ready, tanh_ready = (sem(f"f_{n}_ready") for n in ("g1", "g2", "g3", "tanh"))
        signed_ready, twist_ready, updated = sem("f_signed_ready"), sem("f_twist_ready"), sem("f_updated")
        sum_ready, stats_ready, deviation_ready = sem("g_sum_ready"), sem("g_stats_ready"), sem("g_deviation_ready")
        norm_chain, stored = sem("g_norm_chain"), sem("g_stored")
        inverse_ready, offset_ready = sem("g_inverse_ready"), sem("g_offset_ready")
        normed = {"act": sem("g_normed_act"), "dve": sem("g_normed_dve")}
        BY_DVE = (TILES - 4, TILES - 1)
        block = ctx.enter_context(nc.Block())

        def cycles(engine, one):
            with engine.Fori(0, CYCLES - 1) as cycle:
                for s in range(SETS):
                    one(cycle, s, (cycle, s + 1) if s < SETS - 1 else (cycle + 1, 0))
            for s in range(SETS):
                one(CYCLES - 1, s, (CYCLES - 1, s + 1) if s < SETS - 1 else None)

        @block.sync
        def _(sp):
            done = {"act": 0, "dve": 0}
            for t in range(TILES):
                who = "dve" if t in range(*BY_DVE) else "act"
                done[who] += 1
                sp.wait_ge(normed[who], done[who])
                sp.dma_start(out[t * N:(t + 1) * N].rearrange("(c p) d -> p c d", p=P), xc[:, t * CPT:(t + 1) * CPT]).then_inc(stored, 16)
            sp.wait_ge(stored, TILES * 16)

        def groups(t):
            return t.rearrange("p c (g w) -> p c g w", g=4)

        @block.gpsimd
        def _(pool):
            for primed in (turn_read, g1_ready, g2_ready, g3_ready, tanh_ready, l1_done):
                pool.sem_inc(primed, START)
            pool.sem_inc(updated, SETS)
            nc.gpsimd.memset(eps[:], EPS).then_inc(eps_set, 1)
            with pool.Fori(0, CYCLES) as cycle:
                for s in range(SETS):
                    pool.wait_ge(signed_ready, cycle * SETS + s + 1)
                    old = groups(xc[:, s * SC:(s + 1) * SC])
                    nc.gpsimd.tensor_tensor(twisted[:, :, 2:4], old[:, :, 0:2],
                                            signed[:].rearrange("p q c g -> p (q c) g")[:, :, 2:4].unsqueeze(3).broadcast_to([P, 16, 2, 32]),
                                            ALU.mult).then_inc(twist_ready, 1)

        @block.scalar
        def _(act):
            def gelu1(cycle, s, q):
                n = s * 4 + q
                act.wait_ge(l1_done, START + cycle * TILES + n + 1)
                nc.scalar.activation(g1[:, q % 2], l1_ps[:, q % 2], ACT.Gelu, bias=cb[:, 0:1]).then_inc(g1_ready, 1)

            def gelu2(cycle, s, pair):
                act.wait_ge(l2_done, cycle * TILES + s * 4 + pair * 2 + 2)
                nc.scalar.activation(g2[:, pair], l2_ps[:, pair], ACT.Gelu, bias=cb[:, 1:2]).then_inc(g2_ready, 1)

            def read_turn(cycle, s, q):
                n = s * 4 + q
                act.wait_ge(turned, cycle * TILES + n + 1)
                act.wait_ge(l1_done, START + cycle * TILES + max(n - 1, 0))
                nc.scalar.activation(xt[:, q % 2], turn_ps[:, q % 2], ACT.Copy).then_inc(turn_read, 1)

            def one(cycle, s, following):
                read_turn(cycle, s, 3)
                gelu1(cycle, s, 2)
                gelu2(cycle, s, 0)
                gelu1(cycle, s, 3)
                gelu2(cycle, s, 1)
                if following:
                    read_turn(*following, 0)
                    read_turn(*following, 1)
                act.wait_ge(l3_done, cycle * (SETS * 2) + s * 2 + 2)
                nc.scalar.activation(g3[:], l3_ps[:], ACT.Gelu, bias=cb[:, 2:3]).then_inc(g3_ready, 1)
                if following:
                    gelu1(*following, 0)
                    read_turn(*following, 2)
                act.wait_ge(l4_done, cycle * SETS + s + 1)
                nc.scalar.activation(tanh_t[:, s].rearrange("p c q -> p (c q)"), l4_ps[:, 0:16], ACT.Tanh, scale=0.5,
                                     bias=half_b[:, 0:1]).then_inc(tanh_ready, 1)
                if following:
                    gelu1(*following, 1)

            act.wait_ge(small_ready, 1)
            read_turn(0, 0, 0)
            act.wait_ge(global_done, 1)
            nc.scalar.activation(g1s[:], g1_ps[0:64], ACT.Gelu, bias=gb1[:, 0:1]).then_inc(global_read, 1)
            read_turn(0, 0, 1)
            act.wait_ge(global_done, 2)
            nc.scalar.activation(g2s[:], g2_ps[0:32], ACT.Gelu, bias=gb2[:, 0:1]).then_inc(global_read, 1)
            gelu1(0, 0, 0)
            act.wait_ge(global_done, 3)
            nc.scalar.activation(tanh_g[:], g3_ps, ACT.Tanh, scale=0.5, bias=half_b[:, 1:2]).then_inc(global_read, 1)
            read_turn(0, 0, 2)
            gelu1(0, 0, 1)
            cycles(act, one)
            act.wait_ge(eps_set, 1)
            for s in range(SETS):
                act.wait_ge(stats_ready, s + 1)
                nc.scalar.activation(deviation[:, s], mean_var[:, s, :, 1], ACT.Sqrt, bias=eps[:, 0:1]).then_inc(deviation_ready, 1)
                act.wait_ge(offset_ready, s + 1)
                for t in range(s * 4, s * 4 + 4):
                    if t in range(*BY_DVE):
                        continue
                    for c in range(t * CPT % SC, t * CPT % SC + CPT):
                        last = nc.scalar.activation(xc[:, s * SC + c], x3[:, s * SC + c], ACT.Identity, scale=inverse[:, s, c:c + 1],
                                                    bias=offset[:, s, c:c + 1])
                    last.then_inc(normed["act"], 1)

        @block.tensor
        def _(pe):
            def turn(cycle, s, q):
                n = s * 4 + q
                if q == 0:
                    pe.wait_ge(updated, cycle * SETS + s + 1)
                pe.wait_ge(turn_read, START + cycle * TILES + max(n - 1, 0))
                for c in range(CPT):
                    last = nc.tensor.transpose(turn_ps[:, q % 2, c * P:(c + 1) * P], xc[:, n * CPT + c], ident[:])
                last.then_inc(turned, 1)

            def layer1(cycle, s, q):
                n = s * 4 + q
                pe.wait_ge(turn_read, START + cycle * TILES + n + 1)
                pe.wait_ge(g1_ready, START + cycle * TILES + max(n - 1, 0))
                nc.tensor.matmul(l1_ps[:, q % 2], w1[:], xt[:, q % 2], start=True, stop=True).then_inc(l1_done, 1)

            def layer2(cycle, s, q):
                n = s * 4 + q
                pe.wait_ge(g1_ready, START + cycle * TILES + n + 1)
                pe.wait_ge(g2_ready, START + cycle * (SETS * 2) + s * 2)
                half = slice(64 * (q % 2), 64 * (q % 2) + 64)
                nc.tensor.matmul(l2_ps[half, q // 2], w2[:], g1[:, q % 2], start=True, stop=True).then_inc(l2_done, 1)

            def layer3(cycle, s, pair):
                pe.wait_ge(g2_ready, START + cycle * (SETS * 2) + s * 2 + pair + 1)
                pe.wait_ge(g3_ready, START + cycle * SETS + s)
                nc.tensor.matmul(l3_ps[64 * pair:64 * pair + 64], w3[:], g2[:, pair], start=True, stop=True).then_inc(l3_done, 1)

            def one(cycle, s, following):
                turn(cycle, s, 3)
                layer2(cycle, s, 0)
                layer1(cycle, s, 2)
                layer2(cycle, s, 1)
                layer1(cycle, s, 3)
                layer3(cycle, s, 0)
                layer2(cycle, s, 2)
                layer2(cycle, s, 3)
                if following:
                    turn(*following, 0)
                    turn(*following, 1)
                layer3(cycle, s, 1)
                if following:
                    layer1(*following, 0)
                    turn(*following, 2)
                pe.wait_ge(g3_ready, START + cycle * SETS + s + 1)
                pe.wait_ge(tanh_ready, START + cycle * SETS + s)
                for c in range(CPT):
                    last = nc.tensor.matmul(l4_ps[:, c * 4:c * 4 + 4], g3[:, c * P:(c + 1) * P], w4[:], start=True, stop=True)
                last.then_inc(l4_done, 1)
                if following:
                    layer1(*following, 1)

            for b in range(BATCH):
                last = nc.tensor.matmul(mean_ps[:, b:b + 1], chunk_sums[:, b], mean[:], start=True, stop=True)
            last.then_inc(mean_done, 1)
            turn(0, 0, 0)
            turn(0, 0, 1)
            pe.wait_ge(ctx_ready, 1)
            nc.tensor.matmul(g1_ps[0:64], gw1[:], ctx_sb[:], start=True, stop=True).then_inc(global_done, 1)
            layer1(0, 0, 0)
            pe.wait_ge(global_read, 1)
            nc.tensor.matmul(g2_ps[0:32], gw2[:], g1s[:], start=True, stop=True).then_inc(global_done, 1)
            turn(0, 0, 2)
            pe.wait_ge(global_read, 2)
            nc.tensor.matmul(g3_ps, gw3[:], g2s[:], start=True, stop=True).then_inc(global_done, 1)
            layer1(0, 0, 1)
            cycles(pe, one)

        @block.vector
        def _(dve):
            nc.vector.tensor_scalar(half_b[:], cb[:, 3:5], 0.5, None, ALU.mult)
            nc.vector.tensor_scalar(ranges[:, 0:1], cb[:, 5:6], 0.3, None, ALU.mult)
            nc.vector.tensor_scalar(ranges[:, 1:2], cb[:, 5:6], 0.7, None, ALU.mult).then_inc(small_ready, 1)
            dve.wait_ge(mean_done, 1)
            nc.vector.tensor_copy(ctx_sb[:], mean_ps).then_inc(ctx_ready, 1)
            dve.wait_ge(global_read, 3)
            dve.wait_ge(small_ready, 1)
            nc.vector.tensor_scalar(by_batch[:], tanh_g[:], ranges[:, 1:2], BASE_COUPLING, ALU.mult, ALU.add).then_inc(base_ready, 1)
            dve.wait_ge(base_ready, 1)
            for s in range(SETS):
                last = nc.vector.tensor_copy(base[:, s].rearrange("p c (b q) -> p c b q", b=2),
                                             by_batch[:, 2 * s:2 * s + 2].unsqueeze(1).unsqueeze(3).broadcast_to([P, CPT, 2, 2]))
            last.then_inc(base_ready, 1)
            dve.wait_ge(base_ready, 2)

            def scales(s):
                dve.wait_ge(deviation_ready, s + 1)
                nc.vector.reciprocal(inverse[:, s], deviation[:, s]).then_inc(inverse_ready, 1)
                dve.wait_ge(inverse_ready, s + 1)
                nc.vector.scalar_tensor_tensor(out=offset[:, s], in0=mean_var[:, s, :, 0], scalar=-1.0, in1=inverse[:, s],
                                               op0=ALU.mult, op1=ALU.mult).then_inc(offset_ready, 1)

            CHAIN = 2

            def one(cycle, s, following):
                chained = Count(cycle * (SETS * CHAIN) + s * CHAIN)
                dve.wait_ge(tanh_ready, START + cycle * SETS + s + 1)
                nc.vector.scalar_tensor_tensor(out=coupling[:], in0=tanh_t[:, s], scalar=ranges[:, 0:1], in1=base[:, s],
                                               op0=ALU.mult, op1=ALU.add).then_inc(chain, 1)
                dve.wait_ge(chain, chained.next())
                nc.vector.tensor_tensor(signed[:], coupling[:].rearrange("p c q -> p q c").unsqueeze(3).broadcast_to([P, 4, CPT, 4]),
                                        sign[:].unsqueeze(1).unsqueeze(1).broadcast_to([P, 4, CPT, 4]), ALU.mult).then_inc(signed_ready, 1)
                dve.wait_ge(signed_ready, cycle * SETS + s + 1)
                at = slice(s * SC, (s + 1) * SC)
                nc.vector.tensor_tensor(twisted[:, :, 0:2], groups(xc[:, at])[:, :, 2:4],
                                        signed[:].rearrange("p q c g -> p (q c) g")[:, :, 0:2].unsqueeze(3).broadcast_to([P, 16, 2, 32]),
                                        ALU.mult).then_inc(chain, 1)
                dve.wait_ge(chain, chained.next())
                dve.wait_ge(twist_ready, cycle * SETS + s + 1)
                nc.vector.tensor_tensor(xc[:, at], xc[:, at], twisted[:].rearrange("p c g w -> p c (g w)"), ALU.add).then_inc(updated, 1)
                if isinstance(cycle, int):
                    if s > 0:
                        scales(s - 1)
                    dve.wait_ge(updated, CYCLES * SETS + s + 1)
                    nc.vector.tensor_tensor(x3[:, at], x3[:, at], xc[:, at], ALU.add).then_inc(sum_ready, 1)
                    dve.wait_ge(sum_ready, s + 1)
                    for c in range(SC):
                        last = nc.vector.bn_stats(stats[:, c], x3[:, s * SC + c])
                    last.then_inc(norm_chain, 1)
                    dve.wait_ge(norm_chain, s + 1)
                    for c in range(SC):
                        last = nc.vector.bn_aggr(mean_var[:, s, c], stats[:, c])
                    last.then_inc(stats_ready, 1)

            cycles(dve, one)
            scales(SETS - 1)
            for t in range(*BY_DVE):
                for c in range(t * CPT, t * CPT + CPT):
                    last = nc.vector.tensor_scalar(xc[:, c], x3[:, c], mean_var[:, SETS - 1, c % SC, 0:1],
                                                   inverse[:, SETS - 1, c % SC:c % SC + 1], ALU.subtract, ALU.mult)
                last.then_inc(normed["dve"], 1)


def scratch(nc):
    def dram(name, shape, dt=F32):
        return nc.dram_tensor(f"scratch_{name}", shape, dt, kind="Internal").ap()

    return {
        "parts": [dram(f"parts{z}", (PARTS * HD * HEADS, TOKENS), BF16) for z in range(2)],
        "vals": dram("vals", (TOKENS, HEADS * VW)),
        "outs": dram("outs", (HEADS, VW, TOKENS)),
        "rz": dram("rz", (HEADS, TOKENS)),
    }


def build(nc, io, out):
    scr = scratch(nc)
    with ExitStack() as ctx:
        def sb(name, shape, dt=F32):
            return ctx.enter_context(nc.sbuf_tensor(name, shape, dt))

        names = ("ident", "woT", "w1", "b1", "w2", "bo", "b2", "cos1", "sin1", "mask", "decay", "keep", "gn_w", "gn_b",
                 "cw1", "cw2", "cw3", "cw4", "cb", "gw1", "gw2", "gw3", "gb1", "gb2", "mean", "sign")
        held = {name: sb(f"held_{name}", io[name].shape) for name in names}
        held["w_high"], held["w_low"] = (sb(f"held_{n}", io["wqkv"].shape, F32R) for n in ("w_high", "w_low"))
        held["o"], held["rz"], held["residual"] = sb("held_o", [P, 2, N]), sb("held_rz", [P, 2, N]), sb("held_residual", [P, 2, CPT, P])
        with ExitStack() as operands:
            def operand(name, shape, dt=F32):
                return operands.enter_context(nc.sbuf_tensor(name, shape, dt))

            held["q"] = operand("held_q", [P, GROUPS, GH, SEQ], BF16)
            held["k"] = operand("held_k", [P, GROUPS, GH, SEQ], BF16)
            held["v"] = operand("held_v", [P, GROUPS, CPB, GH * VW])
            project_and_split(nc, io, scr, held)
            attend(nc, io, scr, held)
        held["x2b"], held["x2T"] = sb("held_x2b", [P, CHUNKS, DIM]), sb("held_x2T", [P, TOKENS])
        project_out_and_ffn(nc, io, scr, held)
        r, x3 = (sb(name, [P, CHUNKS, DIM]) for name in ("r", "x3"))
        chunk_sums = sb("chunk_sums", [P, BATCH, DIM])
        retain(nc, held, r, x3, chunk_sums)
        couple(nc, held, x3, r, chunk_sums, out)


def _layout(x):
    import numpy as _np

    f = _np.float32
    a = {k: _np.asarray(v) for k, v in x.items()}
    col = lambda v: _np.ascontiguousarray(v.reshape(-1, 1))
    arrays = {"x": a["L0_attn_x"].reshape(TOKENS, DIM)}
    arrays["xT"] = _np.ascontiguousarray(arrays["x"].T)
    other = _np.arange(DIM).reshape(HEADS, 2, HD // 2)[:, ::-1].reshape(-1)
    wq, wk, wv = a["L0_attn_wq"], a["L0_attn_wk"], a["L0_attn_wv"]
    by_dim = _np.arange(DIM).reshape(HEADS, HD).T.reshape(-1)
    other = other[by_dim]
    arrays["w0"] = _np.stack([wq[by_dim].T, wq[other].T, wk[by_dim].T, wk[other].T, wv.T], 1)
    bq, bk = a["L0_attn_bq"], a["L0_attn_bk"]
    arrays["bias0"] = _np.stack([bq[by_dim], bq[other], bk[by_dim], bk[other]], 1)
    arrays["bv"] = _np.tile(a["L0_attn_bv"], (P, CPT))
    theta = f(10000.0) ** (f(-2.0) * _np.arange(HD // 2, dtype=f) / f(HD))
    angle = _np.repeat(_np.arange(SEQ, dtype=f)[:, None] * theta[None, :], 2, -1).T
    sign = _np.where(_np.arange(HD) < HD // 2, -1, 1)[:, None]
    arrays["cos0"] = _np.repeat(_np.cos(angle), HEADS, 0).astype(f)
    arrays["sin0"] = _np.repeat(_np.sin(angle) * sign, HEADS, 0).astype(f)
    arrays["ident"] = _np.eye(P, dtype=f)
    arrays["woT"] = _np.ascontiguousarray(a["L0_attn_wo"].T)
    arrays["bo"] = _np.tile(a["L0_attn_bo"], (P, CPT))
    arrays["w1"] = a["L0_ffn_W1"]
    arrays["b1"] = _np.ascontiguousarray(a["L0_ffn_b1"].reshape(INTER // P, P).T)
    arrays["w2"] = _np.ascontiguousarray(a["L0_ffn_W2"].reshape(INTER // P, P, DIM).transpose(1, 0, 2))
    arrays["b2"] = _np.tile(a["L0_ffn_b2"], (P, CPT))
    order = _np.concatenate([_np.arange(0, ROPE_DIM, 2), _np.arange(1, ROPE_DIM, 2), _np.arange(ROPE_DIM, DIM)])
    heads = (_np.arange(RHEADS)[:, None] * DIM + order).reshape(-1)
    arrays["wqkv"] = _np.stack([a["L1_attn_W_Q"][:, heads], a["L1_attn_W_K"][:, heads], a["L1_attn_W_V"]], 1)
    inv = f(1.0) / f(10000.0) ** (_np.arange(0, ROPE_DIM, 2, dtype=f) / f(ROPE_DIM))
    angle = _np.arange(SEQ, dtype=f)[:, None] * inv[None, :]
    turn = lambda v: _np.ascontiguousarray(v.reshape(CPB, P, ROPE_DIM)[::-1].transpose(1, 0, 2).astype(f))
    arrays["cos1"] = turn(_np.concatenate([_np.cos(angle)] * 2, -1))
    arrays["sin1"] = turn(_np.concatenate([_np.sin(angle), -_np.sin(angle)], -1))
    n = _np.arange(P)
    arrays["mask"] = _np.where(n[:, None] >= n[None, :], GAMMA ** (n[:, None] - float(P)), 0.0).astype(f)
    arrays["decay"] = _np.stack([GAMMA ** n.astype(_np.float64), GAMMA ** (P - n.astype(_np.float64))], 1).astype(f)
    keep = _np.full((P, CPB), GAMMA ** float(P))
    keep[:, 0] = 0.0
    arrays["keep"] = keep.astype(f)
    arrays["gn_w"] = _np.tile(a["L1_attn_gn_weight"], (P, 1))
    arrays["gn_b"] = _np.tile(a["L1_attn_gn_bias"], (P, 1))
    arrays["cw1"] = a["L1_ffn_cn_w1"]
    arrays["cw2"] = a["L1_ffn_cn_w2"]
    w3, w4 = a["L1_ffn_cn_w3"], a["L1_ffn_cn_w4"]
    blocks = _np.zeros((P, 64), f)
    blocks[:64, :32] = w3
    blocks[64:, 32:] = w3
    arrays["cw3"] = blocks
    blocks = _np.zeros((P, 4), f)
    for q in range(4):
        blocks[32 * q:32 * q + 32, q:q + 1] = w4
    arrays["cw4"] = blocks
    arrays["cb"] = _np.stack([a["L1_ffn_cn_b1"], _np.tile(a["L1_ffn_cn_b2"], 2), _np.tile(a["L1_ffn_cn_b3"], 4),
                              _np.tile(a["L1_ffn_cn_b4"], P), _np.tile(a["L1_ffn_gc_b3"], P),
                              _np.tile(a["L1_ffn_adaptive_range"], P)], 1)
    arrays["gw1"] = a["L1_ffn_gc_w1"]
    arrays["gw2"] = a["L1_ffn_gc_w2"]
    arrays["gw3"] = _np.tile(a["L1_ffn_gc_w3"], (1, P))
    arrays["gb1"] = col(a["L1_ffn_gc_b1"])
    arrays["gb2"] = col(a["L1_ffn_gc_b2"])
    arrays["mean"] = _np.full((P, 1), 1.0 / SEQ, f)
    arrays["sign"] = _np.tile(_np.array([1, -1, -1, 1], f), (P, 1))
    return {k: _np.ascontiguousarray(v) for k, v in arrays.items()}


def kernel(**inputs):
    import concourse.bacc as _bacc
    from concourse import mybir as _mybir
    from concourse.bass_utils import run_bass_kernel_spmd as _run

    nc = _bacc.Bacc("TRN2", target_bir_lowering=False, num_devices=1)
    arrays = {f"in_{k}": v for k, v in _layout(inputs).items()}
    io = {k[3:]: nc.dram_tensor(k, v.shape, _mybir.dt.from_np(v.dtype), kind="ExternalInput").ap()
          for k, v in arrays.items()}
    out = nc.dram_tensor("out", (TOKENS, DIM), F32, kind="ExternalOutput").ap()
    build(nc, io, out)
    r = _run(nc, [arrays], core_ids=[0])
    return r.results[0]["out"].reshape(BATCH, SEQ, DIM)
```
